# Optimizing a Trainium2 kernel written in Bass

```python
import numpy as np
import jax
import jax.numpy as jnp

def _softmax(x, axis=-1):
    return jax.nn.softmax(x, axis=axis)

def _gelu(x):
    return jax.nn.gelu(x, approximate=True)

def _silu(x):
    return jax.nn.silu(x)

def _sigmoid(x):
    return jax.nn.sigmoid(x)

def _layernorm(x, axis=-1, eps=1e-05):
    m = jnp.mean(x, axis=axis, keepdims=True)
    v = jnp.var(x, axis=axis, keepdims=True)
    return (x - m) / jnp.sqrt(v + eps)

def _scatter_add(tgt, idx, src, axis=0):
    return tgt.at[idx].add(src)

def _segment_sum(src, seg, n):
    return jax.ops.segment_sum(src, seg, n)
kernel_name = 'mk_early_fusion_d1_tok_img2048_r4_cc095c'

def setup_inputs(seed: int=0):
    np.random.seed(seed)
    _w = jnp.asarray

    def _rec_inputs():
        import jax
        import jax.numpy as jnp
        _rk = jax.random.key(seed)
        x = -0.00340659 + 1.00146 * jax.random.normal(jax.random.fold_in(_rk, 1), (16, 256, 64, 2), jnp.float32)
        txt = 0.000411298 + 0.588087 * jax.random.normal(jax.random.fold_in(_rk, 2), (16, 77, 512), jnp.float32)
        return (x, txt)
    x, txt = _rec_inputs()

    def _L0_tok_setup():
        import jax, jax.numpy as jnp
        import numpy as np
        CH, H, N, N_SSM, SEQ_L = (1, 256, 64, 256, 512)

        def _kernel(C_ri, log_dt, B_ri, inv_A_real, A_imag, L):
            C = C_ri[..., 0] + 1j * C_ri[..., 1]
            B = B_ri[..., 0] + 1j * B_ri[..., 1]
            A = -jnp.exp(inv_A_real) + 1j * A_imag
            rep = log_dt.shape[0] // inv_A_real.shape[0]
            B = jnp.tile(B, (rep, 1))
            A = jnp.tile(A, (rep, 1))
            dt = jnp.exp(log_dt)
            dtA = A * dt[:, None]
            Ct = B[None] * C / (1.0 - dtA / 2) * dt[:, None]
            dA = (1.0 + dtA / 2) / (1.0 - dtA / 2)
            dA_log = jnp.log(dA)
            l = jnp.arange(L, dtype=jnp.float32)
            V = jnp.exp(dA_log[:, :, None] * l)
            K = 2.0 * jnp.einsum('chn,hnl->chl', Ct, V).real
            return K
        key = jax.random.key(seed)
        ks = jax.random.split(key, 5)
        return {'C_ri': jax.random.normal(ks[0], (CH, H, N, 2), dtype=jnp.float32), 'log_dt': jax.random.normal(ks[1], (H,), dtype=jnp.float32), 'B_ri': jax.random.normal(ks[2], (N_SSM, N, 2), dtype=jnp.float32), 'inv_A_real': jax.random.normal(ks[3], (N_SSM, N), dtype=jnp.float32), 'A_imag': jax.random.normal(ks[4], (N_SSM, N), dtype=jnp.float32), 'L': SEQ_L}
    _L0_tok_all = _L0_tok_setup()
    _L0_tok_in = {k: v for k, v in _L0_tok_all.items() if k in ('log_dt', 'B_ri', 'inv_A_real', 'A_imag')}
    del _L0_tok_all

    def _L0_attn_setup():
        import jax, jax.numpy as jnp
        import numpy as np
        from jax import lax
        BATCH = 2
        SEQ = 512
        HID = 512
        EXPAND = 2
        INTER = EXPAND * HID
        HEADS = 64
        PDIM = INTER // HEADS
        NSTATE = 128
        G = 1
        HPG = HEADS // G
        KCONV = 4
        GTS = G * NSTATE
        CONV_DIM = INTER + 2 * GTS
        PROJ_DIM = 2 * INTER + 2 * GTS + HEADS
        EPS = 1e-05
        MUP = (0.25, 0.5, 0.5, 0.5, 1.0)

        def _mup_vector():
            return jnp.concatenate([jnp.full((INTER,), MUP[0], jnp.float32), jnp.full((INTER,), MUP[1], jnp.float32), jnp.full((GTS,), MUP[2], jnp.float32), jnp.full((GTS,), MUP[3], jnp.float32), jnp.full((HEADS,), MUP[4], jnp.float32)])

        def _forward(hidden_states, in_proj_w, conv_w, conv_b, A_log, D, dt_bias, norm_w, out_proj_w):
            b, l, _ = hidden_states.shape
            proj = hidden_states @ in_proj_w * _mup_vector()
            z = proj[..., :INTER]
            xBC = proj[..., INTER:INTER + CONV_DIM]
            dt = proj[..., INTER + CONV_DIM:]
            xBC_cl = jnp.swapaxes(xBC, 1, 2)
            conv = lax.conv_general_dilated(xBC_cl, conv_w[:, None, :], window_strides=(1,), padding=((KCONV - 1, 0),), feature_group_count=CONV_DIM)
            xBC = jax.nn.silu(jnp.swapaxes(conv + conv_b[None, :, None], 1, 2))
            x = xBC[..., :INTER].reshape(b, l, G, HPG, PDIM)
            Bm = xBC[..., INTER:INTER + GTS].reshape(b, l, G, NSTATE)
            Cm = xBC[..., INTER + GTS:].reshape(b, l, G, NSTATE)
            dt = jax.nn.softplus(dt + dt_bias)
            A = -jnp.exp(A_log)
            dA = jnp.exp(dt * A).reshape(b, l, G, HPG)
            dtx = dt.reshape(b, l, G, HPG)[..., None] * x

            def step(state, inp):
                dA_t, dtx_t, B_t, C_t = inp
                state = state * dA_t[..., None, None] + jnp.einsum('bgcp,bgn->bgcpn', dtx_t, B_t)
                y_t = jnp.einsum('bgn,bgcpn->bgcp', C_t, state)
                return (state, y_t)
            inputs = (jnp.moveaxis(dA, 1, 0), jnp.moveaxis(dtx, 1, 0), jnp.moveaxis(Bm, 1, 0), jnp.moveaxis(Cm, 1, 0))
            state0 = jnp.zeros((b, G, HPG, PDIM, NSTATE), hidden_states.dtype)
            _, ys = lax.scan(step, state0, inputs)
            y = jnp.moveaxis(ys, 0, 1) + D.reshape(1, 1, G, HPG, 1) * x
            y = y.reshape(b, l, INTER)
            yg = y.reshape(b, l, G, INTER // G)
            var = jnp.mean(jnp.square(yg), axis=-1, keepdims=True)
            yn = (yg * lax.rsqrt(var + EPS)).reshape(b, l, INTER) * norm_w
            out = yn * jax.nn.silu(z)
            return out @ out_proj_w
        key = jax.random.key(seed)
        ks = jax.random.split(key, 8)
        hidden_states = jax.random.normal(ks[0], (BATCH, SEQ, HID), jnp.float32)
        in_proj_w = jax.random.normal(ks[1], (HID, PROJ_DIM), jnp.float32) * 0.02
        conv_w = jax.random.normal(ks[2], (CONV_DIM, KCONV), jnp.float32) * 0.2
        conv_b = jnp.zeros((CONV_DIM,), jnp.float32)
        A_log = jnp.log(jnp.arange(1, HEADS + 1, dtype=jnp.float32))
        D = jnp.ones((HEADS,), jnp.float32)
        dt_bias = jax.random.uniform(ks[3], (HEADS,), jnp.float32)
        norm_w = jnp.ones((INTER,), jnp.float32)
        out_proj_w = jax.random.normal(ks[4], (INTER, HID), jnp.float32) * 0.02
        return dict(hidden_states=hidden_states, in_proj_w=in_proj_w, conv_w=conv_w, conv_b=conv_b, A_log=A_log, D=D, dt_bias=dt_bias, norm_w=norm_w, out_proj_w=out_proj_w)
    _L0_attn_all = _L0_attn_setup()
    _L0_attn_in = {k: v for k, v in _L0_attn_all.items() if k in ('in_proj_w', 'conv_w', 'conv_b', 'A_log', 'D', 'dt_bias', 'norm_w', 'out_proj_w')}
    del _L0_attn_all

    def _L0_ffn_setup():
        import jax, jax.numpy as jnp
        import numpy as np
        B, S, H = (2, 256, 512)
        I = 256
        E = 32
        Z = 32
        K = 8
        SCALE = 1.5
        CAP = 256
        EPS = 1e-20

        def _moe_forward(x, w_cls, bias, w_gate_up, w_down):
            T = x.shape[0] * x.shape[1]
            xf = x.reshape(T, H)
            logits = xf.astype(jnp.float32) @ w_cls.T
            scores = jax.nn.softmax(logits, axis=-1)
            _, topk_idx = jax.lax.top_k(scores + bias[None, :], K)
            w = jnp.take_along_axis(scores, topk_idx, axis=-1)
            w = w / (w.sum(-1, keepdims=True) + EPS) * SCALE
            routed = topk_idx < E
            w_r = jnp.where(routed, w, 0.0)
            w_z = jnp.where(routed, 0.0, w)
            N = T * K
            flat_ids = jnp.where(routed, topk_idx, E).reshape(-1)
            x_exp = jnp.repeat(xf, K, axis=0)
            order = jnp.argsort(flat_ids)
            ids_s = flat_ids[order]
            counts = jax.ops.segment_sum(jnp.ones(N, jnp.int32), flat_ids, num_segments=E + 1)
            starts = jnp.cumsum(counts) - counts
            pos = jnp.arange(N) - starts[ids_s]
            buf = jnp.zeros((E, CAP, H), xf.dtype).at[ids_s, pos].set(x_exp[order], mode='drop')
            gu = jnp.einsum('ech,ehf->ecf', buf, w_gate_up)
            g, u = jnp.split(gu, 2, axis=-1)
            act = jax.nn.silu(g) * u
            y = jnp.einsum('eci,eih->ech', act, w_down)
            valid = (ids_s < E) & (pos < CAP)
            y_tok = jnp.where(valid[:, None], y[jnp.clip(ids_s, 0, E - 1), jnp.clip(pos, 0, CAP - 1)], 0.0)
            y_exp = jnp.zeros((N, H), xf.dtype).at[order].set(y_tok).reshape(T, K, H)
            routed_out = jnp.einsum('tk,tkh->th', w_r, y_exp)
            out = routed_out * (1.0 + w_z.sum(-1, keepdims=True))
            return out.reshape(x.shape)
        key = jax.random.key(seed)
        ks = jax.random.split(key, 5)
        x = jax.random.normal(ks[0], (B, S, H), jnp.float32)
        w_cls = jax.random.normal(ks[1], (E + Z, H), jnp.float32) / np.float32(np.sqrt(H))
        bias = jax.random.normal(ks[2], (E + Z,), jnp.float32) * 0.02
        w_gate_up = jax.random.normal(ks[3], (E, H, 2 * I), jnp.float32) * 0.02
        w_down = jax.random.normal(ks[4], (E, I, H), jnp.float32) * 0.02
        return {'x': x, 'w_cls': w_cls, 'bias': bias, 'w_gate_up': w_gate_up, 'w_down': w_down}
    _L0_ffn_all = _L0_ffn_setup()
    _L0_ffn_in = {k: v for k, v in _L0_ffn_all.items() if k in ('w_cls', 'bias', 'w_gate_up', 'w_down')}
    del _L0_ffn_all
    return {'x': x, 'txt': txt, 'L0_tok_log_dt': _L0_tok_in['log_dt'], 'L0_tok_B_ri': _L0_tok_in['B_ri'], 'L0_tok_inv_A_real': _L0_tok_in['inv_A_real'], 'L0_tok_A_imag': _L0_tok_in['A_imag'], 'L0_attn_in_proj_w': _L0_attn_in['in_proj_w'], 'L0_attn_conv_w': _L0_attn_in['conv_w'], 'L0_attn_conv_b': _L0_attn_in['conv_b'], 'L0_attn_A_log': _L0_attn_in['A_log'], 'L0_attn_D': _L0_attn_in['D'], 'L0_attn_dt_bias': _L0_attn_in['dt_bias'], 'L0_attn_norm_w': _L0_attn_in['norm_w'], 'L0_attn_out_proj_w': _L0_attn_in['out_proj_w'], 'L0_ffn_w_cls': _L0_ffn_in['w_cls'], 'L0_ffn_bias': _L0_ffn_in['bias'], 'L0_ffn_w_gate_up': _L0_ffn_in['w_gate_up'], 'L0_ffn_w_down': _L0_ffn_in['w_down']}

def reference(x, txt, L0_tok_log_dt, L0_tok_B_ri, L0_tok_inv_A_real, L0_tok_A_imag, L0_attn_in_proj_w, L0_attn_conv_w, L0_attn_conv_b, L0_attn_A_log, L0_attn_D, L0_attn_dt_bias, L0_attn_norm_w, L0_attn_out_proj_w, L0_ffn_w_cls, L0_ffn_bias, L0_ffn_w_gate_up, L0_ffn_w_down):
    import jax
    import jax.numpy as jnp

    def _L0_tok_ref(C_ri, log_dt, B_ri, inv_A_real, A_imag, L):
        import jax, jax.numpy as jnp
        import numpy as np
        CH, H, N, N_SSM, SEQ_L = (1, 256, 64, 256, 512)

        def _kernel(C_ri, log_dt, B_ri, inv_A_real, A_imag, L):
            C = C_ri[..., 0] + 1j * C_ri[..., 1]
            B = B_ri[..., 0] + 1j * B_ri[..., 1]
            A = -jnp.exp(inv_A_real) + 1j * A_imag
            rep = log_dt.shape[0] // inv_A_real.shape[0]
            B = jnp.tile(B, (rep, 1))
            A = jnp.tile(A, (rep, 1))
            dt = jnp.exp(log_dt)
            dtA = A * dt[:, None]
            Ct = B[None] * C / (1.0 - dtA / 2) * dt[:, None]
            dA = (1.0 + dtA / 2) / (1.0 - dtA / 2)
            dA_log = jnp.log(dA)
            l = jnp.arange(L, dtype=jnp.float32)
            V = jnp.exp(dA_log[:, :, None] * l)
            K = 2.0 * jnp.einsum('chn,hnl->chl', Ct, V).real
            return K
        return _kernel(C_ri, log_dt, B_ri, inv_A_real, A_imag, L)

    def _L0_attn_ref(hidden_states, in_proj_w, conv_w, conv_b, A_log, D, dt_bias, norm_w, out_proj_w):
        import jax, jax.numpy as jnp
        import numpy as np
        from jax import lax
        BATCH = 2
        SEQ = 512
        HID = 512
        EXPAND = 2
        INTER = EXPAND * HID
        HEADS = 64
        PDIM = INTER // HEADS
        NSTATE = 128
        G = 1
        HPG = HEADS // G
        KCONV = 4
        GTS = G * NSTATE
        CONV_DIM = INTER + 2 * GTS
        PROJ_DIM = 2 * INTER + 2 * GTS + HEADS
        EPS = 1e-05
        MUP = (0.25, 0.5, 0.5, 0.5, 1.0)

        def _mup_vector():
            return jnp.concatenate([jnp.full((INTER,), MUP[0], jnp.float32), jnp.full((INTER,), MUP[1], jnp.float32), jnp.full((GTS,), MUP[2], jnp.float32), jnp.full((GTS,), MUP[3], jnp.float32), jnp.full((HEADS,), MUP[4], jnp.float32)])

        def _forward(hidden_states, in_proj_w, conv_w, conv_b, A_log, D, dt_bias, norm_w, out_proj_w):
            b, l, _ = hidden_states.shape
            proj = hidden_states @ in_proj_w * _mup_vector()
            z = proj[..., :INTER]
            xBC = proj[..., INTER:INTER + CONV_DIM]
            dt = proj[..., INTER + CONV_DIM:]
            xBC_cl = jnp.swapaxes(xBC, 1, 2)
            conv = lax.conv_general_dilated(xBC_cl, conv_w[:, None, :], window_strides=(1,), padding=((KCONV - 1, 0),), feature_group_count=CONV_DIM)
            xBC = jax.nn.silu(jnp.swapaxes(conv + conv_b[None, :, None], 1, 2))
            x = xBC[..., :INTER].reshape(b, l, G, HPG, PDIM)
            Bm = xBC[..., INTER:INTER + GTS].reshape(b, l, G, NSTATE)
            Cm = xBC[..., INTER + GTS:].reshape(b, l, G, NSTATE)
            dt = jax.nn.softplus(dt + dt_bias)
            A = -jnp.exp(A_log)
            dA = jnp.exp(dt * A).reshape(b, l, G, HPG)
            dtx = dt.reshape(b, l, G, HPG)[..., None] * x

            def step(state, inp):
                dA_t, dtx_t, B_t, C_t = inp
                state = state * dA_t[..., None, None] + jnp.einsum('bgcp,bgn->bgcpn', dtx_t, B_t)
                y_t = jnp.einsum('bgn,bgcpn->bgcp', C_t, state)
                return (state, y_t)
            inputs = (jnp.moveaxis(dA, 1, 0), jnp.moveaxis(dtx, 1, 0), jnp.moveaxis(Bm, 1, 0), jnp.moveaxis(Cm, 1, 0))
            state0 = jnp.zeros((b, G, HPG, PDIM, NSTATE), hidden_states.dtype)
            _, ys = lax.scan(step, state0, inputs)
            y = jnp.moveaxis(ys, 0, 1) + D.reshape(1, 1, G, HPG, 1) * x
            y = y.reshape(b, l, INTER)
            yg = y.reshape(b, l, G, INTER // G)
            var = jnp.mean(jnp.square(yg), axis=-1, keepdims=True)
            yn = (yg * lax.rsqrt(var + EPS)).reshape(b, l, INTER) * norm_w
            out = yn * jax.nn.silu(z)
            return out @ out_proj_w
        return _forward(hidden_states, in_proj_w, conv_w, conv_b, A_log, D, dt_bias, norm_w, out_proj_w)

    def _L0_ffn_ref(x, w_cls, bias, w_gate_up, w_down):
        import jax, jax.numpy as jnp
        import numpy as np
        B, S, H = (2, 256, 512)
        I = 256
        E = 32
        Z = 32
        K = 8
        SCALE = 1.5
        CAP = 256
        EPS = 1e-20

        def _moe_forward(x, w_cls, bias, w_gate_up, w_down):
            T = x.shape[0] * x.shape[1]
            xf = x.reshape(T, H)
            logits = xf.astype(jnp.float32) @ w_cls.T
            scores = jax.nn.softmax(logits, axis=-1)
            _, topk_idx = jax.lax.top_k(scores + bias[None, :], K)
            w = jnp.take_along_axis(scores, topk_idx, axis=-1)
            w = w / (w.sum(-1, keepdims=True) + EPS) * SCALE
            routed = topk_idx < E
            w_r = jnp.where(routed, w, 0.0)
            w_z = jnp.where(routed, 0.0, w)
            N = T * K
            flat_ids = jnp.where(routed, topk_idx, E).reshape(-1)
            x_exp = jnp.repeat(xf, K, axis=0)
            order = jnp.argsort(flat_ids)
            ids_s = flat_ids[order]
            counts = jax.ops.segment_sum(jnp.ones(N, jnp.int32), flat_ids, num_segments=E + 1)
            starts = jnp.cumsum(counts) - counts
            pos = jnp.arange(N) - starts[ids_s]
            buf = jnp.zeros((E, CAP, H), xf.dtype).at[ids_s, pos].set(x_exp[order], mode='drop')
            gu = jnp.einsum('ech,ehf->ecf', buf, w_gate_up)
            g, u = jnp.split(gu, 2, axis=-1)
            act = jax.nn.silu(g) * u
            y = jnp.einsum('eci,eih->ech', act, w_down)
            valid = (ids_s < E) & (pos < CAP)
            y_tok = jnp.where(valid[:, None], y[jnp.clip(ids_s, 0, E - 1), jnp.clip(pos, 0, CAP - 1)], 0.0)
            y_exp = jnp.zeros((N, H), xf.dtype).at[order].set(y_tok).reshape(T, K, H)
            routed_out = jnp.einsum('tk,tkh->th', w_r, y_exp)
            out = routed_out * (1.0 + w_z.sum(-1, keepdims=True))
            return out.reshape(x.shape)
        return _moe_forward(x, w_cls, bias, w_gate_up, w_down)
    h = _L0_tok_ref(x, L0_tok_log_dt, L0_tok_B_ri, L0_tok_inv_A_real, L0_tok_A_imag, 512)
    h = jnp.concatenate([h, txt], axis=1)
    h = h + _L0_attn_ref(_layernorm(h, axis=-1), L0_attn_in_proj_w, L0_attn_conv_w, L0_attn_conv_b, L0_attn_A_log, L0_attn_D, L0_attn_dt_bias, L0_attn_norm_w, L0_attn_out_proj_w)
    h = h + _L0_ffn_ref(_layernorm(h, axis=-1), L0_ffn_w_cls, L0_ffn_bias, L0_ffn_w_gate_up, L0_ffn_w_down)
    return h

_drawn_inputs = setup_inputs


def setup_inputs(seed=0):
    import zlib

    import numpy as np

    out = dict(_drawn_inputs(seed))
    spreads = {'L0_attn_conv_b': (0.0, 0.28), 'L0_attn_D': (1.0, 0.6), 'L0_attn_norm_w': (1.0, 0.6)}
    factors = {'L0_attn_A_log': 8.0,
     'L0_attn_dt_bias': 8.0,
     'L0_ffn_w_cls': 3.95,
     'L0_ffn_bias': 6.01,
     'L0_ffn_w_gate_up': 3.928,
     'L0_ffn_w_down': 3.917}
    for name, (base, spread) in spreads.items():
        noise = np.random.default_rng([zlib.crc32(name.encode()), seed]).standard_normal(out[name].shape)
        drawn = base * np.exp(spread * noise) if base else spread * noise
        out[name] = jnp.asarray(drawn.astype(out[name].dtype))
    for name, factor in factors.items():
        out[name] = (out[name] * factor).astype(out[name].dtype)
    return out
```

```python
from contextlib import ExitStack

import concourse.bass as bass
from concourse import mybir

ALU = mybir.AluOpType
ACT = mybir.ActivationFunctionType
AX = mybir.AxisListType.X
F32 = mybir.dt.float32
BF16 = mybir.dt.bfloat16
U32 = mybir.dt.uint32

BATCH, SSM_H, SSM_N = 16, 256, 64
TXT = 77
SEQ = SSM_H + TXT
DM = 512
P = 128
KD = DM // P
PAIRS = SSM_H // 2
BLK = DM // P
LOW = P
LOG = LOW.bit_length() - 1
GRP = 16
HEADS, HD, NST = 64, 16, 128
INTER = HEADS * HD
CONV_TILES = (INTER + 2 * NST) // P
B_TILE, C_TILE = INTER // P, INTER // P + 1
XBC0 = INTER
DT0 = 2 * INTER + 2 * NST
PROJ = DT0 + HEADS
CH = 3
Q = SEQ // CH
HH = HEADS // 2
HG = 4
GROUPS = HEADS // HG
E, NE, TOPK, CAP, FI = 32, 64, 8, 256, 256
TOK = BATCH * SEQ
SLOTS = E * CAP
EPS = 1e-5
FLOOR = -120.0
TINY = 1e-30

def _narrow():
    uses = [("xnT", j) for j in range(CH)] + [("dt", 0)]
    uses += [("conv", m) for m in conv_order()]
    uses += [("cum", j) for j in range(CH)]
    for j in range(CH):
        uses.append(("cb", j))
        if j:
            uses += tail_uses(j - 1)
    uses += tail_uses(CH - 1)
    if len(uses) % 2:
        uses.append(("pad", 0))
    return uses


def conv_order():
    return [B_TILE, C_TILE] + list(range(B_TILE))


def tail_uses(j):
    return [("out", j), ("x2T", j), ("logits", j), ("rank", j)]


def _wide():
    uses = []
    for j in range(CH):
        uses += [("xrow", j), ("z", j)]
        if j:
            uses.append(("inter", j))
        if j < CH - 1:
            uses.append(("state", j))
        if j:
            uses.append(("gT", j - 1))
    return uses + [("gT", CH - 1)]


NARROW = _narrow()
WIDE = _wide()


class Steps:

    def __init__(self, eng, sem):
        self.eng, self.sem, self.base, self.n = eng, sem, 0, 0

    def done(self, ins):
        ins.then_inc(self.sem, 1)
        self.n += 1
        return self.n

    def wait(self, n=None):
        self.eng.wait_ge(self.sem, self.base + (self.n if n is None else n))

    def link(self, ins):
        self.done(ins)
        self.wait()

    def loop(self, i, per):
        self.before, self.per = self.n, per
        self.base, self.n = self.n + i * per, 0

    def end(self, turns):
        assert self.n == self.per, ("steps of a turn:", self.n)
        self.base, self.n = 0, self.before + turns * self.per


def bc(ap, shape):
    return ap.broadcast_to(shape)


def make_constants(nc, k, ins, dram):
    with ExitStack() as ctx:
        made = ctx.enter_context(nc.semaphore("made"))
        loaded = ctx.enter_context(nc.semaphore("loaded"))
        cls_loaded = ctx.enter_context(nc.semaphore("cls_loaded"))
        turned = ctx.enter_context(nc.semaphore("turned"))
        dve_step = ctx.enter_context(nc.semaphore("dve_step"))
        act_step = ctx.enter_context(nc.semaphore("act_step"))
        stored = ctx.enter_context(nc.semaphore("stored"))
        wcls = ctx.enter_context(nc.sbuf_tensor("wcls", [NE, DM], F32))
        zero = ctx.enter_context(nc.sbuf_tensor("zero", [P, 2 * DM], F32))
        empty = ctx.enter_context(nc.sbuf_tensor("empty", [P, 2, 2], F32))
        clsT = ctx.enter_context(nc.psum_tensor("clsT", [P, KD, NE], F32))
        block = ctx.enter_context(nc.Block())

        @block.sync
        def _(sp):
            sp.dma_start(wcls[:, :], ins["L0_ffn_w_cls"]).then_inc(cls_loaded, 16)
            with nc.allow_non_contiguous_dma(reason="small per-channel vectors"):
                sp.dma_start(k["conv_w"][:, :, :],
                             ins["L0_attn_conv_w"].rearrange("(m p) t -> p m t", p=P)).then_inc(loaded, 16)
                sp.dma_start(k["conv_b"][:, :],
                             ins["L0_attn_conv_b"].rearrange("(m p) -> p m", p=P)).then_inc(loaded, 16)
            for name, key, width in (("L0_attn_A_log", "neg_a", HEADS), ("L0_attn_D", "skip_d", HEADS),
                                     ("L0_attn_dt_bias", "dt_bias", HEADS), ("L0_ffn_bias", "top_bias", NE)):
                sp.dma_start(k[key][:, :], ins[name].unsqueeze(0).broadcast_to([Q, width])).then_inc(loaded, 16)
            sp.dma_start(dram["h"][:, SSM_H:SEQ, :], ins["txt"]).then_inc(stored, 16)
            sp.wait_ge(made, 1)
            sp.dma_start(dram["slots"].rearrange("(e p t) c -> p e (t c)", p=P, t=2),
                         empty[:, :, :].rearrange("p t c -> p (t c)").unsqueeze(1).broadcast_to([P, E, 4])
                         ).then_inc(stored, 16)
            for name in ("x2", "acc"):
                sp.dma_start(dram[name][TOK:TOK + CAP, :].rearrange("(p t) d -> p (t d)", t=2),
                             zero[:, :]).then_inc(stored, 16)
            sp.wait_ge(stored, 64)

        @block.gpsimd
        def _(pool):
            step = Steps(pool, ctx.enter_context(nc.semaphore("pool_step")))
            step.done(pool.memset(zero[:, :], 0.0))
            step.done(pool.memset(empty[:, :, :], 0.0))
            step.done(pool.memset(k["ident"][:, :], 0.0))
            step.done(pool.memset(k["upto"][:, :], 1.0))
            step.done(pool.memset(k["after"][:, :], 1.0))
            step.done(pool.memset(k["before"][:, :], 1.0))
            step.done(pool.memset(k["ones"][:, :], 1.0))
            step.done(pool.memset(k["half_power"][:, :], -0.5))
            step.done(pool.memset(k["pick"][:, :], 0.0))
            step.done(pool.memset(k["far"][:, :], 0.0))
            step.done(pool.memset(k["ident16"][:, :], 0.0))
            step.done(pool.memset(k["count"][:, :], 0.0))
            step.done(pool.iota(k["token"][:, :], pattern=[[0, 1]], base=0, channel_multiplier=1,
                                allow_small_or_imprecise_dtypes=True))
            step.done(pool.iota(k["numbers"][:, :], pattern=[[1, NE]], base=0, channel_multiplier=0,
                                allow_small_or_imprecise_dtypes=True))
            step.wait()
            step.done(pool.iota(empty[:, :, 0], pattern=[[1, 2]], base=TOK, channel_multiplier=2,
                                allow_small_or_imprecise_dtypes=True))
            step.done(pool.affine_select(out=k["ident"][:, :], in_=k["ident"][:, :], compare_op=ALU.not_equal,
                                         fill=1.0, base=0, pattern=[[-1, P]], channel_multiplier=1))
            step.done(pool.affine_select(out=k["upto"][:, :], in_=k["upto"][:, :], compare_op=ALU.is_ge,
                                         fill=0.0, base=0, pattern=[[1, Q]], channel_multiplier=-1))
            step.done(pool.affine_select(out=k["after"][:, :], in_=k["after"][:, :], compare_op=ALU.is_gt,
                                         fill=0.0, base=0, pattern=[[-1, Q]], channel_multiplier=1))
            step.done(pool.affine_select(out=k["before"][:, :], in_=k["before"][:, :], compare_op=ALU.is_gt,
                                         fill=0.0, base=0, pattern=[[1, Q]], channel_multiplier=-1))
            step.done(pool.affine_select(out=k["far"][:, :], in_=k["far"][:, :], compare_op=ALU.is_ge,
                                         fill=-16384.0, base=0, pattern=[[1, Q]], channel_multiplier=-1))
            step.done(pool.affine_select(out=k["ident16"][:, :], in_=k["ident16"][:, :], compare_op=ALU.not_equal,
                                         fill=1.0, base=0, pattern=[[-1, P]], channel_multiplier=1))
            for part in range(3):
                step.link(pool.affine_select(out=k["pick"][:, :], in_=k["pick"][:, :], compare_op=ALU.not_equal,
                                             fill=1.0, base=-HH * part, pattern=[[-1, HH]], channel_multiplier=1))
            step.link(pool.tensor_scalar(k["unpick"][:, :], k["pick"][:, :], -1.0, None, ALU.mult))
            pool.sem_inc(made, 1)

        @block.tensor
        def _(pe):
            pe.wait_ge(made, 1)
            pe.wait_ge(cls_loaded, 16)
            for c in range(KD):
                last = pe.transpose(clsT[:, c, :], wcls[:, c * P:(c + 1) * P], k["ident"][0:NE, 0:NE])
            last.then_inc(turned, 1)

        @block.vector
        def _(dve):
            step = Steps(dve, dve_step)
            dve.wait_ge(turned, 1)
            step.done(dve.tensor_copy(k["w_cls"][:, :, :], clsT[:, :, :]))
            dve.wait_ge(loaded, 6 * 16)
            step.done(dve.tensor_scalar(k["conv_w"][:, :, :], k["conv_w"][:, :, :], 0.25, None, ALU.mult))
            step.done(dve.tensor_scalar(k["conv_b"][:, :], k["conv_b"][:, :], 0.5, None, ALU.mult))
            dve.wait_ge(act_step, 1)
            step.link(dve.tensor_scalar(k["neg_a"][:, :], k["neg_a"][:, :], -1.0, None, ALU.mult))

        @block.scalar
        def _(act):
            act.wait_ge(loaded, 6 * 16)
            act.activation(k["neg_a"][:, :], k["neg_a"][:, :], ACT.Exp).then_inc(act_step, 1)


def s4d_rows(nc, k, ins, dram):
    with ExitStack() as ctx:
        def sb(name, shape, dt=F32):
            return ctx.enter_context(nc.sbuf_tensor(name, shape, dt))

        def sem(name):
            return ctx.enter_context(nc.semaphore(name))

        inv_a = sb("inv_a", [PAIRS, P])
        a_im = sb("a_im", [PAIRS, P])
        b_ri = sb("b_ri", [PAIRS, P, 2])
        log_dt = sb("log_dt", [PAIRS, 2])
        half_dt = sb("half_dt", [PAIRS, 2])
        two_dt = sb("two_dt", [PAIRS, 2])
        scratch = sb("scratch", [PAIRS, 8, P])
        rows = sb("rows", [PAIRS, 4, P])
        power = sb("power", [P, LOG + 3, 2, PAIRS])
        gain = sb("gain", [P, 2, PAIRS])
        crow = sb("crow", [PAIRS, 2, 2 * P])
        cT = sb("cT", [P, 2, BATCH, PAIRS])
        x = sb("x", [P, 2, BLK, BATCH, PAIRS])
        xt = [sb(f"xt{n}", [P, BATCH, PAIRS]) for n in range(2)]
        v = [sb(f"v{n}", [P, 2, GRP, LOW]) for n in range(2)]
        vt = sb("vt", [P, 4, GRP, LOW // 2])
        xd = sb("xd", [P, 2, GRP, 2, BLK * BATCH])
        kout = sb("kout", [P, GRP, LOW])
        ptab = ctx.enter_context(nc.psum_tensor("ptab", [P, 4, P], F32))
        pct = [ctx.enter_context(nc.psum_tensor(f"pct{n}", [P, 4, P], F32)) for n in range(2)]
        pk = [ctx.enter_context(nc.psum_tensor(f"pk{n}", [P, 4, P], F32)) for n in range(4)]

        params_in = sem("params_in")
        c_in = [sem(f"c_in{n}") for n in range(2)]
        dve_step, pool_step, act_step = sem("dve_step"), sem("pool_step"), sem("act_step")
        exps = sem("exps")
        rows_ready, tab_turned, tab_ready = sem("rows_ready"), sem("tab_turned"), sem("tab_ready")
        c_turned, c_copied = sem("c_turned"), sem("c_copied")
        x_re, x_im = sem("x_re"), sem("x_im")
        v_re, v_im = sem("v_re"), sem("v_im")
        xd_ready, prod_done, k_copied = sem("xd_ready"), sem("prod_done"), sem("k_copied")
        k_stored, kout_free = sem("k_stored"), sem("kout_free")
        cleared = sem("cleared")
        NG = PAIRS // GRP
        block = ctx.enter_context(nc.Block())

        @block.sync
        def _(sp):
            sp.dma_start(inv_a[:, :], ins["L0_tok_inv_A_real"].rearrange("(p r) n -> p (r n)", r=2)).then_inc(params_in, 16)
            sp.dma_start(a_im[:, :], ins["L0_tok_A_imag"].rearrange("(p r) n -> p (r n)", r=2)).then_inc(params_in, 16)
            sp.dma_start(b_ri[:, :, :], ins["L0_tok_B_ri"].rearrange("(p r) n i -> p (r n) i", r=2)).then_inc(params_in, 16)
            sp.dma_start(log_dt[:, :], ins["L0_tok_log_dt"].rearrange("(p r) -> p r", r=2)).then_inc(params_in, 16)
            for c in range(BATCH):
                if c >= 2:
                    sp.wait_ge(c_turned, c - 1)
                sp.dma_start(crow[:, c % 2, :], ins["x"][c].rearrange("(p r) n i -> p (r n i)", r=2)
                             ).then_inc(c_in[c % 2], 16)
            with sp.Fori(0, NG) as g:
                sp.wait_ge(k_copied, 4 * g + 5)
                for r in range(2):
                    for a in range(BLK):
                        lo = (r * BLK + a) * BATCH
                        dst = dram["h"][:, 0:SSM_H, a * P:(a + 1) * P].rearrange(
                            "c (p r) b -> c r p b", r=2)[:, r, bass.ds(g * GRP, GRP), :]
                        sp.dma_start(dst, kout[lo:lo + BATCH, :, :]).then_inc(k_stored, 16)
                sp.wait_ge(k_stored, 16 * 2 * BLK * g + 16 * 2 * BLK)
                sp.sem_inc(kout_free, 1)

        @block.scalar
        def _(act):
            act.wait_ge(params_in, 64)
            act.activation(half_dt[:, :], log_dt[:, :], ACT.Exp).then_inc(exps, 1)
            act.activation(inv_a[:, :], inv_a[:, :], ACT.Exp).then_inc(exps, 1)
            act.wait_ge(tab_turned, 1)
            act.activation(power[:, 0, :, :], ptab[:, 0:2, :], ACT.Copy).then_inc(tab_ready, 1)
            act.activation(gain[:, :, :], ptab[:, 2:4, :], ACT.Copy).then_inc(tab_ready, 1)
            for c in range(BATCH):
                act.wait_ge(c_turned, c + 1)
                act.activation(cT[:, :, c, :], pct[c % 2][:, 0:2, :], ACT.Copy).then_inc(c_copied, 1)
            act.wait_ge(cleared, 1)
            act.wait_ge(x_re, 1)
            act.wait_ge(x_im, 1)
            with act.Fori(0, NG) as g:
                act.wait_ge(prod_done, 4 * g + 1)
                for r in range(2):
                    half = slice(r * SSM_N, (r + 1) * SSM_N)
                    for i in range(2):
                        act.activation(xd[half, i, :, r, :],
                                       x[half, i, :, :, bass.ds(g * GRP, GRP)].rearrange("p a c q -> p q (a c)"),
                                       ACT.Copy, scale=-1.0 if i else 1.0).then_inc(xd_ready, 1)
                act.wait_ge(kout_free, g + 1)
                for b in range(4):
                    act.wait_ge(prod_done, 4 * g + b + 2)
                    act.activation(kout[:, 4 * b:4 * b + 4, :], pk[b][:, :, :], ACT.Copy).then_inc(k_copied, 1)

        @block.tensor
        def _(pe):
            pe.sem_inc(prod_done, 1)
            pe.sem_inc(k_copied, 1)
            pe.sem_inc(kout_free, 1)
            pe.wait_ge(rows_ready, 1)
            for n in range(4):
                last = pe.transpose(ptab[:, n, :], rows[:, n, :], k["ident"][:, :])
            last.then_inc(tab_turned, 1)
            for c in range(BATCH):
                pe.wait_ge(c_in[c % 2], 16 * (c // 2 + 1))
                if c >= 2:
                    pe.wait_ge(c_copied, c - 1)
                for i in range(2):
                    last = pe.transpose(pct[c % 2][:, i, :], crow[:, c % 2, i:2 * P:2], k["ident"][:, :])
                last.then_inc(c_turned, 1)
            with pe.Fori(0, NG // 2) as gg:
                for u in range(2):
                    pe.wait_ge(xd_ready, 8 * gg + 4 * u + 4)
                    pe.wait_ge(v_re, 2 * LOG * gg + LOG * (u + 1) + 1)
                    pe.wait_ge(v_im, 2 * LOG * gg + LOG * (u + 1) + 1)
                    for b in range(4):
                        pe.wait_ge(k_copied, 8 * gg + 4 * u + 1)
                        for q in range(4):
                            pair = 4 * b + q
                            for i in range(2):
                                last = pe.matmul(pk[b][:, q, :], xd[:, i, pair, :, :].rearrange("p r m -> p (r m)"),
                                                 v[u][:, i, pair, :], start=(i == 0), stop=(i == 1))
                        last.then_inc(prod_done, 1)

        def times(eng, out, xr, xi, pr, pi, step, imaginary, t1, t2):
            step.done(eng.tensor_tensor(t1, xr, pi if imaginary else pr, ALU.mult))
            step.link(eng.tensor_tensor(t2, xi, pr if imaginary else pi, ALU.mult))
            return eng.tensor_tensor(out, t1, t2, ALU.add if imaginary else ALU.subtract)

        x_part = [sem("x_part_re"), sem("x_part_im")]
        pow_re, pow_im = sem("pow_re"), sem("pow_im")
        pw = [pow_re, pow_im]
        vs = [v_re, v_im]
        cleared_v = sem("cleared_v")

        def part_of(eng, part, step, spare):
            im = part == 1
            pt = sb(f"pt{part}", [P, 2, PAIRS])
            eng.wait_ge(tab_ready, 2)
            for n in range(LOG):
                if n:
                    eng.wait_ge(pow_re, n)
                    eng.wait_ge(pow_im, n)
                re, imag = power[:, n, 0, :], power[:, n, 1, :]
                times(eng, power[:, n + 1, part, :], re, imag, re, imag, step, im, pt[:, 0, :], pt[:, 1, :]
                      ).then_inc(pw[part], 1)
            eng.wait_ge(pow_re, LOG)
            eng.wait_ge(pow_im, LOG)
            eng.wait_ge(c_copied, BATCH)
            shape = [P, BATCH, PAIRS]
            for a in range(BLK):
                if a == 0:
                    xr, xi, pr, pi = cT[:, 0], cT[:, 1], gain[:, 0, :], gain[:, 1, :]
                else:
                    xr, xi = x[:, 0, a - 1], x[:, 1, a - 1]
                    pr, pi = power[:, LOG, 0, :], power[:, LOG, 1, :]
                    eng.wait_ge(x_part[0], a)
                    eng.wait_ge(x_part[1], a)
                times(eng, x[:, part, a], xr, xi, bc(pr.unsqueeze(1), shape), bc(pi.unsqueeze(1), shape), step, im,
                      xt[part][:, :, :], spare).then_inc(x_part[part], 1)
            eng.wait_ge(x_part[0], BLK)
            eng.wait_ge(x_part[1], BLK)
            eng.sem_inc(x_im if im else x_re, 1)
            for u in range(2):
                step.done(eng.memset(v[u][:, part, :, 0:1], 0.0 if im else 1.0))
            step.wait()
            eng.sem_inc(cleared_v, 1)
            eng.sem_inc(vs[part], 1)
            eng.wait_ge(cleared_v, 2)
            with eng.Fori(0, NG // 2) as gg:
                step.loop(gg, 2 * 2 * LOG)
                for u in range(2):
                    eng.wait_ge(prod_done, 8 * gg + 1)
                    for n in range(LOG):
                        w = 1 << n
                        done = 2 * LOG * gg + LOG * u + n + 1
                        eng.wait_ge(v_re, done)
                        eng.wait_ge(v_im, done)
                        shape_v = [P, GRP, w]
                        pr, pi = (power[:, n, i, bass.ds(gg * 2 * GRP + u * GRP, GRP)].unsqueeze(2).broadcast_to(shape_v)
                                  for i in range(2))
                        times(eng, v[u][:, part, :, w:2 * w], v[u][:, 0, :, 0:w], v[u][:, 1, :, 0:w], pr, pi, step, im,
                              vt[:, 2 * part, :, 0:w], vt[:, 2 * part + 1, :, 0:w]).then_inc(vs[part], 1)
                step.end(NG // 2)

        @block.gpsimd
        def _(pool):
            step = Steps(pool, pool_step)
            step.link(pool.memset(xd[:, :, :, :, :], 0.0))
            pool.sem_inc(cleared, 1)
            part_of(pool, 1, step, v[1][:, :, :, :].rearrange("p i q b -> p (i q b)")[:, 0:BATCH * PAIRS]
                    .rearrange("p (c q) -> p c q", c=BATCH))

        @block.vector
        def _(dve):
            step = Steps(dve, dve_step)
            t = [scratch[:, n, :] for n in range(8)]
            two = lambda ap: ap.rearrange("p (r n) -> p r n", r=2)
            dve.wait_ge(exps, 2)
            step.done(dve.tensor_scalar(two_dt[:, :], half_dt[:, :], 2.0, None, ALU.mult))
            step.link(dve.tensor_scalar(half_dt[:, :], half_dt[:, :], 0.5, None, ALU.mult))
            hd, td = (bc(z[:, :].unsqueeze(2), [PAIRS, 2, SSM_N]) for z in (half_dt, two_dt))
            step.done(dve.tensor_tensor(two(t[0]), two(inv_a[:, :]), hd, ALU.mult))
            step.link(dve.tensor_tensor(two(t[1]), two(a_im[:, :]), hd, ALU.mult))
            step.done(dve.tensor_scalar(t[2], t[0], 1.0, None, ALU.add))
            step.done(dve.tensor_scalar(t[3], t[0], -1.0, 1.0, ALU.mult, ALU.add))
            step.link(dve.tensor_tensor(t[4], t[1], t[1], ALU.mult))
            step.link(dve.tensor_tensor(t[5], t[2], t[2], ALU.mult))
            step.link(dve.tensor_tensor(t[5], t[5], t[4], ALU.add))
            step.link(dve.reciprocal(t[6], t[5]))
            step.link(dve.tensor_tensor(t[7], t[3], t[2], ALU.mult))
            step.link(dve.tensor_tensor(t[7], t[7], t[4], ALU.subtract))
            step.done(dve.tensor_tensor(rows[:, 0, :], t[7], t[6], ALU.mult))
            step.done(dve.scalar_tensor_tensor(rows[:, 1, :], t[1], 2.0, t[6], ALU.mult, ALU.mult))
            dve.wait_ge(params_in, 64)
            br, bi = b_ri[:, :, 0], b_ri[:, :, 1]
            step.done(dve.tensor_tensor(t[0], br, t[2], ALU.mult))
            step.done(dve.tensor_tensor(t[3], bi, t[1], ALU.mult))
            step.done(dve.tensor_tensor(t[4], bi, t[2], ALU.mult))
            step.link(dve.tensor_tensor(t[5], br, t[1], ALU.mult))
            step.done(dve.tensor_tensor(t[0], t[0], t[3], ALU.subtract))
            step.done(dve.tensor_tensor(t[4], t[4], t[5], ALU.add))
            step.link(dve.tensor_tensor(two(t[6]), two(t[6]), td, ALU.mult))
            step.done(dve.tensor_tensor(rows[:, 2, :], t[0], t[6], ALU.mult))
            step.link(dve.tensor_tensor(rows[:, 3, :], t[4], t[6], ALU.mult))
            dve.sem_inc(rows_ready, 1)
            part_of(dve, 0, step, v[0][:, :, :, :].rearrange("p i q b -> p (i q b)")[:, 0:BATCH * PAIRS]
                    .rearrange("p (c q) -> p c q", c=BATCH))


DVE_STEPS = 143


def sequences(nc, k, ins, dram):
    with ExitStack() as ctx:
        def sb(name, shape, dt=F32):
            return ctx.enter_context(nc.sbuf_tensor(name, shape, dt))

        def pb(name):
            return ctx.enter_context(nc.psum_tensor(name, [P, 512], F32))

        def sem(name):
            return ctx.enter_context(nc.semaphore(name))

        w_in = k["w_in"]
        hin = sb("hin", [Q, CH, DM])
        hres = sb("hres", [Q, CH, DM])
        stats = sb("stats", [Q, CH, 6])
        mv = sb("mv", [Q, CH, 2])
        var_e = sb("var_e", [Q, CH])
        rstd = sb("rstd", [Q, CH])
        xn = sb("xn", [Q, CH, DM])
        xnT = sb("xnT", [P, KD, SEQ])
        sp = sb("sp", [Q, 6, CH, HEADS])
        dt = sb("dt", [Q, CH, HEADS])
        a = sb("a", [Q, CH, HEADS])
        a3 = sb("a3", [Q, 2 * CH, 3, HH])
        cacc = [sb(f"cacc{n}", [P, SEQ]) for n in range(2)]
        cth = [sb(f"cth{n}", [P, SEQ]) for n in range(2)]
        xbcT = sb("xbcT", [P, CONV_TILES, SEQ])
        parts = sb("parts", [3 * HH, CH, 2 * Q], BF16)
        mid = sb("mid", [3 * HH, 2 * Q], BF16)
        rest = sb("rest", [3 * HH, 2, 2 * Q])
        grow = sb("grow", [Q, CH, HEADS])
        fall = sb("fall", [Q, CH, HEADS])
        total = sb("total", [P, CH, HEADS])
        xrow = sb("xrow", [Q, INTER])
        zt = sb("zt", [Q, INTER])
        zs = sb("zs", [Q, INTER])
        cbm = sb("cbm", [Q, CH, Q])
        brow = sb("brow", [Q, 2, NST])
        dtx = sb("dtx", [Q, 2, INTER])
        dtxf = sb("dtxf", [Q, 2, INTER])
        skip = sb("skip", [Q, INTER])
        yint = sb("yint", [Q, INTER])
        state = sb("state", [P, 2, INTER])
        kept = sb("kept", [P, INTER])
        lx = [sb(f"lx{n}", [Q, HG, Q]) for n in range(2)]
        m_ = [sb(f"m{n}", [Q, HG, Q]) for n in range(3)]
        y = sb("y", [Q, INTER])
        gg = sb("gg", [Q, INTER])
        ggT = sb("ggT", [P, INTER // P, Q])
        ss = sb("ss", [Q, CH])
        h2 = sb("h2", [Q, CH, DM])
        x2 = sb("x2s", [Q, CH, DM])
        x2T = sb("x2T", [P, KD, Q])
        stat2 = sb("stat2", [Q, 6])
        mv2 = sb("mv2", [Q, 2])
        small = sb("small", [Q, 12])
        ex = sb("ex", [Q, NE])
        score = sb("score", [Q, NE])
        biased = sb("biased", [Q, NE])
        top = sb("top", [Q, TOPK])
        topi = sb("topi", [Q, TOPK], U32)
        r8 = sb("r8", [Q, 8, TOPK])
        hot = sb("hot", [Q, TOPK, NE])
        hots = sb("hots", [Q, TOPK, NE])
        sel = sb("sel", [Q, E])
        place = sb("place", [Q, E])
        entry = sb("entry", [Q, CH, TOPK, 2])
        slot = sb("slot", [Q, CH, TOPK], U32)
        idle = sb("idle", [Q, 4])
        credit = sb("credit", [Q, CH + 1, 2])

        nar = [pb(f"nar{n}") for n in range(2)]
        dec = [pb(f"dec{n}") for n in range(2)]
        wide = ctx.enter_context(nc.psum_tensor("wide", [P, 1024], F32))
        ysum = ctx.enter_context(nc.psum_tensor("ysum", [P, 1024], F32))

        names = ["xn_done", "xn_turned", "xnT_done", "hres_used", "var1", "rstd1", "exp_m", "one_plus", "logged",
                 "sp_m", "a_done", "base", "tanhed", "conv_done", "tapped", "cum_exp", "parts_done", "cbm_done",
                 "xrow_done", "z_tanh", "zs_done", "dtx_done", "dtxf_done", "skip_done", "yint_done",
                 "skip_sum", "state_done", "kept_done", "lx_done", "m_done", "y_heads", "y_full", "y_done",
                 "gg_done", "gg_turned", "sq_done", "ggT_done", "var_y", "rstd_y", "h2_done", "var2", "rstd2", "x2_done",
                 "x2T_done", "neg_max", "exped", "sel_done", "entry_done", "dt_read", "count_done"]
        ev = {n: sem(n) for n in names}
        nar_full = [sem(f"nar_full{n}") for n in range(2)]
        dec_full = [sem(f"dec_full{n}") for n in range(2)]
        wide_full = sem("wide_full")
        entry_free = sem("entry_free")
        hin_in, hres_in = sem("hin_in"), sem("hres_in")
        stored = [sem(f"stored{j}") for j in range(CH)]
        scattered = sem("scattered")
        dve_step = sem("b_dve_step")
        act_step = sem("b_act_step")

        with nc.Block() as first:
            @first.gpsimd
            def _(pool):
                for s in list(ev.values()) + nar_full + dec_full + [wide_full]:
                    pool.sem_inc(s, 1)
                pool.sem_inc(entry_free, 2)
                pool.sem_inc(dve_step, 1)
                pool.dma_start(credit[:, CH, :], dram["x2"][TOK:TOK + Q, 0:2]).then_inc(scattered, 16)
                pool.wait_ge(scattered, 16)

            @first.sync
            def _(sy):
                for j in range(CH):
                    sy.dma_start(credit[:, j, :], dram["x2"][TOK:TOK + Q, 0:2]).then_inc(stored[j], 16)
                    sy.wait_ge(stored[j], 16)

        def narrow(use):
            n = NARROW.index(use)
            return n % 2, len(NARROW) // 2, n // 2

        block = ctx.enter_context(nc.Block())

        def wait(eng, name, n):
            eng.wait_ge(ev[name], n + 1)

        def wait_narrow_full(eng, i, use):
            b, per, n = narrow(use)
            eng.wait_ge(nar_full[b], i * per + n + 2)
            return nar[b]

        def wait_wide_full(eng, i, use):
            eng.wait_ge(wide_full, i * len(WIDE) + WIDE.index(use) + 2)

        def read_by(kind, n):
            return {
                "xnT": [("xnT_done", n + 1, CH)],
                "dt": [("dt_read", 1, 1)],
                "conv": [("tapped", conv_order().index(n) + 1 if kind == "conv" else 0, CONV_TILES)],
                "cum": [("cum_exp", n + 1, CH), ("parts_done", n + 1, CH)],
                "cb": [("cbm_done", n + 1, CH)],
                "out": [("h2_done", n + 1, CH)],
                "x2T": [("x2T_done", n + 1, CH)],
                "logits": [("exped", n + 1, CH)],
                "rank": [("count_done", n + 1, CH)],
                "xrow": [("xrow_done", n + 1, CH)],
                "z": [("zs_done", n + 1, CH)],
                "inter": [("yint_done", n, CH - 1)],
                "state": [("state_done", n + 1, CH - 1)],
                "gT": [("ggT_done", n + 1, CH)],
            }[kind]

        PIECES = {1: "out", 7: "x2T", 10: "logits", 14: "rank"}

        @block.sync
        def _(sy):
            with sy.Fori(0, BATCH) as i:
                wait(sy, "xn_done", CH * i)
                sy.dma_start(hin[:, :, :], dram["h"][i].rearrange("(j p) d -> p j d", p=Q)).then_inc(hin_in, 16)
                wait(sy, "h2_done", CH * i)
                sy.dma_start(hres[:, :, :], dram["h"][i].rearrange("(j p) d -> p j d", p=Q)).then_inc(hres_in, 16)
            for j in range(CH):
                sy.wait_ge(stored[j], 16 + 32 * BATCH)

        @block.tensor
        def _(pe):
            def take(i, uses, use, banks):
                at = uses.index(use)
                was = at - banks
                turn = i if was >= 0 else i - 1
                for event, n, per in read_by(*uses[was]):
                    wait(pe, event, turn * per + n)
                return at % banks

            def take_narrow(i, use):
                return nar[take(i, NARROW, use, 2)]

            def narrow_done(ins_, use):
                ins_.then_inc(nar_full[narrow(use)[0]], 1)

            def take_wide(i, use):
                take(i, WIDE, use, 1)

            def chunk(j):
                return slice(j * Q, (j + 1) * Q)

            def tail(i, j, piece):
                if piece == "out":
                    wait(pe, "gg_done", CH * i + j + 1)
                    take_wide(i, ("gT", j))
                    for f in range(INTER // P):
                        last = pe.transpose(wide[:, (f // 4) * 512 + (f % 4) * Q:(f // 4) * 512 + (f % 4 + 1) * Q],
                                            gg[:, f * P:(f + 1) * P], k["ident"][0:Q, 0:Q])
                    last.then_inc(wide_full, 1)
                    ps = take_narrow(i, ("out", j))
                    wait(pe, "ggT_done", CH * i + j + 1)
                    for f in range(INTER // P):
                        last = pe.matmul(ps[0:Q, :], ggT[:, f, :], k["w_out"][:, f, :], start=(f == 0),
                                         stop=(f == INTER // P - 1))
                    narrow_done(last, ("out", j))
                elif piece == "x2T":
                    wait(pe, "x2_done", CH * i + j + 1)
                    ps = take_narrow(i, ("x2T", j))
                    for c in range(KD):
                        last = pe.transpose(ps[:, c * Q:(c + 1) * Q], x2[:, j, c * P:(c + 1) * P],
                                            k["ident"][0:Q, 0:Q])
                    narrow_done(last, ("x2T", j))
                elif piece == "logits":
                    wait(pe, "x2T_done", CH * i + j + 1)
                    ps = take_narrow(i, ("logits", j))
                    for c in range(KD):
                        last = pe.matmul(ps[0:Q, 0:NE], x2T[:, c, :], k["w_cls"][:, c, :], start=(c == 0),
                                         stop=(c == KD - 1))
                    narrow_done(last, ("logits", j))
                else:
                    wait(pe, "sel_done", CH * i + j + 1)
                    ps = take_narrow(i, ("rank", j))
                    pe.matmul(ps[0:Q, 0:E], k["before"][:, :], sel[:, :], start=True, stop=True)
                    narrow_done(pe.matmul(ps[0:Q, E:2 * E], k["ones"][:, 0:Q], sel[:, :], start=True, stop=True),
                                ("rank", j))

            with pe.Fori(0, BATCH) as i:
                for j in range(CH):
                    wait(pe, "xn_done", CH * i + j + 1)
                    ps = take_narrow(i, ("xnT", j))
                    for c in range(KD):
                        last = pe.transpose(ps[:, c * Q:(c + 1) * Q], xn[:, j, c * P:(c + 1) * P],
                                            k["ident"][0:Q, 0:Q])
                    narrow_done(last, ("xnT", j))
                ps = take_narrow(i, ("dt", 0))
                wait(pe, "xnT_done", CH * i + CH)
                for j in range(CH):
                    for c in range(KD):
                        last = pe.matmul(ps[0:Q, j * HEADS:(j + 1) * HEADS], xnT[:, c, chunk(j)],
                                         w_in[:, c, DT0:PROJ], start=(c == 0), stop=(c == KD - 1))
                narrow_done(last, ("dt", 0))
                for m in conv_order():
                    ps = take_narrow(i, ("conv", m))
                    for c in range(KD):
                        last = pe.matmul(ps[:, 0:SEQ], w_in[:, c, XBC0 + m * P:XBC0 + (m + 1) * P], xnT[:, c, :],
                                         start=(c == 0), stop=(c == KD - 1))
                    narrow_done(last, ("conv", m))
                for j in range(CH):
                    ps = take_narrow(i, ("cum", j))
                    wait(pe, "a_done", i + 1)
                    for half in range(2):
                        pe.matmul(ps[0:3 * HH, half * Q:(half + 1) * Q], a3[:, 2 * j + half, :, :].rearrange("p r h -> p (r h)"),
                                  k["upto"][:, :],
                                  start=True, stop=True)
                    o = 2 * Q
                    pe.matmul(ps[0:Q, o:o + HEADS], k["upto"][:, :], a[:, j, :], start=True, stop=True)
                    pe.matmul(ps[0:Q, o + HEADS:o + 2 * HEADS], k["after"][:, :], a[:, j, :], start=True, stop=True)
                    narrow_done(pe.matmul(ps[:, o + 2 * HEADS:o + 3 * HEADS], k["ones"][:, :], a[:, j, :],
                                          start=True, stop=True), ("cum", j))
                for j in range(CH):
                    bT, cT = xbcT[:, B_TILE, chunk(j)], xbcT[:, C_TILE, chunk(j)]
                    ps = take_narrow(i, ("cb", j))
                    wait(pe, "conv_done", CONV_TILES * i + 2)
                    last = pe.matmul(ps[0:Q, 0:Q], bT, cT, start=True, stop=True)
                    if j < CH - 1:
                        last = pe.transpose(ps[0:Q, P:P + NST], bT, k["ident"][:, :])
                    narrow_done(last, ("cb", j))
                    take_wide(i, ("xrow", j))
                    wait(pe, "conv_done", CONV_TILES * (i + 1))
                    for m in range(B_TILE):
                        last = pe.transpose(wide[0:Q, m * P:(m + 1) * P], xbcT[:, m, chunk(j)], k["ident"][:, :])
                    last.then_inc(wide_full, 1)
                    take_wide(i, ("z", j))
                    for half in range(2):
                        for c in range(KD):
                            last = pe.matmul(wide[0:Q, half * 512:(half + 1) * 512], xnT[:, c, chunk(j)],
                                             w_in[:, c, half * 512:(half + 1) * 512], start=(c == 0),
                                             stop=(c == KD - 1))
                    last.then_inc(wide_full, 1)
                    if j:
                        take_wide(i, ("inter", j))
                        wait(pe, "state_done", 2 * i + j)
                        for half in range(2):
                            last = pe.matmul(wide[0:Q, half * 512:(half + 1) * 512], cT,
                                             state[:, j - 1, half * 512:(half + 1) * 512], start=True, stop=True)
                        last.then_inc(wide_full, 1)
                    if j < CH - 1:
                        take_wide(i, ("state", j))
                        wait(pe, "dtxf_done", 2 * i + j + 1)
                        wait(pe, "cbm_done", CH * i + j + 1)
                        for half in range(2):
                            last = pe.matmul(wide[:, half * 512:(half + 1) * 512], brow[:, j, :],
                                             dtxf[:, j, half * 512:(half + 1) * 512], start=True, stop=True)
                        last.then_inc(wide_full, 1)

                    def decay(g):
                        q = GROUPS * j + g
                        b = q % 2
                        if g == 0:
                            wait(pe, "parts_done", CH * i + j + 1)
                        wait(pe, "lx_done", CH * GROUPS * i + max(q - 1, 0))
                        half, h0 = divmod(g * HG, HH)
                        cum = parts[:, j, half * Q:(half + 1) * Q]
                        pe.matmul(dec[b][0:Q, 0:HG * Q], cum,
                                  k["unpick"][:, h0:h0 + HG].unsqueeze(2).broadcast_to([3 * HH, HG, Q]),
                                  start=True, stop=False, skip_group_check=True)
                        pe.matmul(dec[b][0:Q, 0:HG * Q], k["ident16"][0:Q, 0:Q],
                                  k["far"][:, :].unsqueeze(1).broadcast_to([Q, HG, Q]),
                                  start=False, stop=False, skip_group_check=True)
                        for n_ in range(HG):
                            last_ = pe.matmul(dec[b][0:Q, n_ * Q:(n_ + 1) * Q],
                                              k["pick"][:, h0 + n_:h0 + n_ + 1].broadcast_to([3 * HH, Q]),
                                              cum, start=False, stop=(n_ == HG - 1), skip_group_check=True)
                        last_.then_inc(dec_full[b], 1)

                    decay(0)
                    decay(1)
                    wait(pe, "dtx_done", CH * i + j + 1)
                    wait(pe, "y_done", CH * i + j)
                    for g in range(GROUPS):
                        if g + 2 < GROUPS:
                            decay(g + 2)
                        q = GROUPS * j + g
                        wait(pe, "m_done", CH * GROUPS * i + q + 1)
                        for n in range(HG):
                            h = g * HG + n
                            last = pe.matmul(ysum[0:Q, h * HD:(h + 1) * HD], m_[q % 3][:, n, :],
                                             dtx[:, j % 2, h * HD:(h + 1) * HD], start=True, stop=True)
                        last.then_inc(ev["y_heads"], 1)
                        if j and g in PIECES:
                            tail(i, j - 1, PIECES[g])
                for piece in PIECES.values():
                    tail(i, CH - 1, piece)

        @block.scalar
        def _(act):
            def tail(i, j, piece):
                n = CH * i + j
                if piece == "out":
                    wait_wide_full(act, i, ("gT", j))
                    act.activation(ggT[:, :, :].rearrange("p (u f) q -> p u (f q)", u=2),
                                   wide[:, :].rearrange("p (u c) -> p u c", u=2)[:, :, 0:4 * Q], ACT.Copy
                                   ).then_inc(ev["ggT_done"], 1)
                elif piece == "x2T":
                    wait(act, "x2_done", n + 1)
                    act.dma_start(dram["acc"][0:TOK, :].rearrange("(c j p) d -> c j p d", j=CH, p=Q)[i, j],
                                  h2[:, j, :]).then_inc(stored[j], 16)
                    act.dma_start(dram["x2"][0:TOK, :].rearrange("(c j p) d -> c j p d", j=CH, p=Q)[i, j],
                                  x2[:, j, :]).then_inc(stored[j], 16)
                    ps = wait_narrow_full(act, i, ("x2T", j))
                    act.activation(x2T[:, :, :].rearrange("p c q -> p (c q)"), ps[:, 0:KD * Q], ACT.Copy
                                   ).then_inc(ev["x2T_done"], 1)
                elif piece == "logits":
                    ps = wait_narrow_full(act, i, ("logits", j))
                    wait(act, "neg_max", n + 1)
                    ins_ = act.activation(ex[:, :], ps[0:Q, 0:NE], ACT.Exp, bias=small[:, 0:1],
                                          accum_out=small[:, 1:2])
                    ins_.then_inc(ev["exped"], 1)

            with act.Fori(0, BATCH) as i:
                for j in range(CH):
                    ps = wait_narrow_full(act, i, ("xnT", j))
                    act.activation(xnT[:, :, j * Q:(j + 1) * Q], ps[:, 0:KD * Q].rearrange("p (c q) -> p c q", c=KD),
                                   ACT.Copy).then_inc(ev["xnT_done"], 1)

                def conv_base(n):
                    m = conv_order()[n]
                    ps = wait_narrow_full(act, i, ("conv", m))
                    wait(act, "conv_done", CONV_TILES * i + max(n - 1, 0))
                    act.activation(cacc[n % 2][:, :], ps[:, 0:SEQ], ACT.Identity, scale=k["conv_w"][:, m, 3:4],
                                   bias=k["conv_b"][:, m:m + 1]).then_inc(ev["base"], 1)

                def conv_tanh(n):
                    wait(act, "tapped", CONV_TILES * i + n + 1)
                    act.activation(cth[n % 2][:, :], cacc[n % 2][:, :], ACT.Tanh).then_inc(ev["tanhed"], 1)

                wait(act, "sp_m", i + 1)
                act.activation(sp[:, 2], sp[:, 1], ACT.Exp).then_inc(ev["exp_m"], 1)
                wait(act, "one_plus", i + 1)
                act.activation(sp[:, 4], sp[:, 3], ACT.Ln).then_inc(ev["logged"], 1)
                conv_base(0)
                for n in range(1, CONV_TILES):
                    conv_base(n)
                    conv_tanh(n - 1)
                conv_tanh(CONV_TILES - 1)
                for j in range(CH):
                    o = 2 * Q
                    ps = wait_narrow_full(act, i, ("cum", j))
                    act.activation(grow[:, j, :], ps[0:Q, o:o + HEADS], ACT.Exp)
                    act.activation(fall[:, j, :], ps[0:Q, o + HEADS:o + 2 * HEADS], ACT.Exp)
                    act.activation(total[:, j, :], ps[:, o + 2 * HEADS:o + 3 * HEADS], ACT.Exp
                                   ).then_inc(ev["cum_exp"], 1)
                for j in range(CH):
                    wait_wide_full(act, i, ("xrow", j))
                    wait(act, "skip_done", CH * i + j)
                    act.activation(xrow[:, :], wide[0:Q, :], ACT.Copy).then_inc(ev["xrow_done"], 1)
                    wait_wide_full(act, i, ("z", j))
                    wait(act, "zs_done", CH * i + j)
                    act.activation(zt[:, :], wide[0:Q, :], ACT.Tanh, scale=0.125).then_inc(ev["z_tanh"], 1)
                    for g in range(GROUPS):
                        q = GROUPS * j + g
                        act.wait_ge(dec_full[q % 2], CH * GROUPS // 2 * i + q // 2 + 2)
                        wait(act, "m_done", CH * GROUPS * i + max(q - 1, 0))
                        act.activation(lx[q % 2][:, :, :], dec[q % 2][0:Q, 0:HG * Q].rearrange("p (h t) -> p h t", h=HG),
                                       ACT.Exp).then_inc(ev["lx_done"], 1)
                        if j and g in PIECES:
                            tail(i, j - 1, PIECES[g])
                    wait(act, "y_done", CH * i + j + 1)
                    act.activation(zt[:, :], y[:, :], ACT.Square, accum_out=ss[:, j:j + 1]
                                   ).then_inc(ev["sq_done"], 1)
                for piece in PIECES.values():
                    tail(i, CH - 1, piece)

        @block.gpsimd
        def _(pool):
            def heads(ap):
                return ap.rearrange("p (h d) -> p h d", h=HEADS)

            def spread(ap, rows=Q):
                return ap.unsqueeze(2).broadcast_to([rows, HEADS, HD])

            def tail(i, j, piece):
                n = CH * i + j
                if piece == "out":
                    wait(pool, "var_y", n + 1)
                    pool.tensor_tensor(small[:, 3:4], small[:, 2:3], k["half_power"][0:Q, 0:1], ALU.pow
                                       ).then_inc(ev["rstd_y"], 1)
                    wait(pool, "var2", n + 1)
                    pool.tensor_tensor(small[:, 5:6], small[:, 4:5], k["half_power"][0:Q, 0:1], ALU.pow
                                       ).then_inc(ev["rstd2"], 1)
                elif piece == "rank":
                    pool.wait_ge(scattered, 16 + 16 * TOPK * n)
                    pool.sem_inc(entry_free, 1)
                    wait(pool, "entry_done", n + 1)
                    pool.tensor_tensor(idle[:, 2:3], k["half_power"][0:Q, 0:1], k["half_power"][0:Q, 0:1], ALU.mult)
                    for c in range(TOPK):
                        pool.indirect_dma_start(
                            out=dram["slots"], out_offset=bass.IndirectOffsetOnAxis(ap=slot[:, j, c:c + 1], axis=0),
                            in_=entry[:, j, c, :], in_offset=None, bounds_check=SLOTS - 1, oob_is_err=False
                        ).then_inc(scattered, 16)

            with pool.Fori(0, BATCH) as i:
                wait(pool, "var1", i + 1)
                pool.tensor_tensor(rstd[:, :], var_e[:, :], k["half_power"][0:Q, 0:CH], ALU.pow
                                   ).then_inc(ev["rstd1"], 1)
                for j in range(CH):
                    n = CH * i + j
                    wait(pool, "xrow_done", n + 1)
                    wait(pool, "a_done", i + 1)
                    pool.tensor_tensor(heads(dtx[:, j % 2, :]), heads(xrow[:, :]), spread(dt[:, j, :]), ALU.mult
                                       ).then_inc(ev["dtx_done"], 1)
                    if j < CH - 1:
                        wait(pool, "cum_exp", CH * i + j + 1)
                        wait(pool, "dtx_done", n + 1)
                        pool.tensor_tensor(heads(dtxf[:, j, :]), heads(dtx[:, j % 2, :]), spread(fall[:, j, :]), ALU.mult
                                           ).then_inc(ev["dtxf_done"], 1)
                    pool.tensor_tensor(heads(skip[:, :]), heads(xrow[:, :]), spread(k["skip_d"][:, :]), ALU.mult
                                       ).then_inc(ev["skip_done"], 1)
                    if j == 1:
                        wait(pool, "state_done", 2 * i + 1)
                        pool.tensor_tensor(heads(kept[:, :]), heads(state[:, 0, :]), spread(total[:, 1, :], P), ALU.mult
                                           ).then_inc(ev["kept_done"], 1)
                    wait(pool, "skip_done", n + 1)
                    if j:
                        wait(pool, "yint_done", 2 * i + j)
                        pool.tensor_tensor(skip[:, :], skip[:, :], yint[:, :], ALU.add
                                           ).then_inc(ev["skip_sum"], 1)
                    if j:
                        for g in sorted(PIECES):
                            tail(i, j - 1, PIECES[g])
                    wait(pool, "y_done", n + 1)
                    wait(pool, "zs_done", n + 1)
                    pool.tensor_tensor(gg[:, :], y[:, :], zs[:, :], ALU.mult).then_inc(ev["gg_done"], 1)
                for piece in PIECES.values():
                    tail(i, CH - 1, piece)
            pool.wait_ge(scattered, 16 + 16 * TOPK * CH * BATCH)

        @block.vector
        def _(dve):
            step = Steps(dve, dve_step)
            step.n = 1

            def heads(ap):
                return ap.rearrange("p (h d) -> p h d", h=HEADS)

            def spread(ap):
                return ap.unsqueeze(2).broadcast_to([Q, HEADS, HD])

            def hold():
                dve.memset(idle[:, 0:1], 0.0)

            def done(ins_, name):
                ins_.then_inc(ev[name], 1)

            def tail(i, j, piece):
                n = CH * i + j
                if piece == "out":
                    wait(dve, "sq_done", n + 1)
                    done(dve.tensor_scalar(small[:, 2:3], ss[:, j:j + 1], 1.0 / INTER, EPS, ALU.mult, ALU.add), "var_y")
                    wait(dve, "rstd_y", n + 1)
                    step.link(dve.tensor_scalar(small[:, 6:7], small[:, 3:4], 0.125, None, ALU.mult))
                    if j == 0:
                        dve.wait_ge(hres_in, 16 * i + 16)
                    dve.wait_ge(stored[j], 32 * i + 16)
                    ps = wait_narrow_full(dve, i, ("out", j))
                    ins_ = dve.scalar_tensor_tensor(h2[:, j, :], ps[0:Q, :], small[:, 6:7], hres[:, j, :],
                                                    ALU.mult, ALU.add)
                    done(ins_, "h2_done")
                    wait(dve, "h2_done", n + 1)
                    step.link(dve.bn_stats(stat2[:, :], h2[:, j, :]))
                    hold()
                    step.link(dve.bn_aggr(mv2[:, :], stat2[:, :]))
                    done(dve.tensor_scalar(small[:, 4:5], mv2[:, 1:2], EPS, None, ALU.add), "var2")
                    wait(dve, "rstd2", n + 1)
                    done(dve.tensor_scalar(x2[:, j, :], h2[:, j, :], mv2[:, 0:1], small[:, 5:6], ALU.subtract,
                                           ALU.mult), "x2_done")
                elif piece == "logits":
                    ps = wait_narrow_full(dve, i, ("logits", j))
                    step.link(dve.tensor_reduce(small[:, 7:8], ps[0:Q, 0:NE], AX, ALU.max))
                    done(dve.tensor_scalar(small[:, 0:1], small[:, 7:8], -1.0, None, ALU.mult), "neg_max")
                    wait(dve, "exped", n + 1)
                    step.link(dve.reciprocal(small[:, 8:9], small[:, 1:2]))
                    step.done(dve.tensor_scalar(score[:, :], ex[:, :], small[:, 8:9], None, ALU.mult))
                    step.link(dve.scalar_tensor_tensor(biased[:, :], ex[:, :], small[:, 8:9], k["top_bias"][:, :],
                                                       ALU.mult, ALU.add))
                    hold()
                    step.link(dve.max(top[:, :], biased[:, :]))
                    hold()
                    step.link(dve.max_index(topi[:, :], top[:, :], biased[:, :]))
                    step.link(dve.tensor_copy(r8[:, 0, :], topi[:, :]))
                    step.link(dve.tensor_tensor(hot[:, :, :],
                                                k["numbers"][:, :].unsqueeze(1).broadcast_to([Q, TOPK, NE]),
                                                r8[:, 0, :].unsqueeze(2).broadcast_to([Q, TOPK, NE]), ALU.is_equal))
                    done(dve.tensor_reduce(sel[:, :], hot[:, :, 0:E].rearrange("p c e -> p e c"), AX, ALU.add),
                         "sel_done")
                    step.link(dve.tensor_tensor(hots[:, :, :], hot[:, :, :],
                                                score[:, :].unsqueeze(1).broadcast_to([Q, TOPK, NE]), ALU.mult))
                    step.link(dve.tensor_reduce(r8[:, 1, :], hots[:, :, :], AX, ALU.add))
                    step.link(dve.tensor_reduce(small[:, 9:10], r8[:, 1, :], AX, ALU.add))
                    step.link(dve.tensor_scalar(small[:, 9:10], small[:, 9:10], 1e-20, None, ALU.add))
                    step.link(dve.reciprocal(small[:, 10:11], small[:, 9:10]))
                    step.done(dve.tensor_scalar(r8[:, 2, :], r8[:, 1, :], small[:, 10:11], 1.5, ALU.mult, ALU.mult))
                    step.link(dve.tensor_scalar(r8[:, 3, :], r8[:, 0, :], float(E), None, ALU.is_lt))
                    step.link(dve.tensor_tensor(r8[:, 4, :], r8[:, 2, :], r8[:, 3, :], ALU.mult))
                    step.link(dve.tensor_tensor(r8[:, 5, :], r8[:, 2, :], r8[:, 4, :], ALU.subtract))
                    step.link(dve.tensor_reduce(small[:, 11:12], r8[:, 5, :], AX, ALU.add))
                    step.link(dve.tensor_scalar(small[:, 11:12], small[:, 11:12], 1.0, None, ALU.add))
                    dve.wait_ge(entry_free, n + 1)
                    step.done(dve.tensor_scalar(entry[:, j, :, 1], r8[:, 4, :], small[:, 11:12], None, ALU.mult))
                    step.done(dve.tensor_copy(entry[:, j, :, 0], k["token"][:, 0:1].broadcast_to([Q, TOPK])))
                elif piece == "rank":
                    ps = wait_narrow_full(dve, i, ("rank", j))
                    wait(dve, "count_done", n)
                    step.link(dve.tensor_tensor(place[:, :], ps[0:Q, 0:E], k["count"][:, :], ALU.add))
                    done(dve.tensor_tensor(k["count"][:, :], ps[0:Q, E:2 * E], k["count"][:, :], ALU.add),
                         "count_done")
                    step.link(dve.tensor_tensor(hots[:, :, 0:E], hot[:, :, 0:E],
                                                place[:, :].unsqueeze(1).broadcast_to([Q, TOPK, E]), ALU.mult))
                    step.link(dve.tensor_reduce(r8[:, 6, :], hots[:, :, 0:E], AX, ALU.add))
                    step.done(dve.scalar_tensor_tensor(r8[:, 7, :], r8[:, 0, :], float(CAP), r8[:, 6, :], ALU.mult,
                                                       ALU.add))
                    step.link(dve.tensor_scalar(r8[:, 5, :], r8[:, 6, :], float(CAP), float(4 * NE * CAP), ALU.is_ge,
                                                ALU.mult))
                    done(dve.tensor_tensor(slot[:, j, :], r8[:, 7, :], r8[:, 5, :], ALU.add), "entry_done")
                    step.link(dve.tensor_scalar(k["token"][:, :], k["token"][:, :], float(Q), None, ALU.add))

            with dve.Fori(0, BATCH) as i:
                step.loop(i, DVE_STEPS)
                dve.wait_ge(hin_in, 16 * i + 16)
                for j in range(CH):
                    step.done(dve.bn_stats(stats[:, j, :], hin[:, j, :]))
                step.wait()
                hold()
                for j in range(CH):
                    step.done(dve.bn_aggr(mv[:, j, :], stats[:, j, :]))
                step.wait()
                done(dve.tensor_scalar(var_e[:, :], mv[:, :, 1], EPS, None, ALU.add), "var1")
                wait(dve, "rstd1", i + 1)
                for j in range(CH):
                    done(dve.tensor_scalar(xn[:, j, :], hin[:, j, :], mv[:, j, 0:1], rstd[:, j:j + 1], ALU.subtract,
                                           ALU.mult), "xn_done")

                def conv_taps(n):
                    m = conv_order()[n]
                    ps = wait_narrow_full(dve, i, ("conv", m))
                    wait(dve, "base", CONV_TILES * i + n + 1)
                    for tap in (2, 1, 0):
                        late = 3 - tap
                        acc = cacc[n % 2][:, late:SEQ]
                        ins_ = dve.scalar_tensor_tensor(acc, ps[:, 0:SEQ - late], k["conv_w"][:, m, tap:tap + 1], acc,
                                                        ALU.mult, ALU.add)
                        if tap:
                            step.link(ins_)
                        else:
                            done(ins_, "tapped")

                def conv_silu(n):
                    m = conv_order()[n]
                    wait(dve, "tanhed", CONV_TILES * i + n + 1)
                    done(dve.scalar_tensor_tensor(xbcT[:, m, :], cth[n % 2][:, :], 1.0, cacc[n % 2][:, :], ALU.add,
                                                  ALU.mult), "conv_done")

                u, m, e, w, ln, t = (sp[:, n] for n in range(6))
                heads3 = [Q, CH, HEADS]
                ps = wait_narrow_full(dve, i, ("dt", 0))
                done(dve.tensor_tensor(u, ps[0:Q, 0:CH * HEADS].rearrange("p (j h) -> p j h", j=CH),
                                       k["dt_bias"][:, :].unsqueeze(1).broadcast_to(heads3), ALU.add), "dt_read")
                wait(dve, "dt_read", i + 1)
                step.link(dve.tensor_scalar(t, u, -1.0, None, ALU.mult))
                done(dve.tensor_tensor(m, t, u, ALU.min), "sp_m")
                wait(dve, "exp_m", i + 1)
                done(dve.tensor_scalar(w, e, 1.0, None, ALU.add), "one_plus")
                wait(dve, "logged", i + 1)
                step.done(dve.tensor_scalar(w, w, -1.0, TINY, ALU.add, ALU.add))
                step.link(dve.tensor_scalar(ln, ln, TINY, None, ALU.add))
                step.done(dve.reciprocal(m, w))
                step.link(dve.tensor_tensor(ln, ln, e, ALU.mult))
                step.done(dve.tensor_scalar(u, u, 0.0, None, ALU.max))
                step.link(dve.tensor_tensor(ln, ln, m, ALU.mult))
                step.link(dve.tensor_tensor(dt[:, :, :], u, ln, ALU.add))
                step.link(dve.tensor_tensor(t, dt[:, :, :], k["neg_a"][:, :].unsqueeze(1).broadcast_to(heads3),
                                            ALU.mult))
                step.done(dve.tensor_scalar(a[:, :, :], t, FLOOR, None, ALU.max))
                halves = t.rearrange("p j h -> p (j h)").rearrange("p (n h) -> p n h", h=HH)
                done(dve.tensor_scalar(a3[:, :, :, :], halves.unsqueeze(2).broadcast_to([Q, 2 * CH, 3, HH]), FLOOR,
                                       None, ALU.max), "a_done")
                conv_taps(0)
                for n in range(1, CONV_TILES):
                    conv_taps(n)
                    conv_silu(n - 1)
                conv_silu(CONV_TILES - 1)
                for j in range(CH):
                    ps = wait_narrow_full(dve, i, ("cum", j))
                    wait(dve, "cum_exp", CH * i + j + 1)
                    full = ps[0:3 * HH, 0:2 * Q]
                    hi = parts[:, j, :]
                    step.link(dve.tensor_copy(hi, full))
                    step.link(dve.tensor_tensor(rest[:, 0, :], full, hi, ALU.subtract))
                    step.link(dve.tensor_copy(mid[:, :], rest[:, 0, :]))
                    step.link(dve.tensor_tensor(rest[:, 1, :], rest[:, 0, :], mid[:, :], ALU.subtract))
                    step.done(dve.tensor_copy(parts[HH:2 * HH, j, :], mid[HH:2 * HH, :]))
                    done(dve.tensor_copy(parts[2 * HH:3 * HH, j, :], rest[2 * HH:3 * HH, 1, :]), "parts_done")
                for j in range(CH):
                    n = CH * i + j
                    ps = wait_narrow_full(dve, i, ("cb", j))
                    if j < CH - 1:
                        step.done(dve.tensor_copy(brow[:, j, :], ps[0:Q, P:P + NST]))
                    done(dve.tensor_tensor(cbm[:, j, :], ps[0:Q, 0:Q], k["upto"][:, :], ALU.mult), "cbm_done")
                    wait_wide_full(dve, i, ("z", j))
                    wait(dve, "z_tanh", n + 1)
                    wait(dve, "gg_done", n)
                    done(dve.scalar_tensor_tensor(zs[:, :], zt[:, :], 1.0, wide[0:Q, :], ALU.add, ALU.mult),
                         "zs_done")
                    if j:
                        wait_wide_full(dve, i, ("inter", j))
                        done(dve.tensor_tensor(heads(yint[:, :]), heads(wide[0:Q, :]), spread(grow[:, j, :]), ALU.mult),
                             "yint_done")
                    if j < CH - 1:
                        wait_wide_full(dve, i, ("state", j))
                        if j == 0:
                            ins_ = dve.tensor_copy(state[:, 0, :], wide[:, :])
                        else:
                            wait(dve, "kept_done", i + 1)
                            ins_ = dve.tensor_tensor(state[:, 1, :], kept[:, :], wide[:, :], ALU.add)
                        done(ins_, "state_done")
                    wait(dve, "cbm_done", n + 1)
                    for g in range(GROUPS):
                        q = GROUPS * j + g
                        wait(dve, "lx_done", CH * GROUPS * i + q + 1)
                        dve.wait_ge(ev["y_heads"], CH * GROUPS * i + max(q - 2, 0) + 1)
                        ins_ = dve.scalar_tensor_tensor(m_[q % 3][:, :, :], lx[q % 2][:, :, :], 1.0,
                                                        cbm[:, j, :].unsqueeze(1).broadcast_to([Q, HG, Q]),
                                                        ALU.min, ALU.mult)
                        done(ins_, "m_done")
                        if j and g in PIECES:
                            tail(i, j - 1, PIECES[g])
                    wait(dve, "y_heads", CH * GROUPS * i + GROUPS * (j + 1))
                    wait(dve, "skip_sum" if j else "skip_done", 2 * i + j if j else n + 1)
                    if j:
                        wait(dve, "gg_done", n)
                    done(dve.tensor_tensor(y[:, :], skip[:, :], ysum[0:Q, :], ALU.add), "y_done")
                for piece in PIECES.values():
                    tail(i, CH - 1, piece)
                step.end(BATCH)




def experts(nc, k, ins, dram):
    with ExitStack() as ctx:
        def sb(name, shape, dt=F32):
            return [ctx.enter_context(nc.sbuf_tensor(f"{name}{n}", shape, dt)) for n in range(2)]

        def pb(name):
            return [ctx.enter_context(nc.psum_tensor(f"{name}{n}", [P, 512], F32)) for n in range(2)]

        def sem(name):
            return ctx.enter_context(nc.semaphore(name))

        TILES, KF, ROWS = CAP // P, FI // P, CAP
        wgu, wd = sb("wgu", [P, KD, 2 * FI]), sb("wd", [P, KF, DM])
        tab = sb("tab", [P, TILES, 2])
        gather_at, add_at = sb("gather_at", [P, TILES], U32), sb("add_at", [P, TILES], U32)
        weight = sb("weight", [P, TILES])
        rows, rowsT = sb("rows", [P, TILES, DM]), sb("rowsT", [P, KD, ROWS])
        th, gated, actT = sb("th", [P, KF, ROWS]), sb("gated", [P, KF, ROWS]), sb("actT", [P, KF, ROWS])
        ye = sb("ye", [P, TILES, DM])
        idle = ctx.enter_context(nc.sbuf_tensor("idle2", [P, 4], F32))
        turn_ps, gate_ps, up_ps, down_ps = pb("turn_ps"), pb("gate_ps"), pb("up_ps"), pb("down_ps")

        names = ["turned", "rowsT_done", "converted", "gu_done", "th_done", "act_done", "down_done", "y_out",
                 "earlier_added"]
        ev = {n: sem("e_" + n) for n in names}
        weights_in = [sem(f"weights_in{n}") for n in range(2)]
        tab_in = [sem(f"tab_in{n}") for n in range(2)]
        gathered = [sem(f"gathered{n}") for n in range(2)]
        added, half_turned = sem("added"), sem("half_turned")
        gated_step = sem("gated_step")

        with nc.Block() as first:
            @first.gpsimd
            def _(pool):
                for s in ev.values():
                    pool.sem_inc(s, 1)
                pool.memset(idle[:, :], 0.0).then_inc(gated_step, 1)

        block = ctx.enter_context(nc.Block())

        def wait(eng, name, n):
            eng.wait_ge(ev[name], n + 1)

        @block.sync
        def _(sp):
            def load(i, u):
                n = 2 * i + u
                sp.dma_start(tab[u][:, :, :], dram["slots"].rearrange("(e p t) c -> e p t c", p=P, t=TILES)[n]
                             ).then_inc(tab_in[u], 16)
                sp.dma_start(wgu[u][:, :, :], ins["L0_ffn_w_gate_up"][n].rearrange("(c p) f -> p c f", p=P)
                             ).then_inc(weights_in[u], 16)
                sp.dma_start(wd[u][:, :, :], ins["L0_ffn_w_down"][n].rearrange("(c p) f -> p c f", p=P)
                             ).then_inc(weights_in[u], 16)

            for u in range(2):
                load(0, u)
            with sp.Fori(1, E // 2) as i:
                for u in range(2):
                    wait(sp, "converted", 2 * i + u - 1)
                    wait(sp, "down_done", 2 * i + u - 1)
                    load(i, u)

        @block.gpsimd
        def _(pool):
            step = Steps(pool, sem("idled"))

            def take_waits():
                step.wait()
                step.done(pool.tensor_tensor(idle[:, 0:1], idle[:, 1:2], idle[:, 1:2], ALU.mult))

            def gather(i, u):
                wait(pool, "converted", 2 * i + u + 1)
                wait(pool, "turned", 2 * i + u - 1 if not isinstance(i, int) or i else 0)
                take_waits()
                for t in range(TILES):
                    pool.indirect_dma_start(
                        out=rows[u][:, t, :], out_offset=None, in_=dram["x2"],
                        in_offset=bass.IndirectOffsetOnAxis(ap=gather_at[u][:, t:t + 1], axis=0)
                    ).then_inc(gathered[u], 16)

            def add(i, u):
                n = 2 * i + u
                for t in range(TILES):
                    if t == 0:
                        wait(pool, "y_out", n + 1)
                    if t or u or not isinstance(i, int) or i:
                        pool.wait_ge(added, 16 * (TILES * n + t) if t or u else 32 * n)
                    take_waits()
                    if t == 0:
                        pool.sem_inc(ev["earlier_added"], 1)
                    pool.indirect_dma_start(
                        out=dram["acc"], out_offset=bass.IndirectOffsetOnAxis(ap=add_at[u][:, t:t + 1], axis=0),
                        in_=ye[u][:, t, :], in_offset=None, compute_op=ALU.add
                    ).then_inc(added, 16)

            pool.wait_ge(gated_step, 1)
            pool.sem_inc(step.sem, 1)
            step.n = 1
            gather(0, 0)
            gather(0, 1)
            for u in range(2):
                add(0, u)
                gather(1, u)
            with pool.Fori(1, E // 2 - 1) as i:
                step.loop(i - 1, 2 * (TILES + 1))
                for u in range(2):
                    add(i, u)
                    gather(i + 1, u)
                step.end(E // 2 - 2)
            for u in range(2):
                add(E // 2 - 1, u)
            pool.wait_ge(added, 16 * TILES * E)

        @block.tensor
        def _(pe):
            def turn(i, u):
                pe.wait_ge(gathered[u], 32 * i + 32)
                for t in range(TILES):
                    wait(pe, "rowsT_done", 2 * TILES * i + TILES * u + t - 1 if t or u or not isinstance(i, int) or i else 0)
                    for c in range(KD):
                        last = pe.transpose(turn_ps[t][:, c * P:(c + 1) * P], rows[u][:, t, c * P:(c + 1) * P],
                                            k["ident"][:, :])
                    if t == TILES - 1:
                        last.then_inc(ev["turned"], 1)
                    else:
                        last.then_inc(half_turned, 1)

            def body(i, u, more):
                n = 2 * i + u
                pe.wait_ge(weights_in[u], 32 * i + 32)
                wait(pe, "rowsT_done", TILES * n + TILES)
                wait(pe, "act_done", n - 1 if u or not isinstance(i, int) or i else 0)
                for ps, col in ((gate_ps[u], 0), (up_ps[u], FI)):
                    for f in range(KF):
                        for c in range(KD):
                            last = pe.matmul(ps[:, f * ROWS:(f + 1) * ROWS], wgu[u][:, c, col + f * P:col + (f + 1) * P],
                                             rowsT[u][:, c, :], start=(c == 0), stop=(c == KD - 1))
                last.then_inc(ev["gu_done"], 1)
                if more:
                    turn(i + u, 1 - u)
                wait(pe, "act_done", n + 1)
                wait(pe, "y_out", n)
                for t in range(TILES):
                    for f in range(KF):
                        last = pe.matmul(down_ps[t][:, :], actT[u][:, f, t * P:(t + 1) * P], wd[u][:, f, :],
                                         start=(f == 0), stop=(f == KF - 1))
                last.then_inc(ev["down_done"], 1)

            pe.wait_ge(gated_step, 1)
            turn(0, 0)
            for u in range(2):
                body(0, u, True)
            with pe.Fori(1, E // 2 - 1) as i:
                for u in range(2):
                    body(i, u, True)
            body(E // 2 - 1, 0, True)
            body(E // 2 - 1, 1, False)

        @block.scalar
        def _(act):
            def turned(i, u):
                n = 2 * i + u
                for t in range(TILES):
                    if t == TILES - 1:
                        wait(act, "turned", n + 1)
                    else:
                        act.wait_ge(half_turned, n + 1)
                        wait(act, "gu_done", n - 1 if not isinstance(i, int) or i else 0)
                    act.activation(rowsT[u][:, :, t * P:(t + 1) * P], turn_ps[t][:, :].rearrange("p (c q) -> p c q", c=KD),
                                   ACT.Copy).then_inc(ev["rowsT_done"], 1)

            def body(i, u, more):
                n = 2 * i + u
                wait(act, "gu_done", n + 1)
                wait(act, "act_done", n - 1 if not isinstance(i, int) or i else 0)
                act.activation(th[u][:, :, :].rearrange("p f q -> p (f q)"), gate_ps[u][:, :], ACT.Tanh, scale=0.5
                               ).then_inc(ev["th_done"], 1)
                if more:
                    turned(i + u, 1 - u)

            turned(0, 0)
            for u in range(2):
                body(0, u, True)
            with act.Fori(1, E // 2 - 1) as i:
                for u in range(2):
                    body(i, u, True)
            body(E // 2 - 1, 0, True)
            body(E // 2 - 1, 1, False)

        @block.vector
        def _(dve):
            def convert(i, u):
                dve.wait_ge(tab_in[u], 16 * i + 16)
                dve.tensor_copy(gather_at[u][:, :], tab[u][:, :, 0])
                dve.tensor_scalar(weight[u][:, :], tab[u][:, :, 1], 0.5, None, ALU.mult).then_inc(ev["converted"], 1)

            def body(i, u):
                n = 2 * i + u
                wait(dve, "th_done", n + 1)
                wait(dve, "down_done", n - 1 if not isinstance(i, int) or i else 0)
                dve.scalar_tensor_tensor(gated[u][:, :, :].rearrange("p f q -> p (f q)"),
                                         th[u][:, :, :].rearrange("p f q -> p (f q)"), 1.0, gate_ps[u][:, :],
                                         ALU.add, ALU.mult).then_inc(gated_step, 1)
                dve.wait_ge(gated_step, n + 2)
                dve.tensor_tensor(actT[u][:, :, :].rearrange("p f q -> p (f q)"),
                                  gated[u][:, :, :].rearrange("p f q -> p (f q)"), up_ps[u][:, :], ALU.mult
                                  ).then_inc(ev["act_done"], 1)
                wait(dve, "down_done", n + 1)
                wait(dve, "earlier_added", n)
                wait(dve, "converted", n + 1)
                dve.tensor_copy(add_at[u][:, :], gather_at[u][:, :])
                for t in range(TILES):
                    last = dve.tensor_scalar(ye[u][:, t, :], down_ps[t][:, :], weight[u][:, t:t + 1], None, ALU.mult)
                last.then_inc(ev["y_out"], 1)

            for u in range(2):
                convert(0, u)
            with dve.Fori(0, E // 2 - 1) as i:
                for u in range(2):
                    body(i, u)
                    wait(dve, "y_out", 2 * i + u + 1)
                    convert(i + 1, u)
            for u in range(2):
                body(E // 2 - 1, u)


def load_projections(nc, k, ins):
    with (
        nc.sbuf_tensor("gain_w", [P, INTER // P], F32) as gain,
        nc.semaphore("w_in_loaded") as in_loaded,
        nc.semaphore("w_out_loaded") as out_loaded,
        nc.Block() as block,
    ):
        @block.sync
        def _(sp):
            sp.dma_start(k["w_out"][:, :, :],
                         ins["L0_attn_out_proj_w"].rearrange("(m p) d -> p m d", p=P)).then_inc(out_loaded, 16)
            with nc.allow_non_contiguous_dma(reason="a small per-channel vector"):
                sp.dma_start(gain[:, :],
                             ins["L0_attn_norm_w"].rearrange("(m p) -> p m", p=P)).then_inc(out_loaded, 16)
            sp.dma_start(k["w_in"][:, :, :],
                         ins["L0_attn_in_proj_w"].rearrange("(m p) d -> p m d", p=P)).then_inc(in_loaded, 16)
            sp.wait_ge(in_loaded, 16)

        @block.vector
        def _(dve):
            dve.wait_ge(out_loaded, 32)
            for m in range(INTER // P):
                dve.tensor_scalar(k["w_out"][:, m, :], k["w_out"][:, m, :], gain[:, m:m + 1], None, ALU.mult)


def finish(nc, dram, out):
    with nc.semaphore("out_done") as out_done, nc.Block() as block:
        @block.sync
        def _(sp):
            sp.dma_start(out.rearrange("c s d -> (c s) d"), dram["acc"][0:TOK, :]).then_inc(out_done, 16)
            sp.wait_ge(out_done, 16)


_INS = ["x", "txt", "L0_tok_log_dt", "L0_tok_B_ri", "L0_tok_inv_A_real", "L0_tok_A_imag", "L0_attn_in_proj_w",
        "L0_attn_conv_w", "L0_attn_conv_b", "L0_attn_A_log", "L0_attn_D", "L0_attn_dt_bias", "L0_attn_norm_w",
        "L0_attn_out_proj_w", "L0_ffn_w_cls", "L0_ffn_bias", "L0_ffn_w_gate_up", "L0_ffn_w_down"]


def build(nc, ins, out):
    with ExitStack() as ctx:
        def sb(name, shape, dt=F32):
            return ctx.enter_context(nc.sbuf_tensor(name, shape, dt))

        dram = {
            "h": nc.dram_tensor("h", (BATCH, SEQ, DM), F32).ap(),
            "x2": nc.dram_tensor("x2", (TOK + CAP, DM), F32).ap(),
            "acc": nc.dram_tensor("acc", (TOK + CAP, DM), F32).ap(),
            "slots": nc.dram_tensor("slots", (SLOTS, 2), F32).ap(),
        }
        k = {
            "ident": sb("ident", [P, P]),
            "upto": sb("upto", [Q, Q]),
            "after": sb("after", [Q, Q]),
            "before": sb("before", [Q, Q]),
            "ones": sb("ones", [Q, P]),
            "half_power": sb("half_power", [P, 4]),
            "far": sb("far", [Q, Q], BF16),
            "ident16": sb("ident16", [P, P], BF16),
            "pick": sb("pick", [3 * HH, HH], BF16),
            "unpick": sb("unpick", [3 * HH, HH], BF16),
            "token": sb("token", [Q, 1]),
            "numbers": sb("numbers", [Q, NE]),
            "count": sb("count", [Q, E]),
            "conv_w": sb("conv_w", [P, CONV_TILES, 4]),
            "conv_b": sb("conv_b", [P, CONV_TILES]),
            "neg_a": sb("neg_a", [Q, HEADS]),
            "skip_d": sb("skip_d", [Q, HEADS]),
            "dt_bias": sb("dt_bias", [Q, HEADS]),
            "top_bias": sb("top_bias", [Q, NE]),
            "w_cls": sb("w_cls", [P, KD, NE]),
        }
        make_constants(nc, k, ins, dram)
        s4d_rows(nc, k, ins, dram)
        with ExitStack() as c2:
            k["w_in"] = c2.enter_context(nc.sbuf_tensor("w_in", [P, KD, PROJ], F32))
            k["w_out"] = c2.enter_context(nc.sbuf_tensor("w_out", [P, INTER // P, DM], F32))
            load_projections(nc, k, ins)
            sequences(nc, k, ins, dram)
        experts(nc, k, ins, dram)
        finish(nc, dram, out)


def kernel(**inputs):
    import numpy as _np
    import concourse.bacc as _bacc
    from concourse import mybir as _mybir
    from concourse.bass_utils import run_bass_kernel_spmd as _run

    nc = _bacc.Bacc("TRN2", target_bir_lowering=False, num_devices=1)
    arrays, args = {}, {}
    for name in _INS:
        a = _np.ascontiguousarray(inputs[name])
        arrays[f"in_{name}_dram"] = a
        args[name] = nc.dram_tensor(f"in_{name}_dram", a.shape, _mybir.dt.from_np(a.dtype), kind="ExternalInput").ap()
    out = nc.dram_tensor("out_0_dram", (BATCH, SEQ, DM), F32, kind="ExternalOutput").ap()
    build(nc, args, out)
    r = _run(nc, [arrays], core_ids=[0])
    return r.results[0]["out_0_dram"]
```

```python
from contextlib import ExitStack

import concourse.bass as bass
from concourse import mybir

ALU = mybir.AluOpType
ACT = mybir.ActivationFunctionType
AX = mybir.AxisListType.X
F32 = mybir.dt.float32
BF16 = mybir.dt.bfloat16
U32 = mybir.dt.uint32

BATCH, SSM_H, SSM_N = 16, 256, 64
TXT = 77
SEQ = SSM_H + TXT
DM = 512
P = 128
KD = DM // P
PAIRS = SSM_H // 2
BLK = DM // P
LOW = P
LOG = LOW.bit_length() - 1
GRP = 16
HEADS, HD, NST = 64, 16, 128
INTER = HEADS * HD
CONV_TILES = (INTER + 2 * NST) // P
B_TILE, C_TILE = INTER // P, INTER // P + 1
XBC0 = INTER
DT0 = 2 * INTER + 2 * NST
PROJ = DT0 + HEADS
CH = 3
Q = SEQ // CH
HH = HEADS // 2
HG = 4
GROUPS = HEADS // HG
E, NE, TOPK, CAP, FI = 32, 64, 8, 256, 256
TOK = BATCH * SEQ
SLOTS = E * CAP
EPS = 1e-5
FLOOR = -120.0
TINY = 1e-30

CHAIN = CH * GROUPS
LX, MX = 3, 4


def conv_order():
    return [B_TILE, C_TILE] + list(range(B_TILE))


def make_plan():
    plan = {eng: [[] for _ in range(CHAIN)] for eng in ("pe", "act", "dve", "pool")}

    def at(slot, eng, *names, n=0):
        turn, slot = divmod(slot, CHAIN)
        for name in names:
            plan[eng][slot].append((name, n, -turn))

    def ahead(slot, eng, *names, n=0):
        at(slot - CHAIN, eng, *names, n=n)

    for q in range(CHAIN):
        at(q - 4, "pe", "decay", n=q)
        at(q - 3, "act", "heads", n=q)
        at(q - 2, "dve", "heads", n=q)
        at(q, "pe", "heads", n=q)
    s = GROUPS
    ahead(s + 9, "dve", "norm_sums")
    ahead(s + 10, "dve", "norm_var")
    ahead(s + 11, "pool", "norm_rstd")
    s = 2 * GROUPS
    for j in range(CH):
        ahead(s - 4 + j, "dve", "norm", n=j)
        ahead(s + 2 + j, "pe", "xnT", n=j)
        ahead(s + 2 + j, "act", "xnT", n=j)
    ahead(s + 5, "pe", "dt")
    ahead(s + 5, "dve", "dt_sum")
    ahead(s + 6, "act", "dt_exp")
    ahead(s + 6, "dve", "dt_plus")
    ahead(s + 7, "act", "dt_log")
    ahead(s + 7, "dve", "dt_rest")
    ahead(s + 8, "dve", "dt_end")
    for n in range(CONV_TILES):
        slot = s + 5 + (n + 1) // 2
        ahead(slot, "pe", "conv", n=n)
        ahead(slot, "act", "conv", n=n)
        ahead(slot, "dve", "conv", n=n)
    ahead(s + 10, "act", "conv", n=CONV_TILES)
    ahead(s + 10, "dve", "conv", n=CONV_TILES)
    for j, slot in enumerate((s + 9, s + 11, s + 14)):
        ahead(slot, "pe", "cum", n=j)
        ahead(slot, "act", "cum", n=j)
        ahead(slot + 1, "dve", "cum", n=j)
    for j in range(CH):
        s = (j - 1) * GROUPS
        late = 4 if j == 0 else 0
        at(s + 8 + late, "pe", "cb", n=j)
        at(s + 9 + late, "dve", "cb", n=j)
        at(s + 9 + late, "pe", "xrow", n=j)
        at(s + 10 + late, "act", "xrow", n=j)
        at(s + 11 + late, "pool", "dtx", n=j)
        if j < CH - 1:
            if j:
                at(s + 8, "pool", "kept")
            at(s + 12 + min(late, 3), "pool", "dtxf", n=j)
            at(s + (GROUPS + 4 if j == 0 else 13), "pe", "state", n=j)
            at(s + (GROUPS + 5 if j == 0 else 14), "dve", "state", n=j)
    for j in range(CH):
        s = j * GROUPS
        at(s, "pe", "z", n=j)
        at(s + 1, "act", "z", n=j)
        at(s + 2, "dve", "z", n=j)
        at(s + 3, "pool", "skip", n=j)
        if j:
            at(s + 4, "pe", "inter", n=j)
            at(s + 5, "dve", "inter", n=j)
            at(s + 6, "pool", "skip_sum", n=j)
    for j in range(CH):
        s = (j + 1) * GROUPS
        at(s, "pool", "gate", n=j)
        at(s, "act", "squares", n=j)
        at(s + 1, "dve", "out_var", n=j)
        at(s + 1, "pool", "out_rstd", n=j)
        at(s + 6, "pe", "gT", n=j)
        at(s + 7, "act", "gT", n=j)
        at(s + 8, "pe", "out", n=j)
        at(s + 9, "dve", "out", n=j)
        at(s + 9, "pool", "x2_rstd", n=j)
        at(s + 10, "dve", "x2", n=j)
        at(s + 11, "act", "stores", n=j)
        at(s + 11, "pe", "x2T", n=j)
        at(s + 12, "act", "x2T", n=j)
        at(s + 13, "pe", "logits", n=j)
        at(s + 14, "dve", "largest", n=j)
        at(s + 15, "act", "logits", n=j)
        s += GROUPS
        at(s, "dve", "choices", n=j)
        at(s + 3, "pe", "rank", n=j)
        at(s + 4, "dve", "rank", n=j)
        at(s + 8, "dve", "weights", n=j)
        at(s + (10 if j == 0 else 12), "pool", "scatter", n=j)
    order = {"pe": {"decay": -1, "heads": 1}, "act": {"heads": -1}, "dve": {"heads": -2, "out": -1, "cum": -1}}
    for q in range(CHAIN):
        for eng in order:
            plan[eng][q].sort(key=lambda step: order[eng].get(step[0], 0))
        if q % GROUPS == GROUPS - 1:
            plan["dve"][q].append(("y", q // GROUPS, 0))
    return plan


PLAN = make_plan()
NARROW_USES = ("xnT", "dt", "conv", "cum", "cb", "out", "x2T", "logits", "rank")
WIDE_USES = ("z", "inter", "gT", "xrow", "state")
NARROW = [step for steps in PLAN["pe"] for step in steps if step[0] in NARROW_USES]
WIDE = [step for steps in PLAN["pe"] for step in steps if step[0] in WIDE_USES]
TIMES = {"dt": 1, "conv": CONV_TILES, "inter": CH - 1, "state": CH - 1}
READ = {"xnT": ["xnT_done"], "dt": ["dt_read"], "conv": ["tapped"], "cum": ["cum_exp", "parts_done"],
        "cb": ["cbm_done"], "out": ["h2_done"], "x2T": ["x2T_done"], "logits": ["exped"], "rank": ["count_done"],
        "xrow": ["xrow_done"], "z": ["zs_done"], "inter": ["yint_done"], "state": ["state_done"],
        "gT": ["ggT_done"]}


def turns(eng, steps, plan, stage, loop_start=None, loop_end=None):
    def turn(b, offsets, before):
        stage["now"], stage["before"] = offsets, before
        for slot in plan:
            for name, n, offset in slot:
                if offset in offsets:
                    steps[name](b + offset, n)

    turn(-1, (1,), ())
    turn(0, (0, 1), (1,))
    with eng.Fori(1, BATCH - 1) as b:
        if loop_start:
            loop_start(b - 1)
        turn(b, (-1, 0, 1), (0, 1))
        if loop_end:
            loop_end(BATCH - 2)
    turn(BATCH - 1, (-1, 0), (-1, 0, 1))
    turn(BATCH, (-1,), (-1, 0))


class Steps:

    def __init__(self, eng, sem):
        self.eng, self.sem, self.base, self.n = eng, sem, 0, 0

    def done(self, ins):
        ins.then_inc(self.sem, 1)
        self.n += 1
        return self.n

    def wait(self, n=None):
        self.eng.wait_ge(self.sem, self.base + (self.n if n is None else n))

    def link(self, ins):
        self.done(ins)
        self.wait()

    def loop(self, i, per):
        self.before, self.per = self.n, per
        self.base, self.n = self.n + i * per, 0

    def end(self, turns):
        assert self.n == self.per, ("steps of a turn:", self.n)
        self.base, self.n = 0, self.before + turns * self.per


def bc(ap, shape):
    return ap.broadcast_to(shape)


def make_constants(nc, k, ins, dram):
    with ExitStack() as ctx:
        made = ctx.enter_context(nc.semaphore("made"))
        loaded = ctx.enter_context(nc.semaphore("loaded"))
        cls_loaded = ctx.enter_context(nc.semaphore("cls_loaded"))
        turned = ctx.enter_context(nc.semaphore("turned"))
        dve_step = ctx.enter_context(nc.semaphore("dve_step"))
        act_step = ctx.enter_context(nc.semaphore("act_step"))
        stored = ctx.enter_context(nc.semaphore("stored"))
        wcls = ctx.enter_context(nc.sbuf_tensor("wcls", [NE, DM], F32))
        zero = ctx.enter_context(nc.sbuf_tensor("zero", [P, 2 * DM], F32))
        empty = ctx.enter_context(nc.sbuf_tensor("empty", [P, 2, 2], F32))
        clsT = ctx.enter_context(nc.psum_tensor("clsT", [P, KD, NE], F32))
        block = ctx.enter_context(nc.Block())

        @block.sync
        def _(sp):
            sp.dma_start(wcls[:, :], ins["L0_ffn_w_cls"]).then_inc(cls_loaded, 16)
            with nc.allow_non_contiguous_dma(reason="small per-channel vectors"):
                sp.dma_start(k["conv_w"][:, :, :],
                             ins["L0_attn_conv_w"].rearrange("(m p) t -> p m t", p=P)).then_inc(loaded, 16)
                sp.dma_start(k["conv_b"][:, :],
                             ins["L0_attn_conv_b"].rearrange("(m p) -> p m", p=P)).then_inc(loaded, 16)
            for name, key, width in (("L0_attn_A_log", "neg_a", HEADS), ("L0_attn_D", "skip_d", HEADS),
                                     ("L0_attn_dt_bias", "dt_bias", HEADS), ("L0_ffn_bias", "top_bias", NE)):
                sp.dma_start(k[key][:, :], ins[name].unsqueeze(0).broadcast_to([Q, width])).then_inc(loaded, 16)
            sp.dma_start(dram["h"][:, SSM_H:SEQ, :], ins["txt"]).then_inc(stored, 16)
            sp.wait_ge(made, 1)
            sp.dma_start(dram["slots"].rearrange("(e p t) c -> p e (t c)", p=P, t=2),
                         empty[:, :, :].rearrange("p t c -> p (t c)").unsqueeze(1).broadcast_to([P, E, 4])
                         ).then_inc(stored, 16)
            for name in ("x2", "acc"):
                sp.dma_start(dram[name][TOK:TOK + CAP, :].rearrange("(p t) d -> p (t d)", t=2),
                             zero[:, :]).then_inc(stored, 16)
            sp.wait_ge(stored, 64)

        @block.gpsimd
        def _(pool):
            step = Steps(pool, ctx.enter_context(nc.semaphore("pool_step")))
            step.done(pool.memset(zero[:, :], 0.0))
            step.done(pool.memset(empty[:, :, :], 0.0))
            step.done(pool.memset(k["ident"][:, :], 0.0))
            step.done(pool.memset(k["upto"][:, :], 1.0))
            step.done(pool.memset(k["after"][:, :], 1.0))
            step.done(pool.memset(k["before"][:, :], 1.0))
            step.done(pool.memset(k["ones"][:, :], 1.0))
            step.done(pool.memset(k["half_power"][:, :], -0.5))
            step.done(pool.memset(k["pick"][:, :], 0.0))
            step.done(pool.memset(k["far"][:, :], 0.0))
            step.done(pool.memset(k["ident16"][:, :], 0.0))
            step.done(pool.memset(k["count"][:, :], 0.0))
            step.done(pool.iota(k["token"][:, :], pattern=[[0, 1]], base=0, channel_multiplier=1,
                                allow_small_or_imprecise_dtypes=True))
            step.done(pool.iota(k["numbers"][:, :], pattern=[[1, NE]], base=0, channel_multiplier=0,
                                allow_small_or_imprecise_dtypes=True))
            step.wait()
            step.done(pool.iota(empty[:, :, 0], pattern=[[1, 2]], base=TOK, channel_multiplier=2,
                                allow_small_or_imprecise_dtypes=True))
            step.done(pool.affine_select(out=k["ident"][:, :], in_=k["ident"][:, :], compare_op=ALU.not_equal,
                                         fill=1.0, base=0, pattern=[[-1, P]], channel_multiplier=1))
            step.done(pool.affine_select(out=k["upto"][:, :], in_=k["upto"][:, :], compare_op=ALU.is_ge,
                                         fill=0.0, base=0, pattern=[[1, Q]], channel_multiplier=-1))
            step.done(pool.affine_select(out=k["after"][:, :], in_=k["after"][:, :], compare_op=ALU.is_gt,
                                         fill=0.0, base=0, pattern=[[-1, Q]], channel_multiplier=1))
            step.done(pool.affine_select(out=k["before"][:, :], in_=k["before"][:, :], compare_op=ALU.is_gt,
                                         fill=0.0, base=0, pattern=[[1, Q]], channel_multiplier=-1))
            step.done(pool.affine_select(out=k["far"][:, :], in_=k["far"][:, :], compare_op=ALU.is_ge,
                                         fill=-16384.0, base=0, pattern=[[1, Q]], channel_multiplier=-1))
            step.done(pool.affine_select(out=k["ident16"][:, :], in_=k["ident16"][:, :], compare_op=ALU.not_equal,
                                         fill=1.0, base=0, pattern=[[-1, P]], channel_multiplier=1))
            for part in range(3):
                step.link(pool.affine_select(out=k["pick"][:, :], in_=k["pick"][:, :], compare_op=ALU.not_equal,
                                             fill=1.0, base=-HH * part, pattern=[[-1, HH]], channel_multiplier=1))
            step.link(pool.tensor_scalar(k["unpick"][:, :], k["pick"][:, :], -1.0, None, ALU.mult))
            pool.sem_inc(made, 1)

        @block.tensor
        def _(pe):
            pe.wait_ge(made, 1)
            pe.wait_ge(cls_loaded, 16)
            for c in range(KD):
                last = pe.transpose(clsT[:, c, :], wcls[:, c * P:(c + 1) * P], k["ident"][0:NE, 0:NE])
            last.then_inc(turned, 1)

        @block.vector
        def _(dve):
            step = Steps(dve, dve_step)
            dve.wait_ge(turned, 1)
            step.done(dve.tensor_copy(k["w_cls"][:, :, :], clsT[:, :, :]))
            dve.wait_ge(loaded, 6 * 16)
            step.done(dve.tensor_scalar(k["conv_w"][:, :, :], k["conv_w"][:, :, :], 0.25, None, ALU.mult))
            step.done(dve.tensor_scalar(k["conv_b"][:, :], k["conv_b"][:, :], 0.5, None, ALU.mult))
            dve.wait_ge(act_step, 1)
            step.link(dve.tensor_scalar(k["neg_a"][:, :], k["neg_a"][:, :], -1.0, None, ALU.mult))

        @block.scalar
        def _(act):
            act.wait_ge(loaded, 6 * 16)
            act.activation(k["neg_a"][:, :], k["neg_a"][:, :], ACT.Exp).then_inc(act_step, 1)


def s4d_rows(nc, k, ins, dram):
    with ExitStack() as ctx:
        def sb(name, shape, dt=F32):
            return ctx.enter_context(nc.sbuf_tensor(name, shape, dt))

        def sem(name):
            return ctx.enter_context(nc.semaphore(name))

        inv_a = sb("inv_a", [PAIRS, P])
        a_im = sb("a_im", [PAIRS, P])
        b_ri = sb("b_ri", [PAIRS, P, 2])
        log_dt = sb("log_dt", [PAIRS, 2])
        half_dt = sb("half_dt", [PAIRS, 2])
        two_dt = sb("two_dt", [PAIRS, 2])
        scratch = sb("scratch", [PAIRS, 8, P])
        rows = sb("rows", [PAIRS, 4, P])
        power = sb("power", [P, LOG + 3, 2, PAIRS])
        gain = sb("gain", [P, 2, PAIRS])
        crow = sb("crow", [PAIRS, 2, 2 * P])
        cT = sb("cT", [P, 2, BATCH, PAIRS])
        x = sb("x", [P, 2, BLK, BATCH, PAIRS])
        xt = [sb(f"xt{n}", [P, BATCH, PAIRS]) for n in range(2)]
        v = [sb(f"v{n}", [P, 2, GRP, LOW]) for n in range(2)]
        vt = sb("vt", [P, 4, GRP, LOW // 2])
        xd = sb("xd", [P, 2, GRP, 2, BLK * BATCH])
        kout = sb("kout", [P, GRP, LOW])
        ptab = ctx.enter_context(nc.psum_tensor("ptab", [P, 4, P], F32))
        pct = [ctx.enter_context(nc.psum_tensor(f"pct{n}", [P, 4, P], F32)) for n in range(2)]
        pk = [ctx.enter_context(nc.psum_tensor(f"pk{n}", [P, 4, P], F32)) for n in range(4)]

        params_in = sem("params_in")
        c_in = [sem(f"c_in{n}") for n in range(2)]
        dve_step, pool_step, act_step = sem("dve_step"), sem("pool_step"), sem("act_step")
        exps = sem("exps")
        rows_ready, tab_turned, tab_ready = sem("rows_ready"), sem("tab_turned"), sem("tab_ready")
        c_turned, c_copied = sem("c_turned"), sem("c_copied")
        x_re, x_im = sem("x_re"), sem("x_im")
        v_re, v_im = sem("v_re"), sem("v_im")
        xd_ready, prod_done, k_copied = sem("xd_ready"), sem("prod_done"), sem("k_copied")
        k_stored, kout_free = sem("k_stored"), sem("kout_free")
        cleared = sem("cleared")
        NG = PAIRS // GRP
        block = ctx.enter_context(nc.Block())

        @block.sync
        def _(sp):
            sp.dma_start(inv_a[:, :], ins["L0_tok_inv_A_real"].rearrange("(p r) n -> p (r n)", r=2)).then_inc(params_in, 16)
            sp.dma_start(a_im[:, :], ins["L0_tok_A_imag"].rearrange("(p r) n -> p (r n)", r=2)).then_inc(params_in, 16)
            sp.dma_start(b_ri[:, :, :], ins["L0_tok_B_ri"].rearrange("(p r) n i -> p (r n) i", r=2)).then_inc(params_in, 16)
            sp.dma_start(log_dt[:, :], ins["L0_tok_log_dt"].rearrange("(p r) -> p r", r=2)).then_inc(params_in, 16)
            for c in range(BATCH):
                if c >= 2:
                    sp.wait_ge(c_turned, c - 1)
                sp.dma_start(crow[:, c % 2, :], ins["x"][c].rearrange("(p r) n i -> p (r n i)", r=2)
                             ).then_inc(c_in[c % 2], 16)
            with sp.Fori(0, NG) as g:
                sp.wait_ge(k_copied, 4 * g + 5)
                for r in range(2):
                    for a in range(BLK):
                        lo = (r * BLK + a) * BATCH
                        dst = dram["h"][:, 0:SSM_H, a * P:(a + 1) * P].rearrange(
                            "c (p r) b -> c r p b", r=2)[:, r, bass.ds(g * GRP, GRP), :]
                        sp.dma_start(dst, kout[lo:lo + BATCH, :, :]).then_inc(k_stored, 16)
                sp.wait_ge(k_stored, 16 * 2 * BLK * g + 16 * 2 * BLK)
                sp.sem_inc(kout_free, 1)

        @block.scalar
        def _(act):
            act.wait_ge(params_in, 64)
            act.activation(half_dt[:, :], log_dt[:, :], ACT.Exp).then_inc(exps, 1)
            act.activation(inv_a[:, :], inv_a[:, :], ACT.Exp).then_inc(exps, 1)
            act.wait_ge(tab_turned, 1)
            act.activation(power[:, 0, :, :], ptab[:, 0:2, :], ACT.Copy).then_inc(tab_ready, 1)
            act.activation(gain[:, :, :], ptab[:, 2:4, :], ACT.Copy).then_inc(tab_ready, 1)
            for c in range(BATCH):
                act.wait_ge(c_turned, c + 1)
                act.activation(cT[:, :, c, :], pct[c % 2][:, 0:2, :], ACT.Copy).then_inc(c_copied, 1)
            act.wait_ge(cleared, 1)
            act.wait_ge(x_re, 1)
            act.wait_ge(x_im, 1)
            with act.Fori(0, NG) as g:
                act.wait_ge(prod_done, 4 * g + 1)
                for r in range(2):
                    half = slice(r * SSM_N, (r + 1) * SSM_N)
                    for i in range(2):
                        act.activation(xd[half, i, :, r, :],
                                       x[half, i, :, :, bass.ds(g * GRP, GRP)].rearrange("p a c q -> p q (a c)"),
                                       ACT.Copy, scale=-1.0 if i else 1.0).then_inc(xd_ready, 1)
                act.wait_ge(kout_free, g + 1)
                for b in range(4):
                    act.wait_ge(prod_done, 4 * g + b + 2)
                    act.activation(kout[:, 4 * b:4 * b + 4, :], pk[b][:, :, :], ACT.Copy).then_inc(k_copied, 1)

        @block.tensor
        def _(pe):
            pe.sem_inc(prod_done, 1)
            pe.sem_inc(k_copied, 1)
            pe.sem_inc(kout_free, 1)
            pe.wait_ge(rows_ready, 1)
            for n in range(4):
                last = pe.transpose(ptab[:, n, :], rows[:, n, :], k["ident"][:, :])
            last.then_inc(tab_turned, 1)
            for c in range(BATCH):
                pe.wait_ge(c_in[c % 2], 16 * (c // 2 + 1))
                if c >= 2:
                    pe.wait_ge(c_copied, c - 1)
                for i in range(2):
                    last = pe.transpose(pct[c % 2][:, i, :], crow[:, c % 2, i:2 * P:2], k["ident"][:, :])
                last.then_inc(c_turned, 1)
            with pe.Fori(0, NG // 2) as gg:
                for u in range(2):
                    pe.wait_ge(xd_ready, 8 * gg + 4 * u + 4)
                    pe.wait_ge(v_re, 2 * LOG * gg + LOG * (u + 1) + 1)
                    pe.wait_ge(v_im, 2 * LOG * gg + LOG * (u + 1) + 1)
                    for b in range(4):
                        pe.wait_ge(k_copied, 8 * gg + 4 * u + 1)
                        for q in range(4):
                            pair = 4 * b + q
                            for i in range(2):
                                last = pe.matmul(pk[b][:, q, :], xd[:, i, pair, :, :].rearrange("p r m -> p (r m)"),
                                                 v[u][:, i, pair, :], start=(i == 0), stop=(i == 1))
                        last.then_inc(prod_done, 1)

        def times(eng, out, xr, xi, pr, pi, step, imaginary, t1, t2):
            step.done(eng.tensor_tensor(t1, xr, pi if imaginary else pr, ALU.mult))
            step.link(eng.tensor_tensor(t2, xi, pr if imaginary else pi, ALU.mult))
            return eng.tensor_tensor(out, t1, t2, ALU.add if imaginary else ALU.subtract)

        x_part = [sem("x_part_re"), sem("x_part_im")]
        pow_re, pow_im = sem("pow_re"), sem("pow_im")
        pw = [pow_re, pow_im]
        vs = [v_re, v_im]
        cleared_v = sem("cleared_v")

        def part_of(eng, part, step, spare):
            im = part == 1
            pt = sb(f"pt{part}", [P, 2, PAIRS])
            eng.wait_ge(tab_ready, 2)
            for n in range(LOG):
                if n:
                    eng.wait_ge(pow_re, n)
                    eng.wait_ge(pow_im, n)
                re, imag = power[:, n, 0, :], power[:, n, 1, :]
                times(eng, power[:, n + 1, part, :], re, imag, re, imag, step, im, pt[:, 0, :], pt[:, 1, :]
                      ).then_inc(pw[part], 1)
            eng.wait_ge(pow_re, LOG)
            eng.wait_ge(pow_im, LOG)
            eng.wait_ge(c_copied, BATCH)
            shape = [P, BATCH, PAIRS]
            for a in range(BLK):
                if a == 0:
                    xr, xi, pr, pi = cT[:, 0], cT[:, 1], gain[:, 0, :], gain[:, 1, :]
                else:
                    xr, xi = x[:, 0, a - 1], x[:, 1, a - 1]
                    pr, pi = power[:, LOG, 0, :], power[:, LOG, 1, :]
                    eng.wait_ge(x_part[0], a)
                    eng.wait_ge(x_part[1], a)
                times(eng, x[:, part, a], xr, xi, bc(pr.unsqueeze(1), shape), bc(pi.unsqueeze(1), shape), step, im,
                      xt[part][:, :, :], spare).then_inc(x_part[part], 1)
            eng.wait_ge(x_part[0], BLK)
            eng.wait_ge(x_part[1], BLK)
            eng.sem_inc(x_im if im else x_re, 1)
            for u in range(2):
                step.done(eng.memset(v[u][:, part, :, 0:1], 0.0 if im else 1.0))
            step.wait()
            eng.sem_inc(cleared_v, 1)
            eng.sem_inc(vs[part], 1)
            eng.wait_ge(cleared_v, 2)
            with eng.Fori(0, NG // 2) as gg:
                step.loop(gg, 2 * 2 * LOG)
                for u in range(2):
                    eng.wait_ge(prod_done, 8 * gg + 1)
                    for n in range(LOG):
                        w = 1 << n
                        done = 2 * LOG * gg + LOG * u + n + 1
                        eng.wait_ge(v_re, done)
                        eng.wait_ge(v_im, done)
                        shape_v = [P, GRP, w]
                        pr, pi = (power[:, n, i, bass.ds(gg * 2 * GRP + u * GRP, GRP)].unsqueeze(2).broadcast_to(shape_v)
                                  for i in range(2))
                        times(eng, v[u][:, part, :, w:2 * w], v[u][:, 0, :, 0:w], v[u][:, 1, :, 0:w], pr, pi, step, im,
                              vt[:, 2 * part, :, 0:w], vt[:, 2 * part + 1, :, 0:w]).then_inc(vs[part], 1)
                step.end(NG // 2)

        @block.gpsimd
        def _(pool):
            step = Steps(pool, pool_step)
            step.link(pool.memset(xd[:, :, :, :, :], 0.0))
            pool.sem_inc(cleared, 1)
            part_of(pool, 1, step, v[1][:, :, :, :].rearrange("p i q b -> p (i q b)")[:, 0:BATCH * PAIRS]
                    .rearrange("p (c q) -> p c q", c=BATCH))

        @block.vector
        def _(dve):
            step = Steps(dve, dve_step)
            t = [scratch[:, n, :] for n in range(8)]
            two = lambda ap: ap.rearrange("p (r n) -> p r n", r=2)
            dve.wait_ge(exps, 2)
            step.done(dve.tensor_scalar(two_dt[:, :], half_dt[:, :], 2.0, None, ALU.mult))
            step.link(dve.tensor_scalar(half_dt[:, :], half_dt[:, :], 0.5, None, ALU.mult))
            hd, td = (bc(z[:, :].unsqueeze(2), [PAIRS, 2, SSM_N]) for z in (half_dt, two_dt))
            step.done(dve.tensor_tensor(two(t[0]), two(inv_a[:, :]), hd, ALU.mult))
            step.link(dve.tensor_tensor(two(t[1]), two(a_im[:, :]), hd, ALU.mult))
            step.done(dve.tensor_scalar(t[2], t[0], 1.0, None, ALU.add))
            step.done(dve.tensor_scalar(t[3], t[0], -1.0, 1.0, ALU.mult, ALU.add))
            step.link(dve.tensor_tensor(t[4], t[1], t[1], ALU.mult))
            step.link(dve.tensor_tensor(t[5], t[2], t[2], ALU.mult))
            step.link(dve.tensor_tensor(t[5], t[5], t[4], ALU.add))
            step.link(dve.reciprocal(t[6], t[5]))
            step.link(dve.tensor_tensor(t[7], t[3], t[2], ALU.mult))
            step.link(dve.tensor_tensor(t[7], t[7], t[4], ALU.subtract))
            step.done(dve.tensor_tensor(rows[:, 0, :], t[7], t[6], ALU.mult))
            step.done(dve.scalar_tensor_tensor(rows[:, 1, :], t[1], 2.0, t[6], ALU.mult, ALU.mult))
            dve.wait_ge(params_in, 64)
            br, bi = b_ri[:, :, 0], b_ri[:, :, 1]
            step.done(dve.tensor_tensor(t[0], br, t[2], ALU.mult))
            step.done(dve.tensor_tensor(t[3], bi, t[1], ALU.mult))
            step.done(dve.tensor_tensor(t[4], bi, t[2], ALU.mult))
            step.link(dve.tensor_tensor(t[5], br, t[1], ALU.mult))
            step.done(dve.tensor_tensor(t[0], t[0], t[3], ALU.subtract))
            step.done(dve.tensor_tensor(t[4], t[4], t[5], ALU.add))
            step.link(dve.tensor_tensor(two(t[6]), two(t[6]), td, ALU.mult))
            step.done(dve.tensor_tensor(rows[:, 2, :], t[0], t[6], ALU.mult))
            step.link(dve.tensor_tensor(rows[:, 3, :], t[4], t[6], ALU.mult))
            dve.sem_inc(rows_ready, 1)
            part_of(dve, 0, step, v[0][:, :, :, :].rearrange("p i q b -> p (i q b)")[:, 0:BATCH * PAIRS]
                    .rearrange("p (c q) -> p c q", c=BATCH))


DVE_STEPS = 143


def sequences(nc, k, ins, dram):
    with ExitStack() as ctx:
        def sb(name, shape, dt=F32):
            return ctx.enter_context(nc.sbuf_tensor(name, shape, dt))

        def pb(name):
            return ctx.enter_context(nc.psum_tensor(name, [P, 512], F32))

        def sem(name):
            return ctx.enter_context(nc.semaphore(name))

        w_in = k["w_in"]
        hin = sb("hin", [Q, CH, DM])
        hres = sb("hres", [Q, CH, DM])
        stats = sb("stats", [Q, CH, 6])
        mv = sb("mv", [Q, CH, 2])
        var_e = sb("var_e", [Q, CH])
        rstd = sb("rstd", [Q, CH])
        xnT = sb("xnT", [P, KD, SEQ])
        sp = sb("sp", [Q, 6, CH, HEADS])
        dt = sb("dt", [Q, CH, HEADS])
        a = sb("a", [Q, CH, HEADS])
        a3 = sb("a3", [Q, 2 * CH, 3, HH])
        cacc = [sb(f"cacc{n}", [P, SEQ]) for n in range(3)]
        cth = [sb(f"cth{n}", [P, SEQ]) for n in range(2)]
        xbcT = sb("xbcT", [P, CONV_TILES, SEQ])
        parts = sb("parts", [3 * HH, CH, 2 * Q], BF16)
        mid = sb("mid", [3 * HH, 2 * Q], BF16)
        rest = sb("rest", [3 * HH, 2, 2 * Q])
        grow = sb("grow", [Q, CH, HEADS])
        fall = sb("fall", [Q, CH, HEADS])
        total = sb("total", [P, CH, HEADS])
        xrow = sb("xrow", [Q, INTER])
        zt = sb("zt", [Q, INTER])
        zs = sb("zs", [Q, INTER])
        cbm = sb("cbm", [Q, CH, Q])
        brow = sb("brow", [Q, 2, NST])
        dtx = sb("dtx", [Q, CH, INTER])
        dtxf = sb("dtxf", [Q, INTER])
        skip = sb("skip", [Q, INTER])
        yint = sb("yint", [Q, INTER])
        state = sb("state", [P, 2, INTER])
        kept = sb("kept", [P, INTER])
        lx = [sb(f"lx{n}", [Q, HG, Q]) for n in range(LX)]
        m_ = [sb(f"m{n}", [Q, HG, Q]) for n in range(MX)]
        y = sb("y", [Q, INTER])
        gg = sb("gg", [Q, INTER])
        ggT = sb("ggT", [P, INTER // P, Q])
        ss = sb("ss", [Q, CH])
        h2 = sb("h2", [Q, CH, DM])
        x2 = sb("x2s", [Q, CH, DM])
        x2T = sb("x2T", [P, KD, Q])
        stat2 = sb("stat2", [Q, 6])
        mv2 = sb("mv2", [Q, 2])
        small = sb("small", [Q, 12])
        ex = sb("ex", [Q, NE])
        score = sb("score", [Q, NE])
        biased = sb("biased", [Q, NE])
        top = sb("top", [Q, TOPK])
        topi = sb("topi", [Q, TOPK], U32)
        r8 = sb("r8", [Q, 8, TOPK])
        hot = sb("hot", [Q, TOPK, NE])
        hots = sb("hots", [Q, TOPK, NE])
        sel = sb("sel", [Q, E])
        place = sb("place", [Q, E])
        entry = sb("entry", [Q, CH, TOPK, 2])
        slot = sb("slot", [Q, CH, TOPK], U32)
        idle = sb("idle", [Q, 4])
        credit = sb("credit", [Q, CH + 1, 2])

        nar = [pb(f"nar{n}") for n in range(2)]
        dec = [pb(f"dec{n}") for n in range(2)]
        wide = ctx.enter_context(nc.psum_tensor("wide", [P, 1024], F32))
        ysum = ctx.enter_context(nc.psum_tensor("ysum", [P, 1024], F32))

        names = ["xn_done", "xnT_done", "hres_used", "var1", "rstd1", "exp_m", "one_plus", "logged",
                 "sp_m", "a_done", "base", "tanhed", "conv_done", "tapped", "cum_exp", "parts_done", "cbm_done",
                 "xrow_done", "z_tanh", "zs_done", "dtx_done", "dtxf_done", "skip_done", "yint_done",
                 "skip_sum", "state_done", "kept_done", "lx_done", "m_done", "y_heads", "y_full", "y_done",
                 "gg_done", "gg_turned", "sq_done", "ggT_done", "var_y", "rstd_y", "h2_done", "var2", "rstd2", "x2_done",
                 "x2T_done", "neg_max", "exped", "sel_done", "entry_done", "dt_read", "count_done", "idled"]
        ev = {n: sem(n) for n in names}
        full = {n: sem(n + "_full") for n in NARROW_USES + WIDE_USES}
        dec_full = [sem(f"dec_full{n}") for n in range(2)]
        entry_free = sem("entry_free")
        hin_in, hres_in = sem("hin_in"), sem("hres_in")
        stored = [sem(f"stored{j}") for j in range(CH)]
        scattered = sem("scattered")
        dve_step = sem("b_dve_step")
        act_step = sem("b_act_step")

        with nc.Block() as first:
            @first.gpsimd
            def _(pool):
                for s in list(ev.values()) + list(full.values()) + dec_full:
                    pool.sem_inc(s, 1)
                pool.sem_inc(entry_free, 2)
                pool.sem_inc(dve_step, 1)
                pool.dma_start(credit[:, CH, :], dram["x2"][TOK:TOK + Q, 0:2]).then_inc(scattered, 16)
                pool.wait_ge(scattered, 16)

            @first.sync
            def _(sy):
                for j in range(CH):
                    sy.dma_start(credit[:, j, :], dram["x2"][TOK:TOK + Q, 0:2]).then_inc(stored[j], 16)
                    sy.wait_ge(stored[j], 16)

        block = ctx.enter_context(nc.Block())

        def wait(eng, name, n):
            if isinstance(n, int) and n < 0:
                return
            eng.wait_ge(ev[name], n + 1)

        def number(kind, t, n):
            return TIMES.get(kind, CH) * t + n + (0 if kind == "inter" else 1)

        def wait_full(eng, kind, t, n):
            eng.wait_ge(full[kind], number(kind, t, n) + 1)

        def bank(kind, n):
            return nar[[step[:2] for step in NARROW].index((kind, n)) % 2]

        def chunk(j):
            return slice(j * Q, (j + 1) * Q)

        @block.sync
        def _(sy):
            with sy.Fori(0, BATCH) as i:
                sy.wait_ge(full["xnT"], CH * i + 1)
                sy.dma_start(hin[:, :, :], dram["h"][i].rearrange("(j p) d -> p j d", p=Q)).then_inc(hin_in, 16)
                wait(sy, "h2_done", CH * i)
                sy.dma_start(hres[:, :, :], dram["h"][i].rearrange("(j p) d -> p j d", p=Q)).then_inc(hres_in, 16)
            for j in range(CH):
                sy.wait_ge(stored[j], 16 + 32 * BATCH)

        @block.tensor
        def _(pe):
            stage = {}

            def take(kind, t, n):
                uses, banks = (NARROW, 2) if kind in NARROW_USES else (WIDE, 1)
                at = [step[:2] for step in uses].index((kind, n))
                turn = t - uses[at][2]
                was, there = at - banks, stage["now"]
                while was >= -len(uses):
                    if was < 0:
                        there = stage["before"]
                    if uses[was][2] in there:
                        kind, n, offset = uses[was]
                        turn = (turn if was >= 0 else turn - 1) + offset
                        for event in READ[kind]:
                            wait(pe, event, number(kind, turn, n))
                        return
                    was -= banks

            def take_narrow(kind, t, n):
                take(kind, t, n)
                return bank(kind, n)

            def xnT_(t, j):
                wait(pe, "xn_done", CH * t + j + 1)
                ps = take_narrow("xnT", t, j)
                for c in range(KD):
                    last = pe.transpose(ps[:, c * Q:(c + 1) * Q], hin[:, j, c * P:(c + 1) * P], k["ident"][0:Q, 0:Q])
                last.then_inc(full["xnT"], 1)

            def dt_(t, _n):
                ps = take_narrow("dt", t, 0)
                wait(pe, "xnT_done", CH * t + CH)
                for j in range(CH):
                    for c in range(KD):
                        last = pe.matmul(ps[0:Q, j * HEADS:(j + 1) * HEADS], xnT[:, c, chunk(j)],
                                         w_in[:, c, DT0:PROJ], start=(c == 0), stop=(c == KD - 1))
                last.then_inc(full["dt"], 1)

            def conv_(t, n):
                m = conv_order()[n]
                ps = take_narrow("conv", t, n)
                for c in range(KD):
                    last = pe.matmul(ps[:, 0:SEQ], w_in[:, c, XBC0 + m * P:XBC0 + (m + 1) * P], xnT[:, c, :],
                                     start=(c == 0), stop=(c == KD - 1))
                last.then_inc(full["conv"], 1)

            def cum_(t, j):
                ps = take_narrow("cum", t, j)
                wait(pe, "a_done", t + 1)
                for half in range(2):
                    pe.matmul(ps[0:3 * HH, half * Q:(half + 1) * Q],
                              a3[:, 2 * j + half, :, :].rearrange("p r h -> p (r h)"), k["upto"][:, :],
                              start=True, stop=True)
                o = 2 * Q
                pe.matmul(ps[0:Q, o:o + HEADS], k["upto"][:, :], a[:, j, :], start=True, stop=True)
                pe.matmul(ps[0:Q, o + HEADS:o + 2 * HEADS], k["after"][:, :], a[:, j, :], start=True, stop=True)
                pe.matmul(ps[:, o + 2 * HEADS:o + 3 * HEADS], k["ones"][:, :], a[:, j, :], start=True, stop=True
                          ).then_inc(full["cum"], 1)

            def cb_(t, j):
                ps = take_narrow("cb", t, j)
                wait(pe, "conv_done", CONV_TILES * t + 2)
                last = pe.matmul(ps[0:Q, 0:Q], xbcT[:, B_TILE, chunk(j)], xbcT[:, C_TILE, chunk(j)],
                                 start=True, stop=True)
                if j < CH - 1:
                    last = pe.transpose(ps[0:Q, P:P + NST], xbcT[:, B_TILE, chunk(j)], k["ident"][:, :])
                last.then_inc(full["cb"], 1)

            def xrow_(t, j):
                take("xrow", t, j)
                wait(pe, "conv_done", CONV_TILES * (t + 1))
                for m in range(B_TILE):
                    last = pe.transpose(wide[0:Q, m * P:(m + 1) * P], xbcT[:, m, chunk(j)], k["ident"][:, :])
                last.then_inc(full["xrow"], 1)

            def z_(t, j):
                take("z", t, j)
                for half in range(2):
                    for c in range(KD):
                        last = pe.matmul(wide[0:Q, half * 512:(half + 1) * 512], xnT[:, c, chunk(j)],
                                         w_in[:, c, half * 512:(half + 1) * 512], start=(c == 0), stop=(c == KD - 1))
                last.then_inc(full["z"], 1)

            def inter_(t, j):
                take("inter", t, j)
                wait(pe, "state_done", 2 * t + j)
                for half in range(2):
                    last = pe.matmul(wide[0:Q, half * 512:(half + 1) * 512], xbcT[:, C_TILE, chunk(j)],
                                     state[:, j - 1, half * 512:(half + 1) * 512], start=True, stop=True)
                last.then_inc(full["inter"], 1)

            def state_(t, j):
                take("state", t, j)
                wait(pe, "dtxf_done", 2 * t + j + 1)
                wait(pe, "cbm_done", CH * t + j + 1)
                for half in range(2):
                    last = pe.matmul(wide[:, half * 512:(half + 1) * 512], brow[:, j, :],
                                     dtxf[:, half * 512:(half + 1) * 512], start=True, stop=True)
                last.then_inc(full["state"], 1)

            def decay_(t, q):
                j, g = divmod(q, GROUPS)
                b = q % 2
                if g == 0:
                    wait(pe, "parts_done", CH * t + j + 1)
                wait(pe, "lx_done", CHAIN * t + q - 1)
                half, h0 = divmod(g * HG, HH)
                cum = parts[:, j, half * Q:(half + 1) * Q]
                pe.matmul(dec[b][0:Q, 0:HG * Q], cum,
                          k["unpick"][:, h0:h0 + HG].unsqueeze(2).broadcast_to([3 * HH, HG, Q]),
                          start=True, stop=False, skip_group_check=True)
                pe.matmul(dec[b][0:Q, 0:HG * Q], k["ident16"][0:Q, 0:Q],
                          k["far"][:, :].unsqueeze(1).broadcast_to([Q, HG, Q]),
                          start=False, stop=False, skip_group_check=True)
                for n in range(HG):
                    last = pe.matmul(dec[b][0:Q, n * Q:(n + 1) * Q],
                                     k["pick"][:, h0 + n:h0 + n + 1].broadcast_to([3 * HH, Q]),
                                     cum, start=False, stop=(n == HG - 1), skip_group_check=True)
                last.then_inc(dec_full[b], 1)

            def heads_(t, q):
                j, g = divmod(q, GROUPS)
                if g == 0:
                    wait(pe, "dtx_done", CH * t + j + 1)
                    wait(pe, "y_done", CH * t + j)
                wait(pe, "m_done", CHAIN * t + q + 1)
                for n in range(HG):
                    h = g * HG + n
                    last = pe.matmul(ysum[0:Q, h * HD:(h + 1) * HD], m_[q % MX][:, n, :],
                                     dtx[:, j, h * HD:(h + 1) * HD], start=True, stop=True)
                last.then_inc(ev["y_heads"], 1)

            def gT_(t, j):
                wait(pe, "gg_done", CH * t + j + 1)
                take("gT", t, j)
                for f in range(INTER // P):
                    last = pe.transpose(wide[:, (f // 4) * 512 + (f % 4) * Q:(f // 4) * 512 + (f % 4 + 1) * Q],
                                        gg[:, f * P:(f + 1) * P], k["ident"][0:Q, 0:Q])
                last.then_inc(full["gT"], 1)

            def out_(t, j):
                ps = take_narrow("out", t, j)
                wait(pe, "ggT_done", CH * t + j + 1)
                for f in range(INTER // P):
                    last = pe.matmul(ps[0:Q, :], ggT[:, f, :], k["w_out"][:, f, :], start=(f == 0),
                                     stop=(f == INTER // P - 1))
                last.then_inc(full["out"], 1)

            def x2T_(t, j):
                wait(pe, "x2_done", CH * t + j + 1)
                ps = take_narrow("x2T", t, j)
                for c in range(KD):
                    last = pe.transpose(ps[:, c * Q:(c + 1) * Q], x2[:, j, c * P:(c + 1) * P], k["ident"][0:Q, 0:Q])
                last.then_inc(full["x2T"], 1)

            def logits_(t, j):
                wait(pe, "x2T_done", CH * t + j + 1)
                ps = take_narrow("logits", t, j)
                for c in range(KD):
                    last = pe.matmul(ps[0:Q, 0:NE], x2T[:, c, :], k["w_cls"][:, c, :], start=(c == 0),
                                     stop=(c == KD - 1))
                last.then_inc(full["logits"], 1)

            def rank_(t, j):
                wait(pe, "sel_done", CH * t + j + 1)
                ps = take_narrow("rank", t, j)
                pe.matmul(ps[0:Q, 0:E], k["before"][:, :], sel[:, :], start=True, stop=True)
                pe.matmul(ps[0:Q, E:2 * E], k["ones"][:, 0:Q], sel[:, :], start=True, stop=True
                          ).then_inc(full["rank"], 1)

            turns(pe, {"xnT": xnT_, "dt": dt_, "conv": conv_, "cum": cum_, "cb": cb_, "xrow": xrow_, "z": z_,
                       "inter": inter_, "state": state_, "decay": decay_, "heads": heads_, "gT": gT_, "out": out_,
                       "x2T": x2T_, "logits": logits_, "rank": rank_}, PLAN["pe"], stage)

        @block.scalar
        def _(act):
            def xnT_(t, j):
                wait_full(act, "xnT", t, j)
                act.wait_ge(full["z"], CH * t + 1)
                act.activation(xnT[:, :, chunk(j)], bank("xnT", j)[:, 0:KD * Q].rearrange("p (c q) -> p c q", c=KD),
                               ACT.Copy).then_inc(ev["xnT_done"], 1)

            def dt_exp_(t, _n):
                wait(act, "sp_m", t + 1)
                act.activation(sp[:, 2], sp[:, 1], ACT.Exp).then_inc(ev["exp_m"], 1)

            def dt_log_(t, _n):
                wait(act, "one_plus", t + 1)
                act.activation(sp[:, 4], sp[:, 3], ACT.Ln).then_inc(ev["logged"], 1)

            def conv_(t, n):
                if n < CONV_TILES:
                    m = conv_order()[n]
                    wait_full(act, "conv", t, n)
                    wait(act, "conv_done", CONV_TILES * t + n - 2)
                    act.activation(cacc[n % 3][:, :], bank("conv", n)[:, 0:SEQ], ACT.Identity,
                                   scale=k["conv_w"][:, m, 3:4], bias=k["conv_b"][:, m:m + 1]
                                   ).then_inc(ev["base"], 1)
                if n:
                    wait(act, "tapped", CONV_TILES * t + n)
                    act.activation(cth[(n - 1) % 2][:, :], cacc[(n - 1) % 3][:, :], ACT.Tanh
                                   ).then_inc(ev["tanhed"], 1)

            def cum_(t, j):
                o = 2 * Q
                ps = bank("cum", j)
                wait_full(act, "cum", t, j)
                wait(act, "yint_done", 2 * t)
                act.activation(grow[:, j, :], ps[0:Q, o:o + HEADS], ACT.Exp)
                wait(act, "dtxf_done", 2 * t)
                act.activation(fall[:, j, :], ps[0:Q, o + HEADS:o + 2 * HEADS], ACT.Exp)
                wait(act, "kept_done", t)
                act.activation(total[:, j, :], ps[:, o + 2 * HEADS:o + 3 * HEADS], ACT.Exp
                               ).then_inc(ev["cum_exp"], 1)

            def xrow_(t, j):
                wait_full(act, "xrow", t, j)
                wait(act, "skip_done", CH * t + j)
                act.activation(xrow[:, :], wide[0:Q, :], ACT.Copy).then_inc(ev["xrow_done"], 1)

            def z_(t, j):
                wait_full(act, "z", t, j)
                wait(act, "sq_done", CH * t + j)
                act.activation(zt[:, :], wide[0:Q, :], ACT.Tanh, scale=0.125).then_inc(ev["z_tanh"], 1)

            def heads_(t, q):
                act.wait_ge(dec_full[q % 2], CHAIN // 2 * t + q // 2 + 2)
                wait(act, "m_done", CHAIN * t + q - LX + 1)
                act.activation(lx[q % LX][:, :, :], dec[q % 2][0:Q, 0:HG * Q].rearrange("p (h t) -> p h t", h=HG),
                               ACT.Exp).then_inc(ev["lx_done"], 1)

            def squares_(t, j):
                wait(act, "y_done", CH * t + j + 1)
                act.activation(zt[:, :], y[:, :], ACT.Square, accum_out=ss[:, j:j + 1]).then_inc(ev["sq_done"], 1)

            def gT_(t, j):
                wait_full(act, "gT", t, j)
                wait(act, "h2_done", CH * t + j)
                act.activation(ggT[:, :, :].rearrange("p (u f) q -> p u (f q)", u=2),
                               wide[:, :].rearrange("p (u c) -> p u c", u=2)[:, :, 0:4 * Q], ACT.Copy
                               ).then_inc(ev["ggT_done"], 1)

            def stores_(t, j):
                wait(act, "x2_done", CH * t + j + 1)
                act.dma_start(dram["acc"][0:TOK, :].rearrange("(c j p) d -> c j p d", j=CH, p=Q)[t, j],
                              h2[:, j, :]).then_inc(stored[j], 16)
                act.dma_start(dram["x2"][0:TOK, :].rearrange("(c j p) d -> c j p d", j=CH, p=Q)[t, j],
                              x2[:, j, :]).then_inc(stored[j], 16)

            def x2T_(t, j):
                wait_full(act, "x2T", t, j)
                act.activation(x2T[:, :, :].rearrange("p c q -> p (c q)"), bank("x2T", j)[:, 0:KD * Q], ACT.Copy
                               ).then_inc(ev["x2T_done"], 1)

            def logits_(t, j):
                wait_full(act, "logits", t, j)
                wait(act, "neg_max", CH * t + j + 1)
                act.activation(ex[:, :], bank("logits", j)[0:Q, 0:NE], ACT.Exp, bias=small[:, 0:1],
                               accum_out=small[:, 1:2]).then_inc(ev["exped"], 1)

            turns(act, {"xnT": xnT_, "dt_exp": dt_exp_, "dt_log": dt_log_, "conv": conv_, "cum": cum_, "xrow": xrow_,
                        "z": z_, "heads": heads_, "squares": squares_, "gT": gT_, "stores": stores_, "x2T": x2T_,
                        "logits": logits_}, PLAN["act"], {})

        @block.gpsimd
        def _(pool):
            def heads(ap):
                return ap.rearrange("p (h d) -> p h d", h=HEADS)

            def spread(ap, rows=Q):
                return ap.unsqueeze(2).broadcast_to([rows, HEADS, HD])

            def norm_rstd_(t, _n):
                wait(pool, "var1", t + 1)
                pool.tensor_tensor(rstd[:, :], var_e[:, :], k["half_power"][0:Q, 0:CH], ALU.pow
                                   ).then_inc(ev["rstd1"], 1)

            def dtx_(t, j):
                n = CH * t + j
                wait(pool, "xrow_done", n + 1)
                wait(pool, "a_done", t + 1)
                wait(pool, "y_done", n - 1)
                pool.tensor_tensor(heads(dtx[:, j, :]), heads(xrow[:, :]), spread(dt[:, j, :]), ALU.mult
                                   ).then_inc(ev["dtx_done"], 1)

            def dtxf_(t, j):
                wait(pool, "cum_exp", CH * t + j + 1)
                wait(pool, "dtx_done", CH * t + j + 1)
                wait(pool, "state_done", 2 * t + j)
                pool.tensor_tensor(heads(dtxf[:, :]), heads(dtx[:, j, :]), spread(fall[:, j, :]), ALU.mult
                                   ).then_inc(ev["dtxf_done"], 1)

            def skip_(t, j):
                wait(pool, "y_done", CH * t + j)
                pool.tensor_tensor(heads(skip[:, :]), heads(xrow[:, :]), spread(k["skip_d"][:, :]), ALU.mult
                                   ).then_inc(ev["skip_done"], 1)

            def skip_sum_(t, j):
                wait(pool, "skip_done", CH * t + j + 1)
                wait(pool, "yint_done", 2 * t + j)
                pool.tensor_tensor(skip[:, :], skip[:, :], yint[:, :], ALU.add).then_inc(ev["skip_sum"], 1)

            def kept_(t, _n):
                wait(pool, "state_done", 2 * t + 1)
                wait(pool, "cum_exp", CH * t + 2)
                pool.tensor_tensor(heads(kept[:, :]), heads(state[:, 0, :]), spread(total[:, 1, :], P), ALU.mult
                                   ).then_inc(ev["kept_done"], 1)

            def gate_(t, j):
                wait(pool, "y_done", CH * t + j + 1)
                wait(pool, "zs_done", CH * t + j + 1)
                pool.wait_ge(full["gT"], CH * t + j + 1)
                pool.tensor_tensor(gg[:, :], y[:, :], zs[:, :], ALU.mult).then_inc(ev["gg_done"], 1)

            def out_rstd_(t, j):
                wait(pool, "var_y", CH * t + j + 1)
                pool.tensor_tensor(small[:, 3:4], small[:, 2:3], k["half_power"][0:Q, 0:1], ALU.pow
                                   ).then_inc(ev["rstd_y"], 1)

            def x2_rstd_(t, j):
                wait(pool, "var2", CH * t + j + 1)
                pool.tensor_tensor(small[:, 5:6], small[:, 4:5], k["half_power"][0:Q, 0:1], ALU.pow
                                   ).then_inc(ev["rstd2"], 1)

            def scatter_(t, j):
                n = CH * t + j
                pool.wait_ge(scattered, 16 + 16 * TOPK * n)
                pool.sem_inc(entry_free, 1)
                wait(pool, "idled", n)
                wait(pool, "entry_done", n + 1)
                pool.tensor_tensor(idle[:, 2:3], k["half_power"][0:Q, 0:1], k["half_power"][0:Q, 0:1], ALU.mult
                                   ).then_inc(ev["idled"], 1)
                for c in range(TOPK):
                    pool.indirect_dma_start(
                        out=dram["slots"], out_offset=bass.IndirectOffsetOnAxis(ap=slot[:, j, c:c + 1], axis=0),
                        in_=entry[:, j, c, :], in_offset=None, bounds_check=SLOTS - 1, oob_is_err=False
                    ).then_inc(scattered, 16)

            turns(pool, {"norm_rstd": norm_rstd_, "dtx": dtx_, "dtxf": dtxf_, "skip": skip_, "skip_sum": skip_sum_,
                         "kept": kept_, "gate": gate_, "out_rstd": out_rstd_, "x2_rstd": x2_rstd_,
                         "scatter": scatter_}, PLAN["pool"], {})
            pool.wait_ge(scattered, 16 + 16 * TOPK * CH * BATCH)

        @block.vector
        def _(dve):
            step = Steps(dve, dve_step)
            step.n = 1

            def heads(ap):
                return ap.rearrange("p (h d) -> p h d", h=HEADS)

            def spread(ap):
                return ap.unsqueeze(2).broadcast_to([Q, HEADS, HD])

            def hold():
                dve.memset(idle[:, 0:1], 0.0)

            def done(ins_, name):
                ins_.then_inc(ev[name], 1)

            def norm_sums_(t, _n):
                dve.wait_ge(hin_in, 16 * t + 16)
                for j in range(CH):
                    step.done(dve.bn_stats(stats[:, j, :], hin[:, j, :]))

            def norm_var_(t, _n):
                step.wait()
                hold()
                for j in range(CH):
                    step.done(dve.bn_aggr(mv[:, j, :], stats[:, j, :]))
                step.wait()
                done(dve.tensor_scalar(var_e[:, :], mv[:, :, 1], EPS, None, ALU.add), "var1")

            def norm_(t, j):
                wait(dve, "rstd1", t + 1)
                done(dve.tensor_scalar(hin[:, j, :], hin[:, j, :], mv[:, j, 0:1], rstd[:, j:j + 1], ALU.subtract,
                                       ALU.mult), "xn_done")

            def conv_(t, n):
                if n < CONV_TILES:
                    m = conv_order()[n]
                    wait(dve, "base", CONV_TILES * t + n + 1)
                    for tap in (2, 1, 0):
                        late = 3 - tap
                        acc = cacc[n % 3][:, late:SEQ]
                        ins_ = dve.scalar_tensor_tensor(acc, bank("conv", n)[:, 0:SEQ - late],
                                                        k["conv_w"][:, m, tap:tap + 1], acc, ALU.mult, ALU.add)
                        if tap:
                            step.link(ins_)
                        else:
                            done(ins_, "tapped")
                if n:
                    m = conv_order()[n - 1]
                    wait(dve, "tanhed", CONV_TILES * t + n)
                    if m == C_TILE:
                        dve.wait_ge(full["inter"], 2 * t + 1)
                    else:
                        dve.wait_ge(full["cb" if m == B_TILE else "xrow"], CH * t + 1)
                    done(dve.scalar_tensor_tensor(xbcT[:, m, :], cth[(n - 1) % 2][:, :], 1.0, cacc[(n - 1) % 3][:, :],
                                                  ALU.add, ALU.mult), "conv_done")

            su, sm, se, sw, sl, st = (sp[:, n] for n in range(6))
            heads3 = [Q, CH, HEADS]

            def dt_sum_(t, _n):
                wait_full(dve, "dt", t, 0)
                done(dve.tensor_tensor(su, bank("dt", 0)[0:Q, 0:CH * HEADS].rearrange("p (j h) -> p j h", j=CH),
                                       k["dt_bias"][:, :].unsqueeze(1).broadcast_to(heads3), ALU.add), "dt_read")
                wait(dve, "dt_read", t + 1)
                step.link(dve.tensor_scalar(st, su, -1.0, None, ALU.mult))
                done(dve.tensor_tensor(sm, st, su, ALU.min), "sp_m")

            def dt_plus_(t, _n):
                wait(dve, "exp_m", t + 1)
                done(dve.tensor_scalar(sw, se, 1.0, None, ALU.add), "one_plus")

            def dt_rest_(t, _n):
                wait(dve, "logged", t + 1)
                step.done(dve.tensor_scalar(sw, sw, -1.0, TINY, ALU.add, ALU.add))
                step.link(dve.tensor_scalar(sl, sl, TINY, None, ALU.add))
                step.done(dve.reciprocal(sm, sw))
                step.link(dve.tensor_tensor(sl, sl, se, ALU.mult))
                step.done(dve.tensor_scalar(su, su, 0.0, None, ALU.max))
                step.link(dve.tensor_tensor(sl, sl, sm, ALU.mult))

            def dt_end_(t, _n):
                step.wait()
                wait(dve, "dtx_done", CH * t)
                step.link(dve.tensor_tensor(dt[:, :, :], su, sl, ALU.add))
                step.link(dve.tensor_tensor(st, dt[:, :, :], k["neg_a"][:, :].unsqueeze(1).broadcast_to(heads3),
                                            ALU.mult))
                step.done(dve.tensor_scalar(a[:, :, :], st, FLOOR, None, ALU.max))
                halves = st.rearrange("p j h -> p (j h)").rearrange("p (n h) -> p n h", h=HH)
                done(dve.tensor_scalar(a3[:, :, :, :], halves.unsqueeze(2).broadcast_to([Q, 2 * CH, 3, HH]), FLOOR,
                                       None, ALU.max), "a_done")

            def cum_(t, j):
                wait(dve, "cum_exp", CH * t + j + 1)
                wait(dve, "lx_done", CHAIN * t - CHAIN + GROUPS * (j + 1))
                sums = bank("cum", j)[0:3 * HH, 0:2 * Q]
                step.link(dve.tensor_copy(parts[:, j, :], sums))
                step.link(dve.tensor_tensor(rest[:, 0, :], sums, parts[:, j, :], ALU.subtract))
                step.link(dve.tensor_copy(mid[:, :], rest[:, 0, :]))
                step.link(dve.tensor_tensor(rest[:, 1, :], rest[:, 0, :], mid[:, :], ALU.subtract))
                step.done(dve.tensor_copy(parts[HH:2 * HH, j, :], mid[HH:2 * HH, :]))
                done(dve.tensor_copy(parts[2 * HH:3 * HH, j, :], rest[2 * HH:3 * HH, 1, :]), "parts_done")

            def cb_(t, j):
                wait_full(dve, "cb", t, j)
                ps = bank("cb", j)
                if j < CH - 1:
                    dve.wait_ge(full["state"], 2 * t + 1)
                    step.done(dve.tensor_copy(brow[:, j, :], ps[0:Q, P:P + NST]))
                done(dve.tensor_tensor(cbm[:, j, :], ps[0:Q, 0:Q], k["upto"][:, :], ALU.mult), "cbm_done")

            def z_(t, j):
                wait(dve, "z_tanh", CH * t + j + 1)
                wait(dve, "gg_done", CH * t + j)
                done(dve.scalar_tensor_tensor(zs[:, :], zt[:, :], 1.0, wide[0:Q, :], ALU.add, ALU.mult), "zs_done")

            def inter_(t, j):
                wait_full(dve, "inter", t, j)
                wait(dve, "skip_sum", 2 * t + j - 1)
                done(dve.tensor_tensor(heads(yint[:, :]), heads(wide[0:Q, :]), spread(grow[:, j, :]), ALU.mult),
                     "yint_done")

            def state_(t, j):
                wait_full(dve, "state", t, j)
                dve.wait_ge(full["inter"], 2 * t + 1)
                wait(dve, "kept_done", t + j)
                if j == 0:
                    ins_ = dve.tensor_copy(state[:, 0, :], wide[:, :])
                else:
                    ins_ = dve.tensor_tensor(state[:, 1, :], kept[:, :], wide[:, :], ALU.add)
                done(ins_, "state_done")

            def heads_(t, q):
                j = q // GROUPS
                if q % GROUPS == 0:
                    wait(dve, "cbm_done", CH * t + j + 1)
                wait(dve, "lx_done", CHAIN * t + q + 1)
                wait(dve, "y_heads", CHAIN * t + q - MX + 1)
                done(dve.scalar_tensor_tensor(m_[q % MX][:, :, :], lx[q % LX][:, :, :], 1.0,
                                              cbm[:, j, :].unsqueeze(1).broadcast_to([Q, HG, Q]),
                                              ALU.min, ALU.mult), "m_done")

            def y_(t, j):
                wait(dve, "y_heads", CHAIN * t + GROUPS * (j + 1))
                wait(dve, "skip_sum" if j else "skip_done", 2 * t + j if j else CH * t + 1)
                wait(dve, "gg_done", CH * t + j)
                done(dve.tensor_tensor(y[:, :], skip[:, :], ysum[0:Q, :], ALU.add), "y_done")

            def out_var_(t, j):
                wait(dve, "sq_done", CH * t + j + 1)
                done(dve.tensor_scalar(small[:, 2:3], ss[:, j:j + 1], 1.0 / INTER, EPS, ALU.mult, ALU.add), "var_y")

            def out_(t, j):
                n = CH * t + j
                wait(dve, "rstd_y", n + 1)
                step.link(dve.tensor_scalar(small[:, 6:7], small[:, 3:4], 0.125, None, ALU.mult))
                if j == 0:
                    dve.wait_ge(hres_in, 16 * t + 16)
                dve.wait_ge(stored[j], 32 * t + 16)
                wait_full(dve, "out", t, j)
                done(dve.scalar_tensor_tensor(h2[:, j, :], bank("out", j)[0:Q, :], small[:, 6:7], hres[:, j, :],
                                              ALU.mult, ALU.add), "h2_done")
                wait(dve, "h2_done", n + 1)
                step.link(dve.bn_stats(stat2[:, :], h2[:, j, :]))
                hold()
                step.link(dve.bn_aggr(mv2[:, :], stat2[:, :]))
                done(dve.tensor_scalar(small[:, 4:5], mv2[:, 1:2], EPS, None, ALU.add), "var2")

            def x2_(t, j):
                wait(dve, "rstd2", CH * t + j + 1)
                done(dve.tensor_scalar(x2[:, j, :], h2[:, j, :], mv2[:, 0:1], small[:, 5:6], ALU.subtract, ALU.mult),
                     "x2_done")

            def largest_(t, j):
                wait_full(dve, "logits", t, j)
                step.link(dve.tensor_reduce(small[:, 7:8], bank("logits", j)[0:Q, 0:NE], AX, ALU.max))
                done(dve.tensor_scalar(small[:, 0:1], small[:, 7:8], -1.0, None, ALU.mult), "neg_max")

            def choices_(t, j):
                wait(dve, "exped", CH * t + j + 1)
                step.link(dve.reciprocal(small[:, 8:9], small[:, 1:2]))
                step.done(dve.tensor_scalar(score[:, :], ex[:, :], small[:, 8:9], None, ALU.mult))
                step.link(dve.scalar_tensor_tensor(biased[:, :], ex[:, :], small[:, 8:9], k["top_bias"][:, :],
                                                   ALU.mult, ALU.add))
                hold()
                step.link(dve.max(top[:, :], biased[:, :]))
                hold()
                step.link(dve.max_index(topi[:, :], top[:, :], biased[:, :]))
                step.link(dve.tensor_copy(r8[:, 0, :], topi[:, :]))
                step.link(dve.tensor_tensor(hot[:, :, :],
                                            k["numbers"][:, :].unsqueeze(1).broadcast_to([Q, TOPK, NE]),
                                            r8[:, 0, :].unsqueeze(2).broadcast_to([Q, TOPK, NE]), ALU.is_equal))
                done(dve.tensor_reduce(sel[:, :], hot[:, :, 0:E].rearrange("p c e -> p e c"), AX, ALU.add),
                     "sel_done")

            def weights_(t, j):
                step.link(dve.tensor_tensor(hots[:, :, :], hot[:, :, :],
                                            score[:, :].unsqueeze(1).broadcast_to([Q, TOPK, NE]), ALU.mult))
                step.link(dve.tensor_reduce(r8[:, 1, :], hots[:, :, :], AX, ALU.add))
                step.link(dve.tensor_reduce(small[:, 9:10], r8[:, 1, :], AX, ALU.add))
                step.link(dve.tensor_scalar(small[:, 9:10], small[:, 9:10], 1e-20, None, ALU.add))
                step.link(dve.reciprocal(small[:, 10:11], small[:, 9:10]))
                step.done(dve.tensor_scalar(r8[:, 2, :], r8[:, 1, :], small[:, 10:11], 1.5, ALU.mult, ALU.mult))
                step.link(dve.tensor_scalar(r8[:, 3, :], r8[:, 0, :], float(E), None, ALU.is_lt))
                step.link(dve.tensor_tensor(r8[:, 4, :], r8[:, 2, :], r8[:, 3, :], ALU.mult))
                step.link(dve.tensor_tensor(r8[:, 5, :], r8[:, 2, :], r8[:, 4, :], ALU.subtract))
                step.link(dve.tensor_reduce(small[:, 11:12], r8[:, 5, :], AX, ALU.add))
                step.link(dve.tensor_scalar(small[:, 11:12], small[:, 11:12], 1.0, None, ALU.add))
                step.done(dve.tensor_scalar(entry[:, j, :, 1], r8[:, 4, :], small[:, 11:12], None, ALU.mult))
                step.link(dve.tensor_copy(entry[:, j, :, 0], k["token"][:, 0:1].broadcast_to([Q, TOPK])))
                done(dve.tensor_scalar(k["token"][:, :], k["token"][:, :], float(Q), None, ALU.add), "entry_done")

            def rank_(t, j):
                wait_full(dve, "rank", t, j)
                wait(dve, "count_done", CH * t + j)
                ps = bank("rank", j)
                step.link(dve.tensor_tensor(place[:, :], ps[0:Q, 0:E], k["count"][:, :], ALU.add))
                done(dve.tensor_tensor(k["count"][:, :], ps[0:Q, E:2 * E], k["count"][:, :], ALU.add), "count_done")
                step.link(dve.tensor_tensor(hots[:, :, 0:E], hot[:, :, 0:E],
                                            place[:, :].unsqueeze(1).broadcast_to([Q, TOPK, E]), ALU.mult))
                step.link(dve.tensor_reduce(r8[:, 6, :], hots[:, :, 0:E], AX, ALU.add))
                step.done(dve.scalar_tensor_tensor(r8[:, 7, :], r8[:, 0, :], float(CAP), r8[:, 6, :], ALU.mult,
                                                   ALU.add))
                step.link(dve.tensor_scalar(r8[:, 5, :], r8[:, 6, :], float(CAP), float(4 * NE * CAP), ALU.is_ge,
                                            ALU.mult))
                dve.wait_ge(entry_free, CH * t + j + 1)
                step.done(dve.tensor_tensor(slot[:, j, :], r8[:, 7, :], r8[:, 5, :], ALU.add))

            turns(dve, {"norm_sums": norm_sums_, "norm_var": norm_var_, "norm": norm_, "conv": conv_,
                        "dt_sum": dt_sum_, "dt_plus": dt_plus_, "dt_rest": dt_rest_, "dt_end": dt_end_, "cum": cum_, "cb": cb_, "z": z_,
                        "inter": inter_, "state": state_, "heads": heads_, "y": y_, "out_var": out_var_,
                        "out": out_, "x2": x2_, "largest": largest_, "choices": choices_, "weights": weights_,
                        "rank": rank_}, PLAN["dve"], {}, lambda i: step.loop(i, DVE_STEPS), step.end)


def experts(nc, k, ins, dram):
    with ExitStack() as ctx:
        def sb(name, shape, dt=F32):
            return [ctx.enter_context(nc.sbuf_tensor(f"{name}{n}", shape, dt)) for n in range(2)]

        def pb(name):
            return [ctx.enter_context(nc.psum_tensor(f"{name}{n}", [P, 512], F32)) for n in range(2)]

        def sem(name):
            return ctx.enter_context(nc.semaphore(name))

        TILES, KF, ROWS = CAP // P, FI // P, CAP
        wgu, wd = sb("wgu", [P, KD, 2 * FI]), sb("wd", [P, KF, DM])
        tab = sb("tab", [P, TILES, 2])
        gather_at, add_at = sb("gather_at", [P, TILES], U32), sb("add_at", [P, TILES], U32)
        weight = sb("weight", [P, TILES])
        rows, rowsT = sb("rows", [P, TILES, DM]), sb("rowsT", [P, KD, ROWS])
        th, gated, actT = sb("th", [P, KF, ROWS]), sb("gated", [P, KF, ROWS]), sb("actT", [P, KF, ROWS])
        ye = sb("ye", [P, TILES, DM])
        idle = ctx.enter_context(nc.sbuf_tensor("idle2", [P, 4], F32))
        turn_ps, gate_ps, up_ps, down_ps = pb("turn_ps"), pb("gate_ps"), pb("up_ps"), pb("down_ps")

        names = ["turned", "rowsT_done", "converted", "gu_done", "th_done", "act_done", "down_done", "y_out",
                 "earlier_added"]
        ev = {n: sem("e_" + n) for n in names}
        weights_in = [sem(f"weights_in{n}") for n in range(2)]
        tab_in = [sem(f"tab_in{n}") for n in range(2)]
        gathered = [sem(f"gathered{n}") for n in range(2)]
        added, half_turned = sem("added"), sem("half_turned")
        gated_step = sem("gated_step")

        with nc.Block() as first:
            @first.gpsimd
            def _(pool):
                for s in ev.values():
                    pool.sem_inc(s, 1)
                pool.memset(idle[:, :], 0.0).then_inc(gated_step, 1)

        block = ctx.enter_context(nc.Block())

        def wait(eng, name, n):
            eng.wait_ge(ev[name], n + 1)

        @block.sync
        def _(sp):
            def load(i, u):
                n = 2 * i + u
                sp.dma_start(tab[u][:, :, :], dram["slots"].rearrange("(e p t) c -> e p t c", p=P, t=TILES)[n]
                             ).then_inc(tab_in[u], 16)
                sp.dma_start(wgu[u][:, :, :], ins["L0_ffn_w_gate_up"][n].rearrange("(c p) f -> p c f", p=P)
                             ).then_inc(weights_in[u], 16)
                sp.dma_start(wd[u][:, :, :], ins["L0_ffn_w_down"][n].rearrange("(c p) f -> p c f", p=P)
                             ).then_inc(weights_in[u], 16)

            for u in range(2):
                load(0, u)
            with sp.Fori(1, E // 2) as i:
                for u in range(2):
                    wait(sp, "converted", 2 * i + u - 1)
                    wait(sp, "down_done", 2 * i + u - 1)
                    load(i, u)

        @block.gpsimd
        def _(pool):
            step = Steps(pool, sem("idled"))

            def take_waits():
                step.wait()
                step.done(pool.tensor_tensor(idle[:, 0:1], idle[:, 1:2], idle[:, 1:2], ALU.mult))

            def gather(i, u):
                wait(pool, "converted", 2 * i + u + 1)
                wait(pool, "turned", 2 * i + u - 1 if not isinstance(i, int) or i else 0)
                take_waits()
                for t in range(TILES):
                    pool.indirect_dma_start(
                        out=rows[u][:, t, :], out_offset=None, in_=dram["x2"],
                        in_offset=bass.IndirectOffsetOnAxis(ap=gather_at[u][:, t:t + 1], axis=0)
                    ).then_inc(gathered[u], 16)

            def add(i, u):
                n = 2 * i + u
                for t in range(TILES):
                    if t == 0:
                        wait(pool, "y_out", n + 1)
                    if t or u or not isinstance(i, int) or i:
                        pool.wait_ge(added, 16 * (TILES * n + t) if t or u else 32 * n)
                    take_waits()
                    if t == 0:
                        pool.sem_inc(ev["earlier_added"], 1)
                    pool.indirect_dma_start(
                        out=dram["acc"], out_offset=bass.IndirectOffsetOnAxis(ap=add_at[u][:, t:t + 1], axis=0),
                        in_=ye[u][:, t, :], in_offset=None, compute_op=ALU.add
                    ).then_inc(added, 16)

            pool.wait_ge(gated_step, 1)
            pool.sem_inc(step.sem, 1)
            step.n = 1
            gather(0, 0)
            gather(0, 1)
            for u in range(2):
                add(0, u)
                gather(1, u)
            with pool.Fori(1, E // 2 - 1) as i:
                step.loop(i - 1, 2 * (TILES + 1))
                for u in range(2):
                    add(i, u)
                    gather(i + 1, u)
                step.end(E // 2 - 2)
            for u in range(2):
                add(E // 2 - 1, u)
            pool.wait_ge(added, 16 * TILES * E)

        @block.tensor
        def _(pe):
            def turn(i, u):
                pe.wait_ge(gathered[u], 32 * i + 32)
                for t in range(TILES):
                    wait(pe, "rowsT_done", 2 * TILES * i + TILES * u + t - 1 if t or u or not isinstance(i, int) or i else 0)
                    for c in range(KD):
                        last = pe.transpose(turn_ps[t][:, c * P:(c + 1) * P], rows[u][:, t, c * P:(c + 1) * P],
                                            k["ident"][:, :])
                    if t == TILES - 1:
                        last.then_inc(ev["turned"], 1)
                    else:
                        last.then_inc(half_turned, 1)

            def body(i, u, more):
                n = 2 * i + u
                pe.wait_ge(weights_in[u], 32 * i + 32)
                wait(pe, "rowsT_done", TILES * n + TILES)
                wait(pe, "act_done", n - 1 if u or not isinstance(i, int) or i else 0)
                for ps, col in ((gate_ps[u], 0), (up_ps[u], FI)):
                    for f in range(KF):
                        for c in range(KD):
                            last = pe.matmul(ps[:, f * ROWS:(f + 1) * ROWS], wgu[u][:, c, col + f * P:col + (f + 1) * P],
                                             rowsT[u][:, c, :], start=(c == 0), stop=(c == KD - 1))
                last.then_inc(ev["gu_done"], 1)
                if more:
                    turn(i + u, 1 - u)
                wait(pe, "act_done", n + 1)
                wait(pe, "y_out", n)
                for t in range(TILES):
                    for f in range(KF):
                        last = pe.matmul(down_ps[t][:, :], actT[u][:, f, t * P:(t + 1) * P], wd[u][:, f, :],
                                         start=(f == 0), stop=(f == KF - 1))
                last.then_inc(ev["down_done"], 1)

            pe.wait_ge(gated_step, 1)
            turn(0, 0)
            for u in range(2):
                body(0, u, True)
            with pe.Fori(1, E // 2 - 1) as i:
                for u in range(2):
                    body(i, u, True)
            body(E // 2 - 1, 0, True)
            body(E // 2 - 1, 1, False)

        @block.scalar
        def _(act):
            def turned(i, u):
                n = 2 * i + u
                for t in range(TILES):
                    if t == TILES - 1:
                        wait(act, "turned", n + 1)
                    else:
                        act.wait_ge(half_turned, n + 1)
                        wait(act, "gu_done", n - 1 if not isinstance(i, int) or i else 0)
                    act.activation(rowsT[u][:, :, t * P:(t + 1) * P], turn_ps[t][:, :].rearrange("p (c q) -> p c q", c=KD),
                                   ACT.Copy).then_inc(ev["rowsT_done"], 1)

            def body(i, u, more):
                n = 2 * i + u
                wait(act, "gu_done", n + 1)
                wait(act, "act_done", n - 1 if not isinstance(i, int) or i else 0)
                act.activation(th[u][:, :, :].rearrange("p f q -> p (f q)"), gate_ps[u][:, :], ACT.Tanh, scale=0.5
                               ).then_inc(ev["th_done"], 1)
                if more:
                    turned(i + u, 1 - u)

            turned(0, 0)
            for u in range(2):
                body(0, u, True)
            with act.Fori(1, E // 2 - 1) as i:
                for u in range(2):
                    body(i, u, True)
            body(E // 2 - 1, 0, True)
            body(E // 2 - 1, 1, False)

        @block.vector
        def _(dve):
            def convert(i, u):
                dve.wait_ge(tab_in[u], 16 * i + 16)
                dve.tensor_copy(gather_at[u][:, :], tab[u][:, :, 0])
                dve.tensor_scalar(weight[u][:, :], tab[u][:, :, 1], 0.5, None, ALU.mult).then_inc(ev["converted"], 1)

            def body(i, u):
                n = 2 * i + u
                wait(dve, "th_done", n + 1)
                wait(dve, "down_done", n - 1 if not isinstance(i, int) or i else 0)
                dve.scalar_tensor_tensor(gated[u][:, :, :].rearrange("p f q -> p (f q)"),
                                         th[u][:, :, :].rearrange("p f q -> p (f q)"), 1.0, gate_ps[u][:, :],
                                         ALU.add, ALU.mult).then_inc(gated_step, 1)
                dve.wait_ge(gated_step, n + 2)
                dve.tensor_tensor(actT[u][:, :, :].rearrange("p f q -> p (f q)"),
                                  gated[u][:, :, :].rearrange("p f q -> p (f q)"), up_ps[u][:, :], ALU.mult
                                  ).then_inc(ev["act_done"], 1)
                wait(dve, "down_done", n + 1)
                wait(dve, "earlier_added", n)
                wait(dve, "converted", n + 1)
                dve.tensor_copy(add_at[u][:, :], gather_at[u][:, :])
                for t in range(TILES):
                    last = dve.tensor_scalar(ye[u][:, t, :], down_ps[t][:, :], weight[u][:, t:t + 1], None, ALU.mult)
                last.then_inc(ev["y_out"], 1)

            for u in range(2):
                convert(0, u)
            with dve.Fori(0, E // 2 - 1) as i:
                for u in range(2):
                    body(i, u)
                    wait(dve, "y_out", 2 * i + u + 1)
                    convert(i + 1, u)
            for u in range(2):
                body(E // 2 - 1, u)


def load_projections(nc, k, ins):
    with (
        nc.sbuf_tensor("gain_w", [P, INTER // P], F32) as gain,
        nc.semaphore("w_in_loaded") as in_loaded,
        nc.semaphore("w_out_loaded") as out_loaded,
        nc.Block() as block,
    ):
        @block.sync
        def _(sp):
            sp.dma_start(k["w_out"][:, :, :],
                         ins["L0_attn_out_proj_w"].rearrange("(m p) d -> p m d", p=P)).then_inc(out_loaded, 16)
            with nc.allow_non_contiguous_dma(reason="a small per-channel vector"):
                sp.dma_start(gain[:, :],
                             ins["L0_attn_norm_w"].rearrange("(m p) -> p m", p=P)).then_inc(out_loaded, 16)
            sp.dma_start(k["w_in"][:, :, :],
                         ins["L0_attn_in_proj_w"].rearrange("(m p) d -> p m d", p=P)).then_inc(in_loaded, 16)
            sp.wait_ge(in_loaded, 16)

        @block.vector
        def _(dve):
            dve.wait_ge(out_loaded, 32)
            for m in range(INTER // P):
                dve.tensor_scalar(k["w_out"][:, m, :], k["w_out"][:, m, :], gain[:, m:m + 1], None, ALU.mult)


def finish(nc, dram, out):
    with nc.semaphore("out_done") as out_done, nc.Block() as block:
        @block.sync
        def _(sp):
            sp.dma_start(out.rearrange("c s d -> (c s) d"), dram["acc"][0:TOK, :]).then_inc(out_done, 16)
            sp.wait_ge(out_done, 16)


_INS = ["x", "txt", "L0_tok_log_dt", "L0_tok_B_ri", "L0_tok_inv_A_real", "L0_tok_A_imag", "L0_attn_in_proj_w",
        "L0_attn_conv_w", "L0_attn_conv_b", "L0_attn_A_log", "L0_attn_D", "L0_attn_dt_bias", "L0_attn_norm_w",
        "L0_attn_out_proj_w", "L0_ffn_w_cls", "L0_ffn_bias", "L0_ffn_w_gate_up", "L0_ffn_w_down"]


def build(nc, ins, out):
    with ExitStack() as ctx:
        def sb(name, shape, dt=F32):
            return ctx.enter_context(nc.sbuf_tensor(name, shape, dt))

        dram = {
            "h": nc.dram_tensor("h", (BATCH, SEQ, DM), F32).ap(),
            "x2": nc.dram_tensor("x2", (TOK + CAP, DM), F32).ap(),
            "acc": nc.dram_tensor("acc", (TOK + CAP, DM), F32).ap(),
            "slots": nc.dram_tensor("slots", (SLOTS, 2), F32).ap(),
        }
        k = {
            "ident": sb("ident", [P, P]),
            "upto": sb("upto", [Q, Q]),
            "after": sb("after", [Q, Q]),
            "before": sb("before", [Q, Q]),
            "ones": sb("ones", [Q, P]),
            "half_power": sb("half_power", [P, 4]),
            "far": sb("far", [Q, Q], BF16),
            "ident16": sb("ident16", [P, P], BF16),
            "pick": sb("pick", [3 * HH, HH], BF16),
            "unpick": sb("unpick", [3 * HH, HH], BF16),
            "token": sb("token", [Q, 1]),
            "numbers": sb("numbers", [Q, NE]),
            "count": sb("count", [Q, E]),
            "conv_w": sb("conv_w", [P, CONV_TILES, 4]),
            "conv_b": sb("conv_b", [P, CONV_TILES]),
            "neg_a": sb("neg_a", [Q, HEADS]),
            "skip_d": sb("skip_d", [Q, HEADS]),
            "dt_bias": sb("dt_bias", [Q, HEADS]),
            "top_bias": sb("top_bias", [Q, NE]),
            "w_cls": sb("w_cls", [P, KD, NE]),
        }
        make_constants(nc, k, ins, dram)
        s4d_rows(nc, k, ins, dram)
        with ExitStack() as c2:
            k["w_in"] = c2.enter_context(nc.sbuf_tensor("w_in", [P, KD, PROJ], F32))
            k["w_out"] = c2.enter_context(nc.sbuf_tensor("w_out", [P, INTER // P, DM], F32))
            load_projections(nc, k, ins)
            sequences(nc, k, ins, dram)
        experts(nc, k, ins, dram)
        finish(nc, dram, out)


def kernel(**inputs):
    import numpy as _np
    import concourse.bacc as _bacc
    from concourse import mybir as _mybir
    from concourse.bass_utils import run_bass_kernel_spmd as _run

    nc = _bacc.Bacc("TRN2", target_bir_lowering=False, num_devices=1)
    arrays, args = {}, {}
    for name in _INS:
        a = _np.ascontiguousarray(inputs[name])
        arrays[f"in_{name}_dram"] = a
        args[name] = nc.dram_tensor(f"in_{name}_dram", a.shape, _mybir.dt.from_np(a.dtype), kind="ExternalInput").ap()
    out = nc.dram_tensor("out_0_dram", (BATCH, SEQ, DM), F32, kind="ExternalOutput").ap()
    build(nc, args, out)
    r = _run(nc, [arrays], core_ids=[0])
    return r.results[0]["out_0_dram"]
```

```python
from contextlib import ExitStack

import concourse.bass as bass
from concourse import mybir

ALU = mybir.AluOpType
ACT = mybir.ActivationFunctionType
AX = mybir.AxisListType.X
F32 = mybir.dt.float32
BF16 = mybir.dt.bfloat16
U32 = mybir.dt.uint32

BATCH, SSM_H, SSM_N = 16, 256, 64
TXT = 77
SEQ = SSM_H + TXT
DM = 512
P = 128
KD = DM // P
PAIRS = SSM_H // 2
BLK = DM // P
LOW = P
LOG = LOW.bit_length() - 1
GRP = 16
HEADS, HD, NST = 64, 16, 128
INTER = HEADS * HD
CONV_TILES = (INTER + 2 * NST) // P
B_TILE, C_TILE = INTER // P, INTER // P + 1
XBC0 = INTER
DT0 = 2 * INTER + 2 * NST
PROJ = DT0 + HEADS
CH = 3
Q = SEQ // CH
HH = HEADS // 2
HG = 4
GROUPS = HEADS // HG
E, NE, TOPK, CAP, FI = 32, 64, 8, 256, 256
TOK = BATCH * SEQ
SLOTS = E * CAP
EPS = 1e-5
FLOOR = -120.0
TINY = 1e-30

CHAIN = CH * GROUPS
LX, MX = 3, 4


def conv_order():
    return [B_TILE, C_TILE] + list(range(B_TILE))


def make_plan():
    plan = {eng: [[] for _ in range(CHAIN)] for eng in ("pe", "act", "dve", "pool")}

    def at(slot, eng, *names, n=0):
        turn, slot = divmod(slot, CHAIN)
        for name in names:
            plan[eng][slot].append((name, n, -turn))

    def ahead(slot, eng, *names, n=0):
        at(slot - CHAIN, eng, *names, n=n)

    for q in range(CHAIN):
        at(q - 4, "pe", "decay", n=q)
        at(q - 3, "act", "heads", n=q)
        at(q - 2, "dve", "heads", n=q)
        at(q, "pe", "heads", n=q)
    s = GROUPS
    ahead(s + 4, "dve", "norm_sums")
    ahead(s + 6, "dve", "norm_var")
    ahead(s + 7, "pool", "norm_rstd")
    s = 2 * GROUPS
    for j in range(CH):
        ahead(s - 4 + j, "dve", "norm", n=j)
        ahead(s + 2 + j, "pe", "xnT", n=j)
        ahead(s + 2 + j, "act", "xnT", n=j)
    ahead(s + 5, "pe", "dt")
    ahead(s + 5, "dve", "dt_sum")
    ahead(s + 6, "act", "dt_exp")
    ahead(s + 6, "dve", "dt_plus")
    ahead(s + 7, "act", "dt_log")
    ahead(s + 8, "dve", "dt_rest")
    ahead(s + 9, "dve", "dt_end")
    for n in range(CONV_TILES):
        slot = s + 5 + (n + 1) // 2
        ahead(slot, "pe", "conv", n=n)
        ahead(slot, "act", "conv", n=n)
        ahead(slot, "dve", "conv", n=n)
    ahead(s + 10, "act", "conv", n=CONV_TILES)
    ahead(s + 10, "dve", "conv", n=CONV_TILES)
    for j, slot in enumerate((s + 10, s + GROUPS + 5, s + 2 * GROUPS + 6)):
        ahead(slot, "pe", "cum", n=j)
        ahead(slot, "act", "cum", n=j)
        ahead(slot + 1, "dve", "cum", n=j)
    for j in range(CH):
        s = (j - 1) * GROUPS
        late = 4 if j == 0 else 0
        at(s + 8 + late, "pe", "cb", n=j)
        at(s + 9 + late, "dve", "cb", n=j)
        at(s + 9 + late, "pe", "xrow", n=j)
        at(s + 10 + late, "act", "xrow", n=j)
        at(s + 11 + late, "pool", "dtx", n=j)
        if j < CH - 1:
            if j:
                at(s + 8, "pool", "kept")
            at(s + 12 + min(late, 3), "pool", "dtxf", n=j)
            at(s + (GROUPS + 4 if j == 0 else 13), "pe", "state", n=j)
            at(s + (GROUPS + 5 if j == 0 else 14), "dve", "state", n=j)
    for j in range(CH):
        s = j * GROUPS
        at(s, "pe", "z", n=j)
        at(s + 1, "act", "z", n=j)
        at(s + 2, "dve", "z", n=j)
        at(s + 3, "pool", "skip", n=j)
        if j:
            at(s + 4, "pe", "inter", n=j)
            at(s + 5, "dve", "inter", n=j)
            at(s + 6, "pool", "skip_sum", n=j)
    for j in range(CH):
        s = (j + 1) * GROUPS
        at(s, "pool", "gate", n=j)
        at(s, "act", "squares", n=j)
        at(s + 1, "dve", "out_var", n=j)
        at(s + 1, "pool", "out_rstd", n=j)
        at(s + 6, "pe", "gT", n=j)
        at(s + 7, "act", "gT", n=j)
        at(s + 8, "pe", "out", n=j)
        at(s + 9, "dve", "out", n=j)
        at(s + 9, "pool", "x2_rstd", n=j)
        at(s + 10, "dve", "x2", n=j)
        at(s + 11, "act", "stores", n=j)
        at(s + 11, "pe", "x2T", n=j)
        at(s + 12, "act", "x2T", n=j)
        at(s + 13, "pe", "logits", n=j)
        at(s + 14, "dve", "largest", n=j)
        at(s + 15, "act", "logits", n=j)
        s += GROUPS
        at(s, "dve", "choices", n=j)
        at(s + 3, "pe", "rank", n=j)
        at(s + 4, "dve", "rank", n=j)
        at(s + 8, "dve", "weights", n=j)
        at(s + (10 if j == 0 else 12), "pool", "scatter", n=j)
    order = {"pe": {"decay": -1, "heads": 1}, "act": {"heads": -1}, "dve": {"heads": -2, "out": -1, "cum": -1}}
    for q in range(CHAIN):
        for eng in order:
            plan[eng][q].sort(key=lambda step: order[eng].get(step[0], 0))
        if q % GROUPS == GROUPS - 1:
            plan["dve"][q].append(("y", q // GROUPS, 0))
    return plan


PLAN = make_plan()
NARROW_USES = ("xnT", "dt", "conv", "cum", "cb", "out", "x2T", "logits", "rank")
WIDE_USES = ("z", "inter", "gT", "xrow", "state")
NARROW = [step for steps in PLAN["pe"] for step in steps if step[0] in NARROW_USES]
WIDE = [step for steps in PLAN["pe"] for step in steps if step[0] in WIDE_USES]
TIMES = {"dt": 1, "conv": CONV_TILES, "inter": CH - 1, "state": CH - 1}
READ = {"xnT": ["xnT_done"], "dt": ["dt_read"], "conv": ["tapped"], "cum": ["cum_exp", "parts_done"],
        "cb": ["cbm_done"], "out": ["h2_done"], "x2T": ["x2T_done"], "logits": ["exped"], "rank": ["count_done"],
        "xrow": ["xrow_done"], "z": ["zs_done"], "inter": ["yint_done"], "state": ["state_done"],
        "gT": ["ggT_done"]}


def turns(eng, steps, plan, stage, loop_start=None, loop_end=None):
    def turn(b, offsets, before):
        stage["now"], stage["before"] = offsets, before
        for slot in plan:
            for name, n, offset in slot:
                if offset in offsets:
                    steps[name](b + offset, n)

    turn(-1, (1,), ())
    turn(0, (0, 1), (1,))
    with eng.Fori(1, BATCH - 1) as b:
        if loop_start:
            loop_start(b - 1)
        turn(b, (-1, 0, 1), (0, 1))
        if loop_end:
            loop_end(BATCH - 2)
    turn(BATCH - 1, (-1, 0), (-1, 0, 1))
    turn(BATCH, (-1,), (-1, 0))


class Steps:

    def __init__(self, eng, sem):
        self.eng, self.sem, self.base, self.n = eng, sem, 0, 0

    def done(self, ins):
        ins.then_inc(self.sem, 1)
        self.n += 1
        return self.n

    def wait(self, n=None):
        self.eng.wait_ge(self.sem, self.base + (self.n if n is None else n))

    def link(self, ins):
        self.done(ins)
        self.wait()

    def loop(self, i, per):
        self.before, self.per = self.n, per
        self.base, self.n = self.n + i * per, 0

    def end(self, turns):
        assert self.n == self.per, ("steps of a turn:", self.n)
        self.base, self.n = 0, self.before + turns * self.per


def bc(ap, shape):
    return ap.broadcast_to(shape)


def make_constants(nc, k, ins, dram):
    with ExitStack() as ctx:
        made = ctx.enter_context(nc.semaphore("made"))
        loaded = ctx.enter_context(nc.semaphore("loaded"))
        cls_loaded = ctx.enter_context(nc.semaphore("cls_loaded"))
        turned = ctx.enter_context(nc.semaphore("turned"))
        dve_step = ctx.enter_context(nc.semaphore("dve_step"))
        act_step = ctx.enter_context(nc.semaphore("act_step"))
        stored, zero, empty = k["stored"], k["zero"], k["empty"]
        wcls = ctx.enter_context(nc.sbuf_tensor("wcls", [NE, DM], F32))
        clsT = ctx.enter_context(nc.psum_tensor("clsT", [P, KD, NE], F32))
        block = ctx.enter_context(nc.Block())

        @block.sync
        def _(sp):
            sp.dma_start(wcls[:, :], ins["L0_ffn_w_cls"]).then_inc(cls_loaded, 16)
            with nc.allow_non_contiguous_dma(reason="small per-channel vectors"):
                sp.dma_start(k["conv_w"][:, :, :],
                             ins["L0_attn_conv_w"].rearrange("(m p) t -> p m t", p=P)).then_inc(loaded, 16)
                sp.dma_start(k["conv_b"][:, :],
                             ins["L0_attn_conv_b"].rearrange("(m p) -> p m", p=P)).then_inc(loaded, 16)
            for name, key, width in (("L0_attn_A_log", "neg_a", HEADS), ("L0_attn_D", "skip_d", HEADS),
                                     ("L0_attn_dt_bias", "dt_bias", HEADS), ("L0_ffn_bias", "top_bias", NE)):
                sp.dma_start(k[key][:, :], ins[name].unsqueeze(0).broadcast_to([Q, width])).then_inc(loaded, 16)
            sp.dma_start(dram["h"][:, SSM_H:SEQ, :], ins["txt"]).then_inc(stored, 16)
            sp.wait_ge(made, 1)
            sp.dma_start(dram["slots"].rearrange("(e p t) c -> p e (t c)", p=P, t=2),
                         empty[:, :, :].rearrange("p t c -> p (t c)").unsqueeze(1).broadcast_to([P, E, 4])
                         ).then_inc(stored, 16)
            sp.dma_start(dram["x2"][TOK:TOK + CAP, :].rearrange("(p t) d -> p (t d)", t=2),
                         zero[:, :]).then_inc(stored, 16)

        @block.gpsimd
        def _(pool):
            step = Steps(pool, ctx.enter_context(nc.semaphore("pool_step")))
            step.done(pool.memset(zero[:, :], 0.0))
            step.done(pool.memset(empty[:, :, :], 0.0))
            step.done(pool.memset(k["ident"][:, :], 0.0))
            step.done(pool.memset(k["upto"][:, :], 1.0))
            step.done(pool.memset(k["after"][:, :], 1.0))
            step.done(pool.memset(k["before"][:, :], 1.0))
            step.done(pool.memset(k["ones"][:, :], 1.0))
            step.done(pool.memset(k["half_power"][:, :], -0.5))
            step.done(pool.memset(k["pick"][:, :], 0.0))
            step.done(pool.memset(k["far"][:, :], 0.0))
            step.done(pool.memset(k["ident16"][:, :], 0.0))
            step.done(pool.memset(k["count"][:, :], 0.0))
            step.done(pool.iota(k["token"][:, :], pattern=[[0, 1]], base=0, channel_multiplier=1,
                                allow_small_or_imprecise_dtypes=True))
            step.done(pool.iota(k["numbers"][:, :], pattern=[[1, NE]], base=0, channel_multiplier=0,
                                allow_small_or_imprecise_dtypes=True))
            step.wait()
            step.done(pool.iota(empty[:, :, 0], pattern=[[1, 2]], base=TOK, channel_multiplier=2,
                                allow_small_or_imprecise_dtypes=True))
            step.done(pool.affine_select(out=k["ident"][:, :], in_=k["ident"][:, :], compare_op=ALU.not_equal,
                                         fill=1.0, base=0, pattern=[[-1, P]], channel_multiplier=1))
            step.done(pool.affine_select(out=k["upto"][:, :], in_=k["upto"][:, :], compare_op=ALU.is_ge,
                                         fill=0.0, base=0, pattern=[[1, Q]], channel_multiplier=-1))
            step.done(pool.affine_select(out=k["after"][:, :], in_=k["after"][:, :], compare_op=ALU.is_gt,
                                         fill=0.0, base=0, pattern=[[-1, Q]], channel_multiplier=1))
            step.done(pool.affine_select(out=k["before"][:, :], in_=k["before"][:, :], compare_op=ALU.is_gt,
                                         fill=0.0, base=0, pattern=[[1, Q]], channel_multiplier=-1))
            step.done(pool.affine_select(out=k["far"][:, :], in_=k["far"][:, :], compare_op=ALU.is_ge,
                                         fill=-16384.0, base=0, pattern=[[1, Q]], channel_multiplier=-1))
            step.done(pool.affine_select(out=k["ident16"][:, :], in_=k["ident16"][:, :], compare_op=ALU.not_equal,
                                         fill=1.0, base=0, pattern=[[-1, P]], channel_multiplier=1))
            for part in range(3):
                step.link(pool.affine_select(out=k["pick"][:, :], in_=k["pick"][:, :], compare_op=ALU.not_equal,
                                             fill=1.0, base=-HH * part, pattern=[[-1, HH]], channel_multiplier=1))
            step.link(pool.tensor_scalar(k["unpick"][:, :], k["pick"][:, :], -1.0, None, ALU.mult))
            pool.sem_inc(made, 1)

        @block.tensor
        def _(pe):
            pe.wait_ge(made, 1)
            pe.wait_ge(cls_loaded, 16)
            for c in range(KD):
                last = pe.transpose(clsT[:, c, :], wcls[:, c * P:(c + 1) * P], k["ident"][0:NE, 0:NE])
            last.then_inc(turned, 1)

        @block.vector
        def _(dve):
            step = Steps(dve, dve_step)
            dve.wait_ge(turned, 1)
            step.done(dve.tensor_copy(k["w_cls"][:, :, :], clsT[:, :, :]))
            dve.wait_ge(loaded, 6 * 16)
            step.done(dve.tensor_scalar(k["conv_w"][:, :, :], k["conv_w"][:, :, :], 0.25, None, ALU.mult))
            step.done(dve.tensor_scalar(k["conv_b"][:, :], k["conv_b"][:, :], 0.5, None, ALU.mult))
            dve.wait_ge(act_step, 1)
            step.link(dve.tensor_scalar(k["neg_a"][:, :], k["neg_a"][:, :], -1.0, None, ALU.mult))

        @block.scalar
        def _(act):
            act.wait_ge(loaded, 6 * 16)
            act.activation(k["neg_a"][:, :], k["neg_a"][:, :], ACT.Exp).then_inc(act_step, 1)


def s4d_rows(nc, k, ins, dram):
    with ExitStack() as ctx:
        def sb(name, shape, dt=F32):
            return ctx.enter_context(nc.sbuf_tensor(name, shape, dt))

        def sem(name):
            return ctx.enter_context(nc.semaphore(name))

        inv_a = sb("inv_a", [PAIRS, P])
        a_im = sb("a_im", [PAIRS, P])
        b_ri = sb("b_ri", [PAIRS, P, 2])
        log_dt = sb("log_dt", [PAIRS, 2])
        half_dt = sb("half_dt", [PAIRS, 2])
        two_dt = sb("two_dt", [PAIRS, 2])
        scratch = sb("scratch", [PAIRS, 8, P])
        rows = sb("rows", [PAIRS, 4, P])
        power = sb("power", [P, LOG + 1, 2, PAIRS])
        gain = sb("gain", [P, 2, PAIRS])
        crow = sb("crow", [PAIRS, 2, 2 * P])
        cT = sb("cT", [P, 2, BATCH, PAIRS])
        x = sb("x", [P, 2, BLK, BATCH, PAIRS])
        xt = [sb(f"xt{n}", [P, BATCH, PAIRS]) for n in range(2)]
        v = [sb(f"v{n}", [P, 2, GRP, LOW]) for n in range(2)]
        vt = sb("vt", [P, 4, GRP, LOW // 2])
        xd = sb("xd", [P, 2, GRP, 2, BLK * BATCH])
        kout = sb("kout", [P, GRP, LOW])
        ptab = ctx.enter_context(nc.psum_tensor("ptab", [P, 4, P], F32))
        pct = [ctx.enter_context(nc.psum_tensor(f"pct{n}", [P, 4, P], F32)) for n in range(2)]
        pk = [ctx.enter_context(nc.psum_tensor(f"pk{n}", [P, 4, P], F32)) for n in range(4)]

        params_in = sem("params_in")
        c_in = [sem(f"c_in{n}") for n in range(2)]
        dve_step, pool_step, act_step = sem("dve_step"), sem("pool_step"), sem("act_step")
        exps = sem("exps")
        rows_ready, tab_turned, tab_ready = sem("rows_ready"), sem("tab_turned"), sem("tab_ready")
        c_turned, c_copied = sem("c_turned"), sem("c_copied")
        x_re, x_im = sem("x_re"), sem("x_im")
        v_re, v_im = sem("v_re"), sem("v_im")
        xd_ready, prod_done, k_copied = sem("xd_ready"), sem("prod_done"), sem("k_copied")
        k_stored, kout_free = sem("k_stored"), sem("kout_free")
        cleared = sem("cleared")
        NG = PAIRS // GRP
        block = ctx.enter_context(nc.Block())

        @block.sync
        def _(sp):
            sp.dma_start(inv_a[:, :], ins["L0_tok_inv_A_real"].rearrange("(p r) n -> p (r n)", r=2)).then_inc(params_in, 16)
            sp.dma_start(a_im[:, :], ins["L0_tok_A_imag"].rearrange("(p r) n -> p (r n)", r=2)).then_inc(params_in, 16)
            sp.dma_start(b_ri[:, :, :], ins["L0_tok_B_ri"].rearrange("(p r) n i -> p (r n) i", r=2)).then_inc(params_in, 16)
            sp.dma_start(log_dt[:, :], ins["L0_tok_log_dt"].rearrange("(p r) -> p r", r=2)).then_inc(params_in, 16)
            for c in range(BATCH):
                if c >= 2:
                    sp.wait_ge(c_turned, c - 1)
                sp.dma_start(crow[:, c % 2, :], ins["x"][c].rearrange("(p r) n i -> p (r n i)", r=2)
                             ).then_inc(c_in[c % 2], 16)
            with sp.Fori(0, NG) as g:
                sp.wait_ge(k_copied, 4 * g + 5)
                for r in range(2):
                    for a in range(BLK):
                        lo = (r * BLK + a) * BATCH
                        dst = dram["h"][:, 0:SSM_H, a * P:(a + 1) * P].rearrange(
                            "c (p r) b -> c r p b", r=2)[:, r, bass.ds(g * GRP, GRP), :]
                        sp.dma_start(dst, kout[lo:lo + BATCH, :, :]).then_inc(k_stored, 16)
                sp.wait_ge(k_stored, 16 * 2 * BLK * g + 16 * 2 * BLK)
                sp.sem_inc(kout_free, 1)
            sp.wait_ge(k["stored"], 48)

        @block.scalar
        def _(act):
            act.wait_ge(params_in, 64)
            act.activation(half_dt[:, :], log_dt[:, :], ACT.Exp).then_inc(exps, 1)
            act.activation(inv_a[:, :], inv_a[:, :], ACT.Exp).then_inc(exps, 1)
            act.wait_ge(tab_turned, 1)
            act.activation(power[:, 0, :, :], ptab[:, 0:2, :], ACT.Copy).then_inc(tab_ready, 1)
            act.activation(gain[:, :, :], ptab[:, 2:4, :], ACT.Copy).then_inc(tab_ready, 1)
            for c in range(BATCH):
                act.wait_ge(c_turned, c + 1)
                act.activation(cT[:, :, c, :], pct[c % 2][:, 0:2, :], ACT.Copy).then_inc(c_copied, 1)
            act.wait_ge(cleared, 1)
            act.wait_ge(x_re, 1)
            act.wait_ge(x_im, 1)
            with act.Fori(0, NG) as g:
                act.wait_ge(prod_done, 4 * g + 5)
                for r in range(2):
                    half = slice(r * SSM_N, (r + 1) * SSM_N)
                    for i in range(2):
                        act.activation(xd[half, i, :, r, :],
                                       x[half, i, :, :, bass.ds(g * GRP, GRP)].rearrange("p a c q -> p q (a c)"),
                                       ACT.Copy, scale=-1.0 if i else 1.0).then_inc(xd_ready, 1)
                act.wait_ge(kout_free, g + 1)
                for b in range(4):
                    act.wait_ge(prod_done, 4 * g + b + 6)
                    act.activation(kout[:, 4 * b:4 * b + 4, :], pk[b][:, :, :], ACT.Copy).then_inc(k_copied, 1)

        @block.tensor
        def _(pe):
            pe.sem_inc(prod_done, 5)
            pe.sem_inc(k_copied, 1)
            pe.sem_inc(kout_free, 1)
            pe.wait_ge(rows_ready, 1)
            for n in range(4):
                last = pe.transpose(ptab[:, n, :], rows[:, n, :], k["ident"][:, :])
            last.then_inc(tab_turned, 1)
            for c in range(BATCH):
                pe.wait_ge(c_in[c % 2], 16 * (c // 2 + 1))
                if c >= 2:
                    pe.wait_ge(c_copied, c - 1)
                for i in range(2):
                    last = pe.transpose(pct[c % 2][:, i, :], crow[:, c % 2, i:2 * P:2], k["ident"][:, :])
                last.then_inc(c_turned, 1)
            with pe.Fori(0, NG // 2) as gg:
                for u in range(2):
                    pe.wait_ge(xd_ready, 8 * gg + 4 * u + 4)
                    pe.wait_ge(v_re, 2 * LOG * gg + LOG * (u + 1) + 1)
                    pe.wait_ge(v_im, 2 * LOG * gg + LOG * (u + 1) + 1)
                    for b in range(4):
                        pe.wait_ge(k_copied, 8 * gg + 4 * u + 1)
                        for q in range(4):
                            pair = 4 * b + q
                            for i in range(2):
                                last = pe.matmul(pk[b][:, q, :], xd[:, i, pair, :, :].rearrange("p r m -> p (r m)"),
                                                 v[u][:, i, pair, :], start=(i == 0), stop=(i == 1))
                        last.then_inc(prod_done, 1)

        def times(eng, out, xr, xi, pr, pi, step, imaginary, t1, t2, other=None):
            if other is None:
                step.done(eng.tensor_tensor(t1, xr, pi if imaginary else pr, ALU.mult))
            elif imaginary:
                t1 = other[1]
            else:
                eng.tensor_tensor(other[1], xr, pi, ALU.mult).then_inc(cross, 1)
                step.done(eng.tensor_tensor(t1, xr, pr, ALU.mult))
            step.link(eng.tensor_tensor(t2, xi, pr if imaginary else pi, ALU.mult))
            if other is not None and imaginary:
                eng.wait_ge(cross, other[0])
            return eng.tensor_tensor(out, t1, t2, ALU.add if imaginary else ALU.subtract)

        cross = sem("cross")
        x_part = [sem("x_part_re"), sem("x_part_im")]
        pow_re, pow_im = sem("pow_re"), sem("pow_im")
        pw = [pow_re, pow_im]
        vs = [v_re, v_im]
        cleared_v = sem("cleared_v")

        def part_of(eng, part, step, spare):
            im = part == 1
            pt = sb(f"pt{part}", [P, 2, PAIRS])
            eng.wait_ge(tab_ready, 2)
            for n in range(LOG):
                if n:
                    eng.wait_ge(pow_re, n)
                    eng.wait_ge(pow_im, n)
                re, imag = power[:, n, 0, :], power[:, n, 1, :]
                times(eng, power[:, n + 1, part, :], re, imag, re, imag, step, im, pt[:, 0, :], pt[:, 1, :]
                      ).then_inc(pw[part], 1)
            eng.wait_ge(pow_re, LOG)
            eng.wait_ge(pow_im, LOG)
            eng.wait_ge(c_copied, BATCH)
            shape = [P, BATCH, PAIRS]
            for a in range(BLK):
                if a == 0:
                    xr, xi, pr, pi = cT[:, 0], cT[:, 1], gain[:, 0, :], gain[:, 1, :]
                else:
                    xr, xi = x[:, 0, a - 1], x[:, 1, a - 1]
                    pr, pi = power[:, LOG, 0, :], power[:, LOG, 1, :]
                    eng.wait_ge(x_part[0], a)
                    eng.wait_ge(x_part[1], a)
                times(eng, x[:, part, a], xr, xi, bc(pr.unsqueeze(1), shape), bc(pi.unsqueeze(1), shape), step, im,
                      xt[part][:, :, :], spare, (a + 1, xt[1][:, :, :])).then_inc(x_part[part], 1)
            eng.wait_ge(x_part[0], BLK)
            eng.wait_ge(x_part[1], BLK)
            eng.sem_inc(x_im if im else x_re, 1)
            for u in range(2):
                step.done(eng.memset(v[u][:, part, :, 0:1], 0.0 if im else 1.0))
            step.wait()
            eng.sem_inc(cleared_v, 1)
            eng.sem_inc(vs[part], 1)
            eng.wait_ge(cleared_v, 2)
            with eng.Fori(0, NG // 2) as gg:
                step.loop(gg, (1 if im else 2) * 2 * LOG)
                for u in range(2):
                    eng.wait_ge(prod_done, 8 * gg + 4 * u + 1)
                    for n in range(LOG):
                        w = 1 << n
                        done = 2 * LOG * gg + LOG * u + n + 1
                        eng.wait_ge(v_re, done)
                        eng.wait_ge(v_im, done)
                        shape_v = [P, GRP, w]
                        pr, pi = (power[:, n, i, bass.ds(gg * 2 * GRP + u * GRP, GRP)].unsqueeze(2).broadcast_to(shape_v)
                                  for i in range(2))
                        times(eng, v[u][:, part, :, w:2 * w], v[u][:, 0, :, 0:w], v[u][:, 1, :, 0:w], pr, pi, step, im,
                              vt[:, 2 * part, :, 0:w], vt[:, 2 * part + 1, :, 0:w],
                              (BLK + done, vt[:, 2, :, 0:w])).then_inc(vs[part], 1)
                step.end(NG // 2)

        @block.gpsimd
        def _(pool):
            step = Steps(pool, pool_step)
            step.link(pool.memset(xd[:, :, :, :, :], 0.0))
            pool.sem_inc(cleared, 1)
            part_of(pool, 1, step, v[1][:, :, :, :].rearrange("p i q b -> p (i q b)")[:, 0:BATCH * PAIRS]
                    .rearrange("p (c q) -> p c q", c=BATCH))

        @block.vector
        def _(dve):
            step = Steps(dve, dve_step)
            t = [scratch[:, n, :] for n in range(8)]
            two = lambda ap: ap.rearrange("p (r n) -> p r n", r=2)
            dve.wait_ge(exps, 2)
            step.done(dve.tensor_scalar(two_dt[:, :], half_dt[:, :], 2.0, None, ALU.mult))
            step.link(dve.tensor_scalar(half_dt[:, :], half_dt[:, :], 0.5, None, ALU.mult))
            hd, td = (bc(z[:, :].unsqueeze(2), [PAIRS, 2, SSM_N]) for z in (half_dt, two_dt))
            step.done(dve.tensor_tensor(two(t[0]), two(inv_a[:, :]), hd, ALU.mult))
            step.link(dve.tensor_tensor(two(t[1]), two(a_im[:, :]), hd, ALU.mult))
            step.done(dve.tensor_scalar(t[2], t[0], 1.0, None, ALU.add))
            step.done(dve.tensor_scalar(t[3], t[0], -1.0, 1.0, ALU.mult, ALU.add))
            step.link(dve.tensor_tensor(t[4], t[1], t[1], ALU.mult))
            step.link(dve.tensor_tensor(t[5], t[2], t[2], ALU.mult))
            step.link(dve.tensor_tensor(t[5], t[5], t[4], ALU.add))
            step.link(dve.reciprocal(t[6], t[5]))
            step.link(dve.tensor_tensor(t[7], t[3], t[2], ALU.mult))
            step.link(dve.tensor_tensor(t[7], t[7], t[4], ALU.subtract))
            step.done(dve.tensor_tensor(rows[:, 0, :], t[7], t[6], ALU.mult))
            step.done(dve.scalar_tensor_tensor(rows[:, 1, :], t[1], 2.0, t[6], ALU.mult, ALU.mult))
            dve.wait_ge(params_in, 64)
            br, bi = b_ri[:, :, 0], b_ri[:, :, 1]
            step.done(dve.tensor_tensor(t[0], br, t[2], ALU.mult))
            step.done(dve.tensor_tensor(t[3], bi, t[1], ALU.mult))
            step.done(dve.tensor_tensor(t[4], bi, t[2], ALU.mult))
            step.link(dve.tensor_tensor(t[5], br, t[1], ALU.mult))
            step.done(dve.tensor_tensor(t[0], t[0], t[3], ALU.subtract))
            step.done(dve.tensor_tensor(t[4], t[4], t[5], ALU.add))
            step.link(dve.tensor_tensor(two(t[6]), two(t[6]), td, ALU.mult))
            step.done(dve.tensor_tensor(rows[:, 2, :], t[0], t[6], ALU.mult))
            step.link(dve.tensor_tensor(rows[:, 3, :], t[4], t[6], ALU.mult))
            dve.sem_inc(rows_ready, 1)
            part_of(dve, 0, step, v[0][:, :, :, :].rearrange("p i q b -> p (i q b)")[:, 0:BATCH * PAIRS]
                    .rearrange("p (c q) -> p c q", c=BATCH))


DVE_STEPS = 143


def sequences(nc, k, ins, dram):
    with ExitStack() as ctx:
        def sb(name, shape, dt=F32):
            return ctx.enter_context(nc.sbuf_tensor(name, shape, dt))

        def pb(name):
            return ctx.enter_context(nc.psum_tensor(name, [P, 512], F32))

        def sem(name):
            return ctx.enter_context(nc.semaphore(name))

        w_in = k["w_in"]
        hin = sb("hin", [Q, CH, DM])
        hres = sb("hres", [Q, CH, DM])
        stats = sb("stats", [Q, CH, 6])
        mv = sb("mv", [Q, CH, 2])
        var_e = sb("var_e", [Q, CH])
        rstd = sb("rstd", [Q, CH])
        xnT = sb("xnT", [P, KD, SEQ])
        sp = sb("sp", [Q, 6, CH, HEADS])
        dt = sb("dt", [Q, CH, HEADS])
        a = sb("a", [Q, CH, HEADS])
        a3 = sb("a3", [Q, 2 * CH, 3, HH])
        cacc = [sb(f"cacc{n}", [P, SEQ]) for n in range(3)]
        cth = [sb(f"cth{n}", [P, SEQ]) for n in range(2)]
        xbcT = sb("xbcT", [P, CONV_TILES, SEQ])
        parts = sb("parts", [3 * HH, CH, 2 * Q], BF16)
        mid = sb("mid", [3 * HH, 2 * Q], BF16)
        rest = sb("rest", [3 * HH, 2, 2 * Q])
        grow = sb("grow", [Q, CH, HEADS])
        fall = sb("fall", [Q, CH, HEADS])
        total = sb("total", [P, CH, HEADS])
        xrow = sb("xrow", [Q, INTER])
        zt = sb("zt", [Q, INTER])
        zs = sb("zs", [Q, INTER])
        cbm = sb("cbm", [Q, CH, Q])
        brow = sb("brow", [Q, 2, NST])
        dtx = sb("dtx", [Q, CH, INTER])
        dtxf = sb("dtxf", [Q, INTER])
        skip = sb("skip", [Q, INTER])
        yint = sb("yint", [Q, INTER])
        state = sb("state", [P, 2, INTER])
        kept = sb("kept", [P, INTER])
        lx = [sb(f"lx{n}", [Q, HG, Q]) for n in range(LX)]
        m_ = [sb(f"m{n}", [Q, HG, Q]) for n in range(MX)]
        y = sb("y", [Q, INTER])
        gg = sb("gg", [Q, INTER])
        ggT = sb("ggT", [P, INTER // P, Q])
        ss = sb("ss", [Q, CH])
        h2 = sb("h2", [Q, CH, DM])
        x2 = sb("x2s", [Q, CH, DM])
        x2T = sb("x2T", [P, KD, Q])
        stat2 = sb("stat2", [Q, 6])
        mv2 = sb("mv2", [Q, 2])
        small = sb("small", [Q, 12])
        ex = sb("ex", [Q, NE])
        score = sb("score", [Q, NE])
        biased = sb("biased", [Q, NE])
        top = sb("top", [Q, TOPK])
        topi = sb("topi", [Q, TOPK], U32)
        r8 = sb("r8", [Q, 8, TOPK])
        hot = sb("hot", [Q, TOPK, NE])
        hots = sb("hots", [Q, TOPK, NE])
        sel = sb("sel", [Q, E])
        place = sb("place", [Q, E])
        entry = sb("entry", [Q, CH, TOPK, 2])
        slot = sb("slot", [Q, CH, TOPK], U32)
        idle = sb("idle", [Q, 4])
        credit = sb("credit", [Q, CH + 1, 2])

        nar = [pb(f"nar{n}") for n in range(2)]
        dec = [pb(f"dec{n}") for n in range(2)]
        wide = ctx.enter_context(nc.psum_tensor("wide", [P, 1024], F32))
        ysum = ctx.enter_context(nc.psum_tensor("ysum", [P, 1024], F32))

        names = ["xn_done", "xnT_done", "var1", "rstd1", "exp_m", "one_plus", "logged",
                 "sp_m", "a_done", "base", "tanhed", "conv_done", "tapped", "cum_exp", "parts_done", "cbm_done",
                 "xrow_done", "z_tanh", "zs_done", "dtx_done", "dtxf_done", "skip_done", "yint_done",
                 "skip_sum", "state_done", "kept_done", "lx_done", "m_done", "y_heads", "y_done",
                 "gg_done", "sq_done", "ggT_done", "var_y", "rstd_y", "h2_done", "var2", "rstd2", "x2_done",
                 "x2T_done", "neg_max", "exped", "sel_done", "entry_done", "dt_read", "count_done", "idled"]
        ev = {n: sem(n) for n in names}
        full = {n: sem(n + "_full") for n in NARROW_USES + WIDE_USES}
        dec_full = [sem(f"dec_full{n}") for n in range(2)]
        entry_free = sem("entry_free")
        hin_in, hres_in = sem("hin_in"), sem("hres_in")
        stored = [sem(f"stored{j}") for j in range(CH)]
        scattered = sem("scattered")
        w_in_loaded, z_loaded = sem("w_in_loaded"), sem("z_loaded")
        w_out_loaded, w_out_scaled = sem("w_out_loaded"), sem("w_out_scaled")
        gain = sb("gain_w", [P, INTER // P])
        dve_step = sem("b_dve_step")
        act_step = sem("b_act_step")

        with nc.Block() as first:
            @first.gpsimd
            def _(pool):
                for s in list(ev.values()) + list(full.values()) + dec_full:
                    pool.sem_inc(s, 1)
                pool.sem_inc(entry_free, 2)
                pool.sem_inc(dve_step, 1)
                pool.dma_start(credit[:, CH, :], dram["x2"][TOK:TOK + Q, 0:2]).then_inc(scattered, 16)
                pool.wait_ge(scattered, 16)

            @first.sync
            def _(sy):
                for j in range(CH):
                    sy.dma_start(credit[:, j, :], dram["x2"][TOK:TOK + Q, 0:2]).then_inc(stored[j], 16)
                    sy.wait_ge(stored[j], 16)

        block = ctx.enter_context(nc.Block())

        def wait(eng, name, n):
            if isinstance(n, int) and n < 0:
                return
            eng.wait_ge(ev[name], n + 1)

        def number(kind, t, n):
            return TIMES.get(kind, CH) * t + n + (0 if kind == "inter" else 1)

        def wait_full(eng, kind, t, n):
            eng.wait_ge(full[kind], number(kind, t, n) + 1)

        def bank(kind, n):
            return nar[[step[:2] for step in NARROW].index((kind, n)) % 2]

        def chunk(j):
            return slice(j * Q, (j + 1) * Q)

        def first_of(t, j):
            return isinstance(t, int) and t == 0 and j == 0

        @block.sync
        def _(sy):
            with sy.Fori(0, BATCH) as i:
                sy.wait_ge(full["xnT"], CH * i + 1)
                sy.dma_start(hin[:, :, :], dram["h"][i].rearrange("(j p) d -> p j d", p=Q)).then_inc(hin_in, 16)
                wait(sy, "h2_done", CH * i)
                sy.dma_start(hres[:, :, :], dram["h"][i].rearrange("(j p) d -> p j d", p=Q)).then_inc(hres_in, 16)
            for j in range(CH):
                sy.wait_ge(stored[j], 16 + 32 * BATCH)

        @block.tensor
        def _(pe):
            stage = {}

            def take(kind, t, n):
                uses, banks = (NARROW, 2) if kind in NARROW_USES else (WIDE, 1)
                at = [step[:2] for step in uses].index((kind, n))
                turn = t - uses[at][2]
                was, there = at - banks, stage["now"]
                while was >= -len(uses):
                    if was < 0:
                        there = stage["before"]
                    if uses[was][2] in there:
                        kind, n, offset = uses[was]
                        turn = (turn if was >= 0 else turn - 1) + offset
                        for event in READ[kind]:
                            wait(pe, event, number(kind, turn, n))
                        return
                    was -= banks

            def take_narrow(kind, t, n):
                take(kind, t, n)
                return bank(kind, n)

            def xnT_(t, j):
                wait(pe, "xn_done", CH * t + j + 1)
                ps = take_narrow("xnT", t, j)
                for c in range(KD):
                    last = pe.transpose(ps[:, c * Q:(c + 1) * Q], hin[:, j, c * P:(c + 1) * P], k["ident"][0:Q, 0:Q])
                last.then_inc(full["xnT"], 1)

            def dt_(t, _n):
                if first_of(t, 0):
                    pe.wait_ge(w_in_loaded, 16)
                ps = take_narrow("dt", t, 0)
                wait(pe, "xnT_done", CH * t + CH)
                for j in range(CH):
                    for c in range(KD):
                        last = pe.matmul(ps[0:Q, j * HEADS:(j + 1) * HEADS], xnT[:, c, chunk(j)],
                                         w_in[:, c, DT0:PROJ], start=(c == 0), stop=(c == KD - 1))
                last.then_inc(full["dt"], 1)

            def conv_(t, n):
                m = conv_order()[n]
                ps = take_narrow("conv", t, n)
                for c in range(KD):
                    last = pe.matmul(ps[:, 0:SEQ], w_in[:, c, XBC0 + m * P:XBC0 + (m + 1) * P], xnT[:, c, :],
                                     start=(c == 0), stop=(c == KD - 1))
                last.then_inc(full["conv"], 1)

            def cum_(t, j):
                ps = take_narrow("cum", t, j)
                wait(pe, "a_done", t + 1)
                for half in range(2):
                    pe.matmul(ps[0:3 * HH, half * Q:(half + 1) * Q],
                              a3[:, 2 * j + half, :, :].rearrange("p r h -> p (r h)"), k["upto"][:, :],
                              start=True, stop=True)
                o = 2 * Q
                pe.matmul(ps[0:Q, o:o + HEADS], k["upto"][:, :], a[:, j, :], start=True, stop=True)
                pe.matmul(ps[0:Q, o + HEADS:o + 2 * HEADS], k["after"][:, :], a[:, j, :], start=True, stop=True)
                pe.matmul(ps[:, o + 2 * HEADS:o + 3 * HEADS], k["ones"][:, :], a[:, j, :], start=True, stop=True
                          ).then_inc(full["cum"], 1)

            def cb_(t, j):
                ps = take_narrow("cb", t, j)
                wait(pe, "conv_done", CONV_TILES * t + 2)
                last = pe.matmul(ps[0:Q, 0:Q], xbcT[:, B_TILE, chunk(j)], xbcT[:, C_TILE, chunk(j)],
                                 start=True, stop=True)
                if j < CH - 1:
                    last = pe.transpose(ps[0:Q, P:P + NST], xbcT[:, B_TILE, chunk(j)], k["ident"][:, :])
                last.then_inc(full["cb"], 1)

            def xrow_(t, j):
                take("xrow", t, j)
                wait(pe, "conv_done", CONV_TILES * (t + 1))
                for m in range(B_TILE):
                    last = pe.transpose(wide[0:Q, m * P:(m + 1) * P], xbcT[:, m, chunk(j)], k["ident"][:, :])
                last.then_inc(full["xrow"], 1)

            def z_(t, j):
                if first_of(t, j):
                    pe.wait_ge(z_loaded, 16)
                take("z", t, j)
                for half in range(2):
                    for c in range(KD):
                        last = pe.matmul(wide[0:Q, half * 512:(half + 1) * 512], xnT[:, c, chunk(j)],
                                         w_in[:, c, half * 512:(half + 1) * 512], start=(c == 0), stop=(c == KD - 1))
                last.then_inc(full["z"], 1)

            def inter_(t, j):
                take("inter", t, j)
                wait(pe, "state_done", 2 * t + j)
                for half in range(2):
                    last = pe.matmul(wide[0:Q, half * 512:(half + 1) * 512], xbcT[:, C_TILE, chunk(j)],
                                     state[:, j - 1, half * 512:(half + 1) * 512], start=True, stop=True)
                last.then_inc(full["inter"], 1)

            def state_(t, j):
                take("state", t, j)
                wait(pe, "dtxf_done", 2 * t + j + 1)
                wait(pe, "cbm_done", CH * t + j + 1)
                for half in range(2):
                    last = pe.matmul(wide[:, half * 512:(half + 1) * 512], brow[:, j, :],
                                     dtxf[:, half * 512:(half + 1) * 512], start=True, stop=True)
                last.then_inc(full["state"], 1)

            def decay_(t, q):
                j, g = divmod(q, GROUPS)
                b = q % 2
                if g == 0:
                    wait(pe, "parts_done", CH * t + j + 1)
                wait(pe, "lx_done", CHAIN * t + q - 1)
                half, h0 = divmod(g * HG, HH)
                cum = parts[:, j, half * Q:(half + 1) * Q]
                pe.matmul(dec[b][0:Q, 0:HG * Q], cum,
                          k["unpick"][:, h0:h0 + HG].unsqueeze(2).broadcast_to([3 * HH, HG, Q]),
                          start=True, stop=False, skip_group_check=True)
                pe.matmul(dec[b][0:Q, 0:HG * Q], k["ident16"][0:Q, 0:Q],
                          k["far"][:, :].unsqueeze(1).broadcast_to([Q, HG, Q]),
                          start=False, stop=False, skip_group_check=True)
                for n in range(HG):
                    last = pe.matmul(dec[b][0:Q, n * Q:(n + 1) * Q],
                                     k["pick"][:, h0 + n:h0 + n + 1].broadcast_to([3 * HH, Q]),
                                     cum, start=False, stop=(n == HG - 1), skip_group_check=True)
                last.then_inc(dec_full[b], 1)

            def heads_(t, q):
                j, g = divmod(q, GROUPS)
                if g == 0:
                    wait(pe, "dtx_done", CH * t + j + 1)
                    wait(pe, "y_done", CH * t + j)
                wait(pe, "m_done", CHAIN * t + q + 1)
                for n in range(HG):
                    h = g * HG + n
                    last = pe.matmul(ysum[0:Q, h * HD:(h + 1) * HD], m_[q % MX][:, n, :],
                                     dtx[:, j, h * HD:(h + 1) * HD], start=True, stop=True)
                last.then_inc(ev["y_heads"], 1)

            def gT_(t, j):
                wait(pe, "gg_done", CH * t + j + 1)
                take("gT", t, j)
                for f in range(INTER // P):
                    last = pe.transpose(wide[:, (f // 4) * 512 + (f % 4) * Q:(f // 4) * 512 + (f % 4 + 1) * Q],
                                        gg[:, f * P:(f + 1) * P], k["ident"][0:Q, 0:Q])
                last.then_inc(full["gT"], 1)

            def out_(t, j):
                ps = take_narrow("out", t, j)
                wait(pe, "ggT_done", CH * t + j + 1)
                if first_of(t, j):
                    pe.wait_ge(w_out_scaled, 1)
                for f in range(INTER // P):
                    last = pe.matmul(ps[0:Q, :], ggT[:, f, :], k["w_out"][:, f, :], start=(f == 0),
                                     stop=(f == INTER // P - 1))
                last.then_inc(full["out"], 1)

            def x2T_(t, j):
                wait(pe, "x2_done", CH * t + j + 1)
                ps = take_narrow("x2T", t, j)
                for c in range(KD):
                    last = pe.transpose(ps[:, c * Q:(c + 1) * Q], x2[:, j, c * P:(c + 1) * P], k["ident"][0:Q, 0:Q])
                last.then_inc(full["x2T"], 1)

            def logits_(t, j):
                wait(pe, "x2T_done", CH * t + j + 1)
                ps = take_narrow("logits", t, j)
                for c in range(KD):
                    last = pe.matmul(ps[0:Q, 0:NE], x2T[:, c, :], k["w_cls"][:, c, :], start=(c == 0),
                                     stop=(c == KD - 1))
                last.then_inc(full["logits"], 1)

            def rank_(t, j):
                wait(pe, "sel_done", CH * t + j + 1)
                ps = take_narrow("rank", t, j)
                pe.matmul(ps[0:Q, 0:E], k["before"][:, :], sel[:, :], start=True, stop=True)
                pe.matmul(ps[0:Q, E:2 * E], k["ones"][:, 0:Q], sel[:, :], start=True, stop=True
                          ).then_inc(full["rank"], 1)

            turns(pe, {"xnT": xnT_, "dt": dt_, "conv": conv_, "cum": cum_, "cb": cb_, "xrow": xrow_, "z": z_,
                       "inter": inter_, "state": state_, "decay": decay_, "heads": heads_, "gT": gT_, "out": out_,
                       "x2T": x2T_, "logits": logits_, "rank": rank_}, PLAN["pe"], stage)

        @block.scalar
        def _(act):
            def xnT_(t, j):
                wait_full(act, "xnT", t, j)
                act.wait_ge(full["z"], CH * t + 1)
                act.activation(xnT[:, :, chunk(j)], bank("xnT", j)[:, 0:KD * Q].rearrange("p (c q) -> p c q", c=KD),
                               ACT.Copy).then_inc(ev["xnT_done"], 1)

            def dt_exp_(t, _n):
                wait(act, "sp_m", t + 1)
                act.activation(sp[:, 2], sp[:, 1], ACT.Exp).then_inc(ev["exp_m"], 1)

            def dt_log_(t, _n):
                wait(act, "one_plus", t + 1)
                act.activation(sp[:, 4], sp[:, 3], ACT.Ln).then_inc(ev["logged"], 1)

            def conv_(t, n):
                if n < CONV_TILES:
                    m = conv_order()[n]
                    wait_full(act, "conv", t, n)
                    wait(act, "conv_done", CONV_TILES * t + n - 2)
                    act.activation(cacc[n % 3][:, :], bank("conv", n)[:, 0:SEQ], ACT.Identity,
                                   scale=k["conv_w"][:, m, 3:4], bias=k["conv_b"][:, m:m + 1]
                                   ).then_inc(ev["base"], 1)
                if n:
                    wait(act, "tapped", CONV_TILES * t + n)
                    act.activation(cth[(n - 1) % 2][:, :], cacc[(n - 1) % 3][:, :], ACT.Tanh
                                   ).then_inc(ev["tanhed"], 1)

            def cum_(t, j):
                o = 2 * Q
                ps = bank("cum", j)
                wait_full(act, "cum", t, j)
                wait(act, "yint_done", 2 * t)
                act.activation(grow[:, j, :], ps[0:Q, o:o + HEADS], ACT.Exp)
                wait(act, "dtxf_done", 2 * t)
                act.activation(fall[:, j, :], ps[0:Q, o + HEADS:o + 2 * HEADS], ACT.Exp)
                wait(act, "kept_done", t)
                act.activation(total[:, j, :], ps[:, o + 2 * HEADS:o + 3 * HEADS], ACT.Exp
                               ).then_inc(ev["cum_exp"], 1)

            def xrow_(t, j):
                wait_full(act, "xrow", t, j)
                wait(act, "skip_done", CH * t + j)
                act.activation(xrow[:, :], wide[0:Q, :], ACT.Copy).then_inc(ev["xrow_done"], 1)

            def z_(t, j):
                wait_full(act, "z", t, j)
                wait(act, "sq_done", CH * t + j)
                act.activation(zt[:, :], wide[0:Q, :], ACT.Tanh, scale=0.125).then_inc(ev["z_tanh"], 1)

            def heads_(t, q):
                act.wait_ge(dec_full[q % 2], CHAIN // 2 * t + q // 2 + 2)
                wait(act, "m_done", CHAIN * t + q - LX + 1)
                act.activation(lx[q % LX][:, :, :], dec[q % 2][0:Q, 0:HG * Q].rearrange("p (h t) -> p h t", h=HG),
                               ACT.Exp).then_inc(ev["lx_done"], 1)

            def squares_(t, j):
                wait(act, "y_done", CH * t + j + 1)
                act.activation(zt[:, :], y[:, :], ACT.Square, accum_out=ss[:, j:j + 1]).then_inc(ev["sq_done"], 1)

            def gT_(t, j):
                wait_full(act, "gT", t, j)
                wait(act, "h2_done", CH * t + j)
                act.activation(ggT[:, :, :].rearrange("p (u f) q -> p u (f q)", u=2),
                               wide[:, :].rearrange("p (u c) -> p u c", u=2)[:, :, 0:4 * Q], ACT.Copy
                               ).then_inc(ev["ggT_done"], 1)

            def stores_(t, j):
                wait(act, "x2_done", CH * t + j + 1)
                act.dma_start(dram["out"].rearrange("(c j p) d -> c j p d", j=CH, p=Q)[t, j],
                              h2[:, j, :]).then_inc(stored[j], 16)
                act.dma_start(dram["x2"][0:TOK, :].rearrange("(c j p) d -> c j p d", j=CH, p=Q)[t, j],
                              x2[:, j, :]).then_inc(stored[j], 16)

            def x2T_(t, j):
                wait_full(act, "x2T", t, j)
                act.activation(x2T[:, :, :].rearrange("p c q -> p (c q)"), bank("x2T", j)[:, 0:KD * Q], ACT.Copy
                               ).then_inc(ev["x2T_done"], 1)

            def logits_(t, j):
                wait_full(act, "logits", t, j)
                wait(act, "neg_max", CH * t + j + 1)
                act.activation(ex[:, :], bank("logits", j)[0:Q, 0:NE], ACT.Exp, bias=small[:, 0:1],
                               accum_out=small[:, 1:2]).then_inc(ev["exped"], 1)

            act.wait_ge(hin_in, 16)
            w_rows = ins["L0_attn_in_proj_w"].rearrange("(m p) d -> p m d", p=P)
            act.dma_start(k["w_in"][:, :, INTER:PROJ], w_rows[:, :, INTER:PROJ]).then_inc(w_in_loaded, 16)
            act.dma_start(k["w_in"][:, :, 0:INTER], w_rows[:, :, 0:INTER]).then_inc(z_loaded, 16)
            act.dma_start(k["w_out"][:, :, :],
                          ins["L0_attn_out_proj_w"].rearrange("(m p) d -> p m d", p=P)).then_inc(w_out_loaded, 16)
            with nc.allow_non_contiguous_dma(reason="a small per-channel vector"):
                act.dma_start(gain[:, :],
                              ins["L0_attn_norm_w"].rearrange("(m p) -> p m", p=P)).then_inc(w_out_loaded, 16)
            turns(act, {"xnT": xnT_, "dt_exp": dt_exp_, "dt_log": dt_log_, "conv": conv_, "cum": cum_, "xrow": xrow_,
                        "z": z_, "heads": heads_, "squares": squares_, "gT": gT_, "stores": stores_, "x2T": x2T_,
                        "logits": logits_}, PLAN["act"], {})

        @block.gpsimd
        def _(pool):
            def heads(ap):
                return ap.rearrange("p (h d) -> p h d", h=HEADS)

            def spread(ap, rows=Q):
                return ap.unsqueeze(2).broadcast_to([rows, HEADS, HD])

            def norm_rstd_(t, _n):
                wait(pool, "var1", t + 1)
                pool.tensor_tensor(rstd[:, :], var_e[:, :], k["half_power"][0:Q, 0:CH], ALU.pow
                                   ).then_inc(ev["rstd1"], 1)

            def dtx_(t, j):
                n = CH * t + j
                wait(pool, "xrow_done", n + 1)
                wait(pool, "a_done", t + 1)
                wait(pool, "y_done", n - 1)
                pool.tensor_tensor(heads(dtx[:, j, :]), heads(xrow[:, :]), spread(dt[:, j, :]), ALU.mult
                                   ).then_inc(ev["dtx_done"], 1)

            def dtxf_(t, j):
                wait(pool, "cum_exp", CH * t + j + 1)
                wait(pool, "dtx_done", CH * t + j + 1)
                wait(pool, "state_done", 2 * t + j)
                pool.tensor_tensor(heads(dtxf[:, :]), heads(dtx[:, j, :]), spread(fall[:, j, :]), ALU.mult
                                   ).then_inc(ev["dtxf_done"], 1)

            def skip_(t, j):
                wait(pool, "y_done", CH * t + j)
                pool.tensor_tensor(heads(skip[:, :]), heads(xrow[:, :]), spread(k["skip_d"][:, :]), ALU.mult
                                   ).then_inc(ev["skip_done"], 1)

            def skip_sum_(t, j):
                wait(pool, "skip_done", CH * t + j + 1)
                wait(pool, "yint_done", 2 * t + j)
                pool.tensor_tensor(skip[:, :], skip[:, :], yint[:, :], ALU.add).then_inc(ev["skip_sum"], 1)

            def kept_(t, _n):
                wait(pool, "state_done", 2 * t + 1)
                wait(pool, "cum_exp", CH * t + 2)
                pool.tensor_tensor(heads(kept[:, :]), heads(state[:, 0, :]), spread(total[:, 1, :], P), ALU.mult
                                   ).then_inc(ev["kept_done"], 1)

            def gate_(t, j):
                wait(pool, "y_done", CH * t + j + 1)
                wait(pool, "zs_done", CH * t + j + 1)
                pool.wait_ge(full["gT"], CH * t + j + 1)
                pool.tensor_tensor(gg[:, :], y[:, :], zs[:, :], ALU.mult).then_inc(ev["gg_done"], 1)

            def out_rstd_(t, j):
                wait(pool, "var_y", CH * t + j + 1)
                pool.tensor_tensor(small[:, 3:4], small[:, 2:3], k["half_power"][0:Q, 0:1], ALU.pow
                                   ).then_inc(ev["rstd_y"], 1)

            def x2_rstd_(t, j):
                wait(pool, "var2", CH * t + j + 1)
                pool.tensor_tensor(small[:, 5:6], small[:, 4:5], k["half_power"][0:Q, 0:1], ALU.pow
                                   ).then_inc(ev["rstd2"], 1)

            def scatter_(t, j):
                n = CH * t + j
                pool.wait_ge(scattered, 16 + 16 * TOPK * n)
                pool.sem_inc(entry_free, 1)
                wait(pool, "idled", n)
                wait(pool, "entry_done", n + 1)
                pool.tensor_tensor(idle[:, 2:3], k["half_power"][0:Q, 0:1], k["half_power"][0:Q, 0:1], ALU.mult
                                   ).then_inc(ev["idled"], 1)
                for c in range(TOPK):
                    pool.indirect_dma_start(
                        out=dram["slots"], out_offset=bass.IndirectOffsetOnAxis(ap=slot[:, j, c:c + 1], axis=0),
                        in_=entry[:, j, c, :], in_offset=None, bounds_check=SLOTS - 1, oob_is_err=False
                    ).then_inc(scattered, 16)

            turns(pool, {"norm_rstd": norm_rstd_, "dtx": dtx_, "dtxf": dtxf_, "skip": skip_, "skip_sum": skip_sum_,
                         "kept": kept_, "gate": gate_, "out_rstd": out_rstd_, "x2_rstd": x2_rstd_,
                         "scatter": scatter_}, PLAN["pool"], {})
            pool.wait_ge(scattered, 16 + 16 * TOPK * CH * BATCH)

        @block.vector
        def _(dve):
            step = Steps(dve, dve_step)
            step.n = 1

            def heads(ap):
                return ap.rearrange("p (h d) -> p h d", h=HEADS)

            def spread(ap):
                return ap.unsqueeze(2).broadcast_to([Q, HEADS, HD])

            def hold():
                dve.memset(idle[:, 0:1], 0.0)

            def done(ins_, name):
                ins_.then_inc(ev[name], 1)

            def norm_sums_(t, _n):
                dve.wait_ge(hin_in, 16 * t + 16)
                for j in range(CH):
                    step.done(dve.bn_stats(stats[:, j, :], hin[:, j, :]))

            def norm_var_(t, _n):
                step.wait()
                hold()
                for j in range(CH):
                    step.done(dve.bn_aggr(mv[:, j, :], stats[:, j, :]))
                step.wait()
                done(dve.tensor_scalar(var_e[:, :], mv[:, :, 1], EPS, None, ALU.add), "var1")

            def norm_(t, j):
                wait(dve, "rstd1", t + 1)
                done(dve.tensor_scalar(hin[:, j, :], hin[:, j, :], mv[:, j, 0:1], rstd[:, j:j + 1], ALU.subtract,
                                       ALU.mult), "xn_done")

            def conv_(t, n):
                if n < CONV_TILES:
                    m = conv_order()[n]
                    wait(dve, "base", CONV_TILES * t + n + 1)
                    for tap in (2, 1, 0):
                        late = 3 - tap
                        acc = cacc[n % 3][:, late:SEQ]
                        ins_ = dve.scalar_tensor_tensor(acc, bank("conv", n)[:, 0:SEQ - late],
                                                        k["conv_w"][:, m, tap:tap + 1], acc, ALU.mult, ALU.add)
                        if tap:
                            step.link(ins_)
                        else:
                            done(ins_, "tapped")
                if n:
                    m = conv_order()[n - 1]
                    wait(dve, "tanhed", CONV_TILES * t + n)
                    if m == C_TILE:
                        dve.wait_ge(full["inter"], 2 * t + 1)
                    else:
                        dve.wait_ge(full["cb" if m == B_TILE else "xrow"], CH * t + 1)
                    done(dve.scalar_tensor_tensor(xbcT[:, m, :], cth[(n - 1) % 2][:, :], 1.0, cacc[(n - 1) % 3][:, :],
                                                  ALU.add, ALU.mult), "conv_done")

            su, sm, se, sw, sl, st = (sp[:, n] for n in range(6))
            heads3 = [Q, CH, HEADS]

            def dt_sum_(t, _n):
                wait_full(dve, "dt", t, 0)
                done(dve.tensor_tensor(su, bank("dt", 0)[0:Q, 0:CH * HEADS].rearrange("p (j h) -> p j h", j=CH),
                                       k["dt_bias"][:, :].unsqueeze(1).broadcast_to(heads3), ALU.add), "dt_read")
                wait(dve, "dt_read", t + 1)
                step.link(dve.tensor_scalar(st, su, -1.0, None, ALU.mult))
                done(dve.tensor_tensor(sm, st, su, ALU.min), "sp_m")

            def dt_plus_(t, _n):
                wait(dve, "exp_m", t + 1)
                done(dve.tensor_scalar(sw, se, 1.0, None, ALU.add), "one_plus")

            def dt_rest_(t, _n):
                wait(dve, "logged", t + 1)
                step.done(dve.tensor_scalar(sw, sw, -1.0, TINY, ALU.add, ALU.add))
                step.link(dve.tensor_scalar(sl, sl, TINY, None, ALU.add))
                step.done(dve.reciprocal(sm, sw))
                step.link(dve.tensor_tensor(sl, sl, se, ALU.mult))
                step.done(dve.tensor_scalar(su, su, 0.0, None, ALU.max))
                step.link(dve.tensor_tensor(sl, sl, sm, ALU.mult))

            def dt_end_(t, _n):
                step.wait()
                wait(dve, "dtx_done", CH * t)
                step.link(dve.tensor_tensor(dt[:, :, :], su, sl, ALU.add))
                step.link(dve.tensor_tensor(st, dt[:, :, :], k["neg_a"][:, :].unsqueeze(1).broadcast_to(heads3),
                                            ALU.mult))
                step.done(dve.tensor_scalar(a[:, :, :], st, FLOOR, None, ALU.max))
                halves = st.rearrange("p j h -> p (j h)").rearrange("p (n h) -> p n h", h=HH)
                done(dve.tensor_scalar(a3[:, :, :, :], halves.unsqueeze(2).broadcast_to([Q, 2 * CH, 3, HH]), FLOOR,
                                       None, ALU.max), "a_done")

            def cum_(t, j):
                wait(dve, "cum_exp", CH * t + j + 1)
                wait(dve, "lx_done", CHAIN * t - CHAIN + GROUPS * (j + 1))
                sums = bank("cum", j)[0:3 * HH, 0:2 * Q]
                step.link(dve.tensor_copy(parts[:, j, :], sums))
                step.link(dve.tensor_tensor(rest[:, 0, :], sums, parts[:, j, :], ALU.subtract))
                step.link(dve.tensor_copy(mid[:, :], rest[:, 0, :]))
                step.link(dve.tensor_tensor(rest[:, 1, :], rest[:, 0, :], mid[:, :], ALU.subtract))
                step.done(dve.tensor_copy(parts[HH:2 * HH, j, :], mid[HH:2 * HH, :]))
                done(dve.tensor_copy(parts[2 * HH:3 * HH, j, :], rest[2 * HH:3 * HH, 1, :]), "parts_done")

            def cb_(t, j):
                wait_full(dve, "cb", t, j)
                ps = bank("cb", j)
                if j < CH - 1:
                    dve.wait_ge(full["state"], 2 * t + 1)
                    step.done(dve.tensor_copy(brow[:, j, :], ps[0:Q, P:P + NST]))
                done(dve.tensor_tensor(cbm[:, j, :], ps[0:Q, 0:Q], k["upto"][:, :], ALU.mult), "cbm_done")

            def z_(t, j):
                wait(dve, "z_tanh", CH * t + j + 1)
                wait(dve, "gg_done", CH * t + j)
                done(dve.scalar_tensor_tensor(zs[:, :], zt[:, :], 1.0, wide[0:Q, :], ALU.add, ALU.mult), "zs_done")

            def inter_(t, j):
                wait_full(dve, "inter", t, j)
                wait(dve, "skip_sum", 2 * t + j - 1)
                done(dve.tensor_tensor(heads(yint[:, :]), heads(wide[0:Q, :]), spread(grow[:, j, :]), ALU.mult),
                     "yint_done")

            def state_(t, j):
                wait_full(dve, "state", t, j)
                dve.wait_ge(full["inter"], 2 * t + 1)
                wait(dve, "kept_done", t + j)
                if j == 0:
                    ins_ = dve.tensor_copy(state[:, 0, :], wide[:, :])
                else:
                    ins_ = dve.tensor_tensor(state[:, 1, :], kept[:, :], wide[:, :], ALU.add)
                done(ins_, "state_done")

            def heads_(t, q):
                j = q // GROUPS
                if q % GROUPS == 0:
                    wait(dve, "cbm_done", CH * t + j + 1)
                wait(dve, "lx_done", CHAIN * t + q + 1)
                wait(dve, "y_heads", CHAIN * t + q - MX + 1)
                done(dve.scalar_tensor_tensor(m_[q % MX][:, :, :], lx[q % LX][:, :, :], 1.0,
                                              cbm[:, j, :].unsqueeze(1).broadcast_to([Q, HG, Q]),
                                              ALU.min, ALU.mult), "m_done")

            def y_(t, j):
                wait(dve, "y_heads", CHAIN * t + GROUPS * (j + 1))
                wait(dve, "skip_sum" if j else "skip_done", 2 * t + j if j else CH * t + 1)
                wait(dve, "gg_done", CH * t + j)
                done(dve.tensor_tensor(y[:, :], skip[:, :], ysum[0:Q, :], ALU.add), "y_done")

            def out_var_(t, j):
                if first_of(t, j):
                    dve.wait_ge(w_out_loaded, 32)
                    for m in range(INTER // P):
                        last = dve.tensor_scalar(k["w_out"][:, m, :], k["w_out"][:, m, :], gain[:, m:m + 1], None,
                                                 ALU.mult)
                    last.then_inc(w_out_scaled, 1)
                wait(dve, "sq_done", CH * t + j + 1)
                done(dve.tensor_scalar(small[:, 2:3], ss[:, j:j + 1], 1.0 / INTER, EPS, ALU.mult, ALU.add), "var_y")

            def out_(t, j):
                n = CH * t + j
                wait(dve, "rstd_y", n + 1)
                step.link(dve.tensor_scalar(small[:, 6:7], small[:, 3:4], 0.125, None, ALU.mult))
                if j == 0:
                    dve.wait_ge(hres_in, 16 * t + 16)
                dve.wait_ge(stored[j], 32 * t + 16)
                wait_full(dve, "out", t, j)
                done(dve.scalar_tensor_tensor(h2[:, j, :], bank("out", j)[0:Q, :], small[:, 6:7], hres[:, j, :],
                                              ALU.mult, ALU.add), "h2_done")
                wait(dve, "h2_done", n + 1)
                step.link(dve.bn_stats(stat2[:, :], h2[:, j, :]))
                hold()
                step.link(dve.bn_aggr(mv2[:, :], stat2[:, :]))
                done(dve.tensor_scalar(small[:, 4:5], mv2[:, 1:2], EPS, None, ALU.add), "var2")

            def x2_(t, j):
                wait(dve, "rstd2", CH * t + j + 1)
                done(dve.tensor_scalar(x2[:, j, :], h2[:, j, :], mv2[:, 0:1], small[:, 5:6], ALU.subtract, ALU.mult),
                     "x2_done")

            def largest_(t, j):
                wait_full(dve, "logits", t, j)
                step.link(dve.tensor_reduce(small[:, 7:8], bank("logits", j)[0:Q, 0:NE], AX, ALU.max))
                done(dve.tensor_scalar(small[:, 0:1], small[:, 7:8], -1.0, None, ALU.mult), "neg_max")

            def choices_(t, j):
                wait(dve, "exped", CH * t + j + 1)
                step.link(dve.reciprocal(small[:, 8:9], small[:, 1:2]))
                step.done(dve.tensor_scalar(score[:, :], ex[:, :], small[:, 8:9], None, ALU.mult))
                step.link(dve.scalar_tensor_tensor(biased[:, :], ex[:, :], small[:, 8:9], k["top_bias"][:, :],
                                                   ALU.mult, ALU.add))
                hold()
                step.link(dve.max(top[:, :], biased[:, :]))
                hold()
                step.link(dve.max_index(topi[:, :], top[:, :], biased[:, :]))
                step.link(dve.tensor_copy(r8[:, 0, :], topi[:, :]))
                step.link(dve.tensor_tensor(hot[:, :, :],
                                            k["numbers"][:, :].unsqueeze(1).broadcast_to([Q, TOPK, NE]),
                                            r8[:, 0, :].unsqueeze(2).broadcast_to([Q, TOPK, NE]), ALU.is_equal))
                done(dve.tensor_reduce(sel[:, :], hot[:, :, 0:E].rearrange("p c e -> p e c"), AX, ALU.add),
                     "sel_done")

            def weights_(t, j):
                step.link(dve.tensor_tensor(hots[:, :, :], hot[:, :, :],
                                            score[:, :].unsqueeze(1).broadcast_to([Q, TOPK, NE]), ALU.mult))
                step.link(dve.tensor_reduce(r8[:, 1, :], hots[:, :, :], AX, ALU.add))
                step.link(dve.tensor_reduce(small[:, 9:10], r8[:, 1, :], AX, ALU.add))
                step.link(dve.tensor_scalar(small[:, 9:10], small[:, 9:10], 1e-20, None, ALU.add))
                step.link(dve.reciprocal(small[:, 10:11], small[:, 9:10]))
                step.done(dve.tensor_scalar(r8[:, 2, :], r8[:, 1, :], small[:, 10:11], 1.5, ALU.mult, ALU.mult))
                step.link(dve.tensor_scalar(r8[:, 3, :], r8[:, 0, :], float(E), None, ALU.is_lt))
                step.link(dve.tensor_tensor(r8[:, 4, :], r8[:, 2, :], r8[:, 3, :], ALU.mult))
                step.link(dve.tensor_tensor(r8[:, 5, :], r8[:, 2, :], r8[:, 4, :], ALU.subtract))
                step.link(dve.tensor_reduce(small[:, 11:12], r8[:, 5, :], AX, ALU.add))
                step.link(dve.tensor_scalar(small[:, 11:12], small[:, 11:12], 1.0, None, ALU.add))
                step.done(dve.tensor_scalar(entry[:, j, :, 1], r8[:, 4, :], small[:, 11:12], None, ALU.mult))
                step.link(dve.tensor_copy(entry[:, j, :, 0], k["token"][:, 0:1].broadcast_to([Q, TOPK])))
                done(dve.tensor_scalar(k["token"][:, :], k["token"][:, :], float(Q), None, ALU.add), "entry_done")

            def rank_(t, j):
                wait_full(dve, "rank", t, j)
                wait(dve, "count_done", CH * t + j)
                ps = bank("rank", j)
                step.link(dve.tensor_tensor(place[:, :], ps[0:Q, 0:E], k["count"][:, :], ALU.add))
                done(dve.tensor_tensor(k["count"][:, :], ps[0:Q, E:2 * E], k["count"][:, :], ALU.add), "count_done")
                step.link(dve.tensor_tensor(hots[:, :, 0:E], hot[:, :, 0:E],
                                            place[:, :].unsqueeze(1).broadcast_to([Q, TOPK, E]), ALU.mult))
                step.link(dve.tensor_reduce(r8[:, 6, :], hots[:, :, 0:E], AX, ALU.add))
                step.done(dve.scalar_tensor_tensor(r8[:, 7, :], r8[:, 0, :], float(CAP), r8[:, 6, :], ALU.mult,
                                                   ALU.add))
                step.link(dve.tensor_scalar(r8[:, 5, :], r8[:, 6, :], float(CAP), float(4 * NE * CAP), ALU.is_ge,
                                            ALU.mult))
                dve.wait_ge(entry_free, CH * t + j + 1)
                step.done(dve.tensor_tensor(slot[:, j, :], r8[:, 7, :], r8[:, 5, :], ALU.add))

            turns(dve, {"norm_sums": norm_sums_, "norm_var": norm_var_, "norm": norm_, "conv": conv_,
                        "dt_sum": dt_sum_, "dt_plus": dt_plus_, "dt_rest": dt_rest_, "dt_end": dt_end_, "cum": cum_, "cb": cb_, "z": z_,
                        "inter": inter_, "state": state_, "heads": heads_, "y": y_, "out_var": out_var_,
                        "out": out_, "x2": x2_, "largest": largest_, "choices": choices_, "weights": weights_,
                        "rank": rank_}, PLAN["dve"], {}, lambda i: step.loop(i, DVE_STEPS), step.end)


def experts(nc, k, ins, dram):
    with ExitStack() as ctx:
        def sb(name, shape, dt=F32):
            return [ctx.enter_context(nc.sbuf_tensor(f"{name}{n}", shape, dt)) for n in range(2)]

        def pb(name):
            return [ctx.enter_context(nc.psum_tensor(f"{name}{n}", [P, 512], F32)) for n in range(2)]

        def sem(name):
            return ctx.enter_context(nc.semaphore(name))

        TILES, KF, ROWS = CAP // P, FI // P, CAP
        wgu, wd = sb("wgu", [P, KD, 2 * FI]), sb("wd", [P, KF, DM])
        table = ctx.enter_context(nc.sbuf_tensor("table", [P, E, TILES, 2], F32))
        gather_at, add_at = sb("gather_at", [P, TILES], U32), sb("add_at", [P, TILES], U32)
        weight = sb("weight", [P, TILES])
        rows, rowsT = sb("rows", [P, TILES, DM]), sb("rowsT", [P, KD, ROWS])
        th, gated, actT = sb("th", [P, KF, ROWS]), sb("gated", [P, KF, ROWS]), sb("actT", [P, KF, ROWS])
        ye = sb("ye", [P, TILES, DM])
        idle = ctx.enter_context(nc.sbuf_tensor("idle2", [P, 4], F32))
        turn_ps, gate_ps, up_ps, down_ps = pb("turn_ps"), pb("gate_ps"), pb("up_ps"), pb("down_ps")

        names = ["turned", "half_turned", "rowsT_done", "converted", "gu_done", "th_done", "gated_done", "act_done",
                 "down_done", "add_at_done", "y_out", "earlier_added"]
        ev = {n: sem("e_" + n) for n in names}
        table_in = sem("table_in")
        wgu_in = [sem(f"wgu_in{n}") for n in range(2)]
        wd_in = [sem(f"wd_in{n}") for n in range(2)]
        gathered = [sem(f"gathered{n}") for n in range(2)]
        added = sem("added")
        idled = sem("idled")

        with nc.Block() as first:
            @first.gpsimd
            def _(pool):
                for s in ev.values():
                    pool.sem_inc(s, 1)
                pool.memset(idle[:, :], 0.0).then_inc(idled, 1)

        block = ctx.enter_context(nc.Block())

        def wait(eng, name, n):
            if isinstance(n, int) and n < 1:
                return
            eng.wait_ge(ev[name], n + 1)

        def pairs(eng, turn, loop_start=None, loop_end=None):
            for u in range(2):
                turn(0, u)
            with eng.Fori(1, E // 2 - 1) as i:
                if loop_start:
                    loop_start(i - 1)
                for u in range(2):
                    turn(i, u)
                if loop_end:
                    loop_end(E // 2 - 2)
            for u in range(2):
                turn(E // 2 - 1, u)

        def there(i, n):
            return not isinstance(i, int) or 0 <= n < E

        @block.sync
        def _(sp):
            def load_gate_up(n, u):
                sp.dma_start(wgu[u][:, :, :], ins["L0_ffn_w_gate_up"][n].rearrange("(c p) f -> p c f", p=P)
                             ).then_inc(wgu_in[u], 16)

            def load_down(n, u):
                sp.dma_start(wd[u][:, :, :], ins["L0_ffn_w_down"][n].rearrange("(c p) f -> p c f", p=P)
                             ).then_inc(wd_in[u], 16)

            def turn(i, u):
                n = 2 * i + u
                if there(i, n + 2):
                    wait(sp, "gu_done", n + 1)
                    load_gate_up(n + 2, u)
                if there(i, n + 1):
                    wait(sp, "down_done", n)
                    load_down(n + 1, 1 - u)

            sp.dma_start(table[:, :, :, :], dram["slots"].rearrange("(e p t) c -> p e t c", p=P, t=TILES)
                         ).then_inc(table_in, 16)
            load_gate_up(0, 0)
            load_gate_up(1, 1)
            load_down(0, 0)
            pairs(sp, turn)

        @block.gpsimd
        def _(pool):
            step = Steps(pool, idled)

            def take_waits():
                step.wait()
                step.done(pool.tensor_tensor(idle[:, 0:1], idle[:, 1:2], idle[:, 1:2], ALU.mult))

            def gather(n, u):
                wait(pool, "converted", n + 1)
                wait(pool, "turned", n - 1)
                take_waits()
                for t in range(TILES):
                    pool.indirect_dma_start(
                        out=rows[u][:, t, :], out_offset=None, in_=dram["x2"],
                        in_offset=bass.IndirectOffsetOnAxis(ap=gather_at[u][:, t:t + 1], axis=0)
                    ).then_inc(gathered[u], 16)

            def add(n, u):
                wait(pool, "y_out", n + 1)
                if not isinstance(n, int) or n:
                    pool.wait_ge(added, 16 * TILES * n)
                take_waits()
                pool.sem_inc(ev["earlier_added"], 1)
                for t in range(TILES):
                    pool.indirect_dma_start(
                        out=dram["out"], out_offset=bass.IndirectOffsetOnAxis(ap=add_at[u][:, t:t + 1], axis=0),
                        in_=ye[u][:, t, :], in_offset=None, compute_op=ALU.add, bounds_check=TOK - 1,
                        oob_is_err=False
                    ).then_inc(added, 16)

            def turn(i, u):
                n = 2 * i + u
                if there(i, n + 2):
                    gather(n + 2, u)
                if there(i, n - 1):
                    add(n - 1, 1 - u)

            step.n = 1
            gather(0, 0)
            gather(1, 1)
            pairs(pool, turn, lambda i: step.loop(i, 2 * 2), step.end)
            add(E - 1, (E - 1) % 2)
            pool.wait_ge(added, 16 * TILES * E)

        @block.tensor
        def _(pe):
            def turn_rows(i, n, u):
                pe.wait_ge(gathered[u], 16 * TILES * i + 16 * TILES)
                for t in range(TILES):
                    wait(pe, "rowsT_done", TILES * n + t - 1)
                    for c in range(KD):
                        last = pe.transpose(turn_ps[t][:, c * P:(c + 1) * P], rows[u][:, t, c * P:(c + 1) * P],
                                            k["ident"][:, :])
                    last.then_inc(ev["turned" if t == TILES - 1 else "half_turned"], 1)

            def gate_up(i, n, u):
                pe.wait_ge(wgu_in[u], 16 * i + 16)
                wait(pe, "rowsT_done", TILES * n + TILES)
                wait(pe, "act_done", n - 1)
                for ps, col in ((gate_ps[u], 0), (up_ps[u], FI)):
                    for f in range(KF):
                        for c in range(KD):
                            last = pe.matmul(ps[:, f * ROWS:(f + 1) * ROWS],
                                             wgu[u][:, c, col + f * P:col + (f + 1) * P],
                                             rowsT[u][:, c, :], start=(c == 0), stop=(c == KD - 1))
                last.then_inc(ev["gu_done"], 1)

            def down(i, n, u):
                pe.wait_ge(wd_in[u], 16 * i + 16)
                wait(pe, "act_done", n + 1)
                wait(pe, "y_out", n)
                for t in range(TILES):
                    for f in range(KF):
                        last = pe.matmul(down_ps[t][:, :], actT[u][:, f, t * P:(t + 1) * P], wd[u][:, f, :],
                                         start=(f == 0), stop=(f == KF - 1))
                last.then_inc(ev["down_done"], 1)

            def turn(i, u):
                n = 2 * i + u
                gate_up(i, n, u)
                if there(i, n + 1):
                    turn_rows(i + u, n + 1, 1 - u)
                if there(i, n - 1):
                    down(i + u - 1, n - 1, 1 - u)

            turn_rows(0, 0, 0)
            pairs(pe, turn)
            down(E // 2 - 1, E - 1, (E - 1) % 2)

        @block.scalar
        def _(act):
            def copy_rows(n, u):
                for t in range(TILES):
                    wait(act, "turned" if t == TILES - 1 else "half_turned", n + 1)
                    wait(act, "gu_done", n - 1)
                    act.activation(rowsT[u][:, :, t * P:(t + 1) * P],
                                   turn_ps[t][:, :].rearrange("p (c q) -> p c q", c=KD),
                                   ACT.Copy).then_inc(ev["rowsT_done"], 1)

            def turn(i, u):
                n = 2 * i + u
                wait(act, "gu_done", n + 1)
                wait(act, "act_done", n - 1)
                act.activation(th[u][:, :, :].rearrange("p f q -> p (f q)"), gate_ps[u][:, :], ACT.Tanh, scale=0.5
                               ).then_inc(ev["th_done"], 1)
                if there(i, n + 1):
                    copy_rows(n + 1, 1 - u)

            copy_rows(0, 0)
            pairs(act, turn)

        @block.vector
        def _(dve):
            def convert(n, u):
                dve.tensor_copy(gather_at[u][:, :], table[:, n, :, 0] if isinstance(n, int)
                                else table[:, bass.ds(n, 1), :, 0].rearrange("p o t -> p (o t)")
                                ).then_inc(ev["converted"], 1)

            def results(n, u):
                wait(dve, "earlier_added", n)
                at = (table[:, n] if isinstance(n, int)
                      else table[:, bass.ds(n, 1), :, :].rearrange("p o t c -> p (o t) c"))
                dve.tensor_copy(add_at[u][:, :], at[:, :, 0]).then_inc(ev["add_at_done"], 1)
                dve.tensor_scalar(weight[u][:, :], at[:, :, 1], 0.5, None, ALU.mult).then_inc(ev["add_at_done"], 1)
                wait(dve, "add_at_done", 2 * n + 2)
                wait(dve, "down_done", n + 1)
                for t in range(TILES):
                    last = dve.tensor_scalar(ye[u][:, t, :], down_ps[t][:, :], weight[u][:, t:t + 1], None, ALU.mult)
                last.then_inc(ev["y_out"], 1)

            def turn(i, u):
                n = 2 * i + u
                if there(i, n + 2):
                    dve.wait_ge(gathered[u], 16 * TILES * i + 16 * TILES)
                    convert(n + 2, u)
                wait(dve, "th_done", n + 1)
                wait(dve, "down_done", n - 1)
                flat = [x[u][:, :, :].rearrange("p f q -> p (f q)") for x in (th, gated, actT)]
                dve.scalar_tensor_tensor(flat[1], flat[0], 1.0, gate_ps[u][:, :], ALU.add, ALU.mult
                                         ).then_inc(ev["gated_done"], 1)
                wait(dve, "gated_done", n + 1)
                dve.tensor_tensor(flat[2], flat[1], up_ps[u][:, :], ALU.mult).then_inc(ev["act_done"], 1)
                if there(i, n - 1):
                    results(n - 1, 1 - u)

            dve.wait_ge(table_in, 16)
            convert(0, 0)
            convert(1, 1)
            pairs(dve, turn)
            results(E - 1, (E - 1) % 2)


_INS = ["x", "txt", "L0_tok_log_dt", "L0_tok_B_ri", "L0_tok_inv_A_real", "L0_tok_A_imag", "L0_attn_in_proj_w",
        "L0_attn_conv_w", "L0_attn_conv_b", "L0_attn_A_log", "L0_attn_D", "L0_attn_dt_bias", "L0_attn_norm_w",
        "L0_attn_out_proj_w", "L0_ffn_w_cls", "L0_ffn_bias", "L0_ffn_w_gate_up", "L0_ffn_w_down"]


def build(nc, ins, out):
    with ExitStack() as ctx:
        def sb(name, shape, dt=F32):
            return ctx.enter_context(nc.sbuf_tensor(name, shape, dt))

        dram = {
            "h": nc.dram_tensor("h", (BATCH, SEQ, DM), F32).ap(),
            "x2": nc.dram_tensor("x2", (TOK + CAP, DM), F32).ap(),
            "out": out.rearrange("c s d -> (c s) d"),
            "slots": nc.dram_tensor("slots", (SLOTS, 2), F32).ap(),
        }
        k = {
            "ident": sb("ident", [P, P]),
            "upto": sb("upto", [Q, Q]),
            "after": sb("after", [Q, Q]),
            "before": sb("before", [Q, Q]),
            "ones": sb("ones", [Q, P]),
            "half_power": sb("half_power", [P, 4]),
            "far": sb("far", [Q, Q], BF16),
            "ident16": sb("ident16", [P, P], BF16),
            "pick": sb("pick", [3 * HH, HH], BF16),
            "unpick": sb("unpick", [3 * HH, HH], BF16),
            "token": sb("token", [Q, 1]),
            "numbers": sb("numbers", [Q, NE]),
            "count": sb("count", [Q, E]),
            "conv_w": sb("conv_w", [P, CONV_TILES, 4]),
            "conv_b": sb("conv_b", [P, CONV_TILES]),
            "neg_a": sb("neg_a", [Q, HEADS]),
            "skip_d": sb("skip_d", [Q, HEADS]),
            "dt_bias": sb("dt_bias", [Q, HEADS]),
            "top_bias": sb("top_bias", [Q, NE]),
            "w_cls": sb("w_cls", [P, KD, NE]),
        }
        with ExitStack() as c1:
            k["stored"] = c1.enter_context(nc.semaphore("stored"))
            k["zero"] = c1.enter_context(nc.sbuf_tensor("zero", [P, 2 * DM], F32))
            k["empty"] = c1.enter_context(nc.sbuf_tensor("empty", [P, 2, 2], F32))
            make_constants(nc, k, ins, dram)
            s4d_rows(nc, k, ins, dram)
        with ExitStack() as c2:
            k["w_in"] = c2.enter_context(nc.sbuf_tensor("w_in", [P, KD, PROJ], F32))
            k["w_out"] = c2.enter_context(nc.sbuf_tensor("w_out", [P, INTER // P, DM], F32))
            sequences(nc, k, ins, dram)
        experts(nc, k, ins, dram)


def kernel(**inputs):
    import numpy as _np
    import concourse.bacc as _bacc
    from concourse import mybir as _mybir
    from concourse.bass_utils import run_bass_kernel_spmd as _run

    nc = _bacc.Bacc("TRN2", target_bir_lowering=False, num_devices=1)
    arrays, args = {}, {}
    for name in _INS:
        a = _np.ascontiguousarray(inputs[name])
        arrays[f"in_{name}_dram"] = a
        args[name] = nc.dram_tensor(f"in_{name}_dram", a.shape, _mybir.dt.from_np(a.dtype), kind="ExternalInput").ap()
    out = nc.dram_tensor("out_0_dram", (BATCH, SEQ, DM), F32, kind="ExternalOutput").ap()
    build(nc, args, out)
    r = _run(nc, [arrays], core_ids=[0])
    return r.results[0]["out_0_dram"]
```
